# Optimizing a Trainium2 kernel written in Bass

```python
import numpy as np
import jax
import jax.numpy as jnp

def _softmax(x, axis=-1):
    return jax.nn.softmax(x, axis=axis)

def _gelu(x):
    return jax.nn.gelu(x, approximate=True)

def _silu(x):
    return jax.nn.silu(x)

def _sigmoid(x):
    return jax.nn.sigmoid(x)

def _layernorm(x, axis=-1, eps=1e-05):
    m = jnp.mean(x, axis=axis, keepdims=True)
    v = jnp.var(x, axis=axis, keepdims=True)
    return (x - m) / jnp.sqrt(v + eps)

def _scatter_add(tgt, idx, src, axis=0):
    return tgt.at[idx].add(src)

def _segment_sum(src, seg, n):
    return jax.ops.segment_sum(src, seg, n)
kernel_name = 'mk_adaln_d2_jaxref_r8_8c1278'

def setup_inputs(seed: int=0):
    np.random.seed(seed)
    _w = jnp.asarray

    def _L0_attn_setup():
        import jax, jax.numpy as jnp
        import numpy as np
        B, L = (2, 128)
        D_MODEL, D_CKV, D_CQ = (128, 32, 64)
        N_HEAD, D_HEAD, D_ROPE = (8, 64, 32)
        N_IDX_HEAD = 4
        K_TS, LW = (96, 64)
        ROPE_BASE = 10000.0

        def _pope(x, angles):
            cos, sin = (jnp.cos(angles), jnp.sin(angles))
            mu1, mu2 = jnp.split(jax.nn.softplus(x), 2, axis=-1)
            return jnp.concatenate([mu1 * cos - mu2 * sin, mu1 * sin + mu2 * cos], axis=-1)

        def _forward(x, W_dkv, W_uk, W_uv, W_dq, W_uq, W_qr, W_kr, W_out, idx_wq, idx_wk, idx_w, raw_delta):
            B_, L_, _ = x.shape
            c_kv = x @ W_dkv
            q_i = (x @ idx_wq).reshape(B_, L_, N_IDX_HEAD, D_HEAD)
            k_i = x @ idx_wk
            s_i = jax.nn.relu(jnp.einsum('bthd,bsd->bths', q_i, k_i))
            I = jnp.einsum('bths,h->bts', s_i, idx_w)
            qpos = jnp.arange(L_)[:, None]
            kpos = jnp.arange(L_)[None, :]
            local = (kpos >= qpos - LW + 1) & (kpos <= qpos)
            causal = kpos > qpos
            I = jnp.where(local[None], jnp.inf, I)
            I = jnp.where(causal[None], -jnp.inf, I)
            kk = min(K_TS, L_)
            _, idx = jax.lax.top_k(I, kk)
            bi = jnp.arange(B_)[:, None, None]
            key_c = (c_kv @ W_uk)[bi, idx].reshape(B_, L_, kk, N_HEAD, D_HEAD)
            value = (c_kv @ W_uv)[bi, idx].reshape(B_, L_, kk, N_HEAD, D_HEAD)
            c_q = x @ W_dq
            query_c = (c_q @ W_uq).reshape(B_, L_, N_HEAD, D_HEAD)
            half = D_ROPE // 2
            theta = 1.0 / ROPE_BASE ** (2.0 * jnp.arange(half, dtype=jnp.float32) / D_ROPE)
            delta = -2.0 * jnp.pi * jax.nn.sigmoid(raw_delta)
            angles_q = jnp.arange(L_, dtype=jnp.float32)[:, None] * theta[None, :] + delta
            query_r = _pope((c_q @ W_qr).reshape(B_, L_, N_HEAD, D_ROPE), angles_q[None, :, None, :])
            kr_sel = (x @ W_kr)[bi, idx]
            angles_k = jnp.arange(kk, dtype=jnp.float32)[:, None] * theta[None, :] + delta
            key_r = _pope(kr_sel, angles_k[None, None, :, :])
            scale = (D_HEAD + D_ROPE) ** (-0.5)
            q_c = query_c.transpose(0, 2, 1, 3)
            q_r = query_r.transpose(0, 2, 1, 3)
            k_c = key_c.transpose(0, 3, 1, 2, 4)
            v = value.transpose(0, 3, 1, 2, 4)
            scores = (jnp.einsum('bhld,bhlkd->bhlk', q_c, k_c) + jnp.einsum('bhld,blkd->bhlk', q_r, key_r)) * scale
            attn = jax.nn.softmax(scores.astype(jnp.float32), axis=-1).astype(v.dtype)
            out = jnp.einsum('bhlk,bhlkd->bhld', attn, v)
            out = out.transpose(0, 2, 1, 3).reshape(B_, L_, N_HEAD * D_HEAD)
            return out @ W_out
        key = jax.random.key(seed)
        ks = jax.random.split(key, 14)

        def w(k, shape, fan_in):
            return jax.random.normal(k, shape, dtype=jnp.float32) * fan_in ** (-0.5)
        return {'x': jax.random.normal(ks[0], (B, L, D_MODEL), dtype=jnp.float32), 'W_dkv': w(ks[1], (D_MODEL, D_CKV), D_MODEL), 'W_uk': w(ks[2], (D_CKV, N_HEAD * D_HEAD), D_CKV), 'W_uv': w(ks[3], (D_CKV, N_HEAD * D_HEAD), D_CKV), 'W_dq': w(ks[4], (D_MODEL, D_CQ), D_MODEL), 'W_uq': w(ks[5], (D_CQ, N_HEAD * D_HEAD), D_CQ), 'W_qr': w(ks[6], (D_CQ, N_HEAD * D_ROPE), D_CQ), 'W_kr': w(ks[7], (D_MODEL, D_ROPE), D_MODEL), 'W_out': w(ks[8], (N_HEAD * D_HEAD, D_MODEL), N_HEAD * D_HEAD), 'idx_wq': w(ks[9], (D_MODEL, N_IDX_HEAD * D_HEAD), D_MODEL), 'idx_wk': w(ks[10], (D_MODEL, D_HEAD), D_MODEL), 'idx_w': jnp.ones((N_IDX_HEAD,), dtype=jnp.float32), 'raw_delta': jax.random.normal(ks[11], (D_ROPE // 2,), dtype=jnp.float32) * 0.1}
    _L0_attn_in = _L0_attn_setup()

    def _L0_ffn_setup():
        import jax, jax.numpy as jnp
        import numpy as np
        DIM = 128
        DEPTH = 2
        HEADS = 8
        DIM_HEAD = 64
        WINDOW = 64
        INNER = HEADS * DIM_HEAD
        HID = int(DIM * 4 * 2 / 3)
        B, N = (2, 1024)
        QK_SCALE = 8.0

        def shift_token(t):
            t1, t2 = jnp.split(t, 2, axis=-1)
            t2 = jnp.pad(t2, ((0, 0), (1, 0), (0, 0)))[:, :-1]
            return jnp.concatenate([t1, t2], axis=-1)

        def l2norm(t):
            return t / jnp.clip(jnp.linalg.norm(t, axis=-1, keepdims=True), 1e-12)

        def rotate_half(x):
            x1, x2 = jnp.split(x, 2, axis=-1)
            return jnp.concatenate([-x2, x1], axis=-1)

        def rotary_xpos(q, k):
            n = q.shape[-2]
            half_idx = jnp.arange(0, DIM_HEAD, 2, dtype=jnp.float32)
            inv_freq = 1.0 / 10000.0 ** (half_idx / DIM_HEAD)
            t = jnp.arange(n, dtype=jnp.float32)
            freqs = t[:, None] * inv_freq[None, :]
            freqs = jnp.concatenate([freqs, freqs], axis=-1)
            base = (half_idx + 0.4 * DIM_HEAD) / (1.4 * DIM_HEAD)
            power = (t - n // 2) / float(WINDOW // 2)
            scale = base[None, :] ** power[:, None]
            scale = jnp.concatenate([scale, scale], axis=-1)
            cos, sin = (jnp.cos(freqs), jnp.sin(freqs))
            q = q * cos * scale + rotate_half(q) * sin * scale
            k = k * cos / scale + rotate_half(k) * sin / scale
            return (q, k)

        def local_attention(q, k, v):
            b, h, n, d = q.shape
            w = n // WINDOW
            bq = q.reshape(b, h, w, WINDOW, d) * QK_SCALE
            bk = k.reshape(b, h, w, WINDOW, d)
            bv = v.reshape(b, h, w, WINDOW, d)

            def look_around(t):
                p = jnp.pad(t, ((0, 0), (0, 0), (1, 0), (0, 0), (0, 0)))
                return jnp.concatenate([p[:, :, :w], p[:, :, 1:]], axis=3)
            bk, bv = (look_around(bk), look_around(bv))
            bt = jnp.arange(n).reshape(w, WINDOW)
            btp = jnp.pad(bt, ((1, 0), (0, 0)), constant_values=-1)
            btk = jnp.concatenate([btp[:w], btp[1:]], axis=1)
            sim = jnp.einsum('bhwid,bhwjd->bhwij', bq, bk)
            i = bt[:, :, None]
            j = btk[:, None, :]
            mask = (i < j) | (i > j + WINDOW) | (j == -1)
            sim = jnp.where(mask, -jnp.finfo(sim.dtype).max, sim)
            attn = jax.nn.softmax(sim, axis=-1)
            out = jnp.einsum('bhwij,bhwjd->bhwid', attn, bv)
            return out.reshape(b, h, n, d)

        def _layer(x, wqkv, qs, ksc, wo, lg, lb, w1, b1, w2, b2):
            b, n, _ = x.shape
            h = shift_token(x)
            qkv = h @ wqkv
            q, k, v = jnp.split(qkv, 3, axis=-1)
            to_heads = lambda t: t.reshape(b, n, HEADS, DIM_HEAD).transpose(0, 2, 1, 3)
            q, k, v = (to_heads(q), to_heads(k), to_heads(v))
            q = l2norm(q) * qs
            k = l2norm(k) * ksc
            q, k = rotary_xpos(q, k)
            o = local_attention(q, k, v)
            o = o.transpose(0, 2, 1, 3).reshape(b, n, INNER)
            x = x + o @ wo
            h = shift_token(x)
            mu = h.mean(-1, keepdims=True)
            var = h.var(-1, keepdims=True)
            h = (h - mu) / jnp.sqrt(var + 1e-05) * lg + lb
            h = h @ w1 + b1
            a, g = jnp.split(h, 2, axis=-1)
            h = a * jax.nn.gelu(g, approximate=False)
            x = x + h @ w2 + b2
            return x
        key = jax.random.key(seed)
        ks = jax.random.split(key, 6)
        return {'x': jax.random.normal(ks[0], (B, N, DIM), jnp.float32), 'wqkv': jax.random.normal(ks[1], (DEPTH, DIM, 3 * INNER), jnp.float32) * 0.02, 'q_scale': jnp.ones((DEPTH, DIM_HEAD), jnp.float32), 'k_scale': jnp.ones((DEPTH, DIM_HEAD), jnp.float32), 'wo': jax.random.normal(ks[2], (DEPTH, INNER, DIM), jnp.float32) * 0.02, 'ln_g': jnp.ones((DEPTH, DIM), jnp.float32), 'ln_b': jnp.zeros((DEPTH, DIM), jnp.float32), 'w1': jax.random.normal(ks[3], (DEPTH, DIM, 2 * HID), jnp.float32) * 0.02, 'b1': jnp.zeros((DEPTH, 2 * HID), jnp.float32), 'w2': jax.random.normal(ks[4], (DEPTH, HID, DIM), jnp.float32) * 0.02, 'b2': jnp.zeros((DEPTH, DIM), jnp.float32)}
    _L0_ffn_in = _L0_ffn_setup()
    _L0_c = _w((lambda *s: np.random.randn(*s).astype(np.float32) * 0.05)(8, 128))
    _L0_wmod = _w((lambda *s: np.random.randn(*s).astype(np.float32) * 0.05)(128, 6 * 128) * 128 ** (-0.5))

    def _L1_attn_setup():
        import jax, jax.numpy as jnp
        import numpy as np
        import math
        FEATURE_DIM = 128
        NUM_HEADS = 16
        HEAD_SIZE = FEATURE_DIM // NUM_HEADS
        key = jax.random.key(seed)
        ks = jax.random.split(key, 5)
        B, T, C = (4, 256, FEATURE_DIM)
        scale = 1.0 / math.sqrt(C)
        x = jax.random.normal(ks[0], (B, T, C), dtype=jnp.float32)
        W_qkv = jax.random.uniform(ks[1], (3 * C, C), jnp.float32, -scale, scale)
        b_qkv = jax.random.uniform(ks[2], (3 * C,), jnp.float32, -scale, scale)
        W_out = jax.random.uniform(ks[3], (C, C), jnp.float32, -scale, scale)
        b_out = jax.random.uniform(ks[4], (C,), jnp.float32, -scale, scale)
        return {'x': x, 'W_qkv': W_qkv, 'b_qkv': b_qkv, 'W_out': W_out, 'b_out': b_out}
    _L1_attn_in = _L1_attn_setup()

    def _L1_ffn_setup():
        import jax, jax.numpy as jnp
        import numpy as np
        B, S, D = (2, 64, 128)
        E, K, I = (16, 8, 128)
        I_SH = 128
        ROUTE_SCALE = 2.826
        key = jax.random.key(seed)
        ks = jax.random.split(key, 8)
        s = 0.02
        return {'x': jax.random.normal(ks[0], (B, S, D), dtype=jnp.float32), 'gate_w': jax.random.normal(ks[1], (E, D), dtype=jnp.float32) * s, 'expert_bias': jnp.zeros((E,), dtype=jnp.float32), 'w_gate': jax.random.normal(ks[2], (E, I, D), dtype=jnp.float32) * s, 'w_up': jax.random.normal(ks[3], (E, I, D), dtype=jnp.float32) * s, 'w_down': jax.random.normal(ks[4], (E, D, I), dtype=jnp.float32) * s, 'shared_gate_w': jax.random.normal(ks[5], (I_SH, D), dtype=jnp.float32) * s, 'shared_up_w': jax.random.normal(ks[6], (I_SH, D), dtype=jnp.float32) * s, 'shared_down_w': jax.random.normal(ks[7], (D, I_SH), dtype=jnp.float32) * s}
    _L1_ffn_in = _L1_ffn_setup()
    _L1_c = _w((lambda *s: np.random.randn(*s).astype(np.float32) * 0.05)(8, 128))
    _L1_wmod = _w((lambda *s: np.random.randn(*s).astype(np.float32) * 0.05)(128, 6 * 128) * 128 ** (-0.5))
    _d = {'L0_attn_x': _L0_attn_in['x'], 'L0_attn_W_dkv': _L0_attn_in['W_dkv'], 'L0_attn_W_uk': _L0_attn_in['W_uk'], 'L0_attn_W_uv': _L0_attn_in['W_uv'], 'L0_attn_W_dq': _L0_attn_in['W_dq'], 'L0_attn_W_uq': _L0_attn_in['W_uq'], 'L0_attn_W_qr': _L0_attn_in['W_qr'], 'L0_attn_W_kr': _L0_attn_in['W_kr'], 'L0_attn_W_out': _L0_attn_in['W_out'], 'L0_attn_idx_wq': _L0_attn_in['idx_wq'], 'L0_attn_idx_wk': _L0_attn_in['idx_wk'], 'L0_attn_idx_w': _L0_attn_in['idx_w'], 'L0_attn_raw_delta': _L0_attn_in['raw_delta'], 'L0_ffn_wqkv': _L0_ffn_in['wqkv'], 'L0_ffn_q_scale': _L0_ffn_in['q_scale'], 'L0_ffn_k_scale': _L0_ffn_in['k_scale'], 'L0_ffn_wo': _L0_ffn_in['wo'], 'L0_ffn_ln_g': _L0_ffn_in['ln_g'], 'L0_ffn_ln_b': _L0_ffn_in['ln_b'], 'L0_ffn_w1': _L0_ffn_in['w1'], 'L0_ffn_b1': _L0_ffn_in['b1'], 'L0_ffn_w2': _L0_ffn_in['w2'], 'L0_ffn_b2': _L0_ffn_in['b2'], 'L0_c': _L0_c, 'L0_wmod': _L0_wmod, 'L1_attn_W_qkv': _L1_attn_in['W_qkv'], 'L1_attn_b_qkv': _L1_attn_in['b_qkv'], 'L1_attn_W_out': _L1_attn_in['W_out'], 'L1_attn_b_out': _L1_attn_in['b_out'], 'L1_ffn_gate_w': _L1_ffn_in['gate_w'], 'L1_ffn_expert_bias': _L1_ffn_in['expert_bias'], 'L1_ffn_w_gate': _L1_ffn_in['w_gate'], 'L1_ffn_w_up': _L1_ffn_in['w_up'], 'L1_ffn_w_down': _L1_ffn_in['w_down'], 'L1_ffn_shared_gate_w': _L1_ffn_in['shared_gate_w'], 'L1_ffn_shared_up_w': _L1_ffn_in['shared_up_w'], 'L1_ffn_shared_down_w': _L1_ffn_in['shared_down_w'], 'L1_c': _L1_c, 'L1_wmod': _L1_wmod}
    _x0 = _d['L0_attn_x']
    _d['L0_attn_x'] = jax.random.normal(jax.random.fold_in(jax.random.key(seed), 1), (8, 256, 128), dtype=_x0.dtype)
    del _x0
    return _d

def reference(L0_attn_x, L0_attn_W_dkv, L0_attn_W_uk, L0_attn_W_uv, L0_attn_W_dq, L0_attn_W_uq, L0_attn_W_qr, L0_attn_W_kr, L0_attn_W_out, L0_attn_idx_wq, L0_attn_idx_wk, L0_attn_idx_w, L0_attn_raw_delta, L0_ffn_wqkv, L0_ffn_q_scale, L0_ffn_k_scale, L0_ffn_wo, L0_ffn_ln_g, L0_ffn_ln_b, L0_ffn_w1, L0_ffn_b1, L0_ffn_w2, L0_ffn_b2, L0_c, L0_wmod, L1_attn_W_qkv, L1_attn_b_qkv, L1_attn_W_out, L1_attn_b_out, L1_ffn_gate_w, L1_ffn_expert_bias, L1_ffn_w_gate, L1_ffn_w_up, L1_ffn_w_down, L1_ffn_shared_gate_w, L1_ffn_shared_up_w, L1_ffn_shared_down_w, L1_c, L1_wmod):

    def _L0_attn_ref(x, W_dkv, W_uk, W_uv, W_dq, W_uq, W_qr, W_kr, W_out, idx_wq, idx_wk, idx_w, raw_delta):
        import jax, jax.numpy as jnp
        import numpy as np
        B, L = (2, 128)
        D_MODEL, D_CKV, D_CQ = (128, 32, 64)
        N_HEAD, D_HEAD, D_ROPE = (8, 64, 32)
        N_IDX_HEAD = 4
        K_TS, LW = (96, 64)
        ROPE_BASE = 10000.0

        def _pope(x, angles):
            cos, sin = (jnp.cos(angles), jnp.sin(angles))
            mu1, mu2 = jnp.split(jax.nn.softplus(x), 2, axis=-1)
            return jnp.concatenate([mu1 * cos - mu2 * sin, mu1 * sin + mu2 * cos], axis=-1)

        def _forward(x, W_dkv, W_uk, W_uv, W_dq, W_uq, W_qr, W_kr, W_out, idx_wq, idx_wk, idx_w, raw_delta):
            B_, L_, _ = x.shape
            c_kv = x @ W_dkv
            q_i = (x @ idx_wq).reshape(B_, L_, N_IDX_HEAD, D_HEAD)
            k_i = x @ idx_wk
            s_i = jax.nn.relu(jnp.einsum('bthd,bsd->bths', q_i, k_i))
            I = jnp.einsum('bths,h->bts', s_i, idx_w)
            qpos = jnp.arange(L_)[:, None]
            kpos = jnp.arange(L_)[None, :]
            local = (kpos >= qpos - LW + 1) & (kpos <= qpos)
            causal = kpos > qpos
            I = jnp.where(local[None], jnp.inf, I)
            I = jnp.where(causal[None], -jnp.inf, I)
            kk = min(K_TS, L_)
            _, idx = jax.lax.top_k(I, kk)
            bi = jnp.arange(B_)[:, None, None]
            key_c = (c_kv @ W_uk)[bi, idx].reshape(B_, L_, kk, N_HEAD, D_HEAD)
            value = (c_kv @ W_uv)[bi, idx].reshape(B_, L_, kk, N_HEAD, D_HEAD)
            c_q = x @ W_dq
            query_c = (c_q @ W_uq).reshape(B_, L_, N_HEAD, D_HEAD)
            half = D_ROPE // 2
            theta = 1.0 / ROPE_BASE ** (2.0 * jnp.arange(half, dtype=jnp.float32) / D_ROPE)
            delta = -2.0 * jnp.pi * jax.nn.sigmoid(raw_delta)
            angles_q = jnp.arange(L_, dtype=jnp.float32)[:, None] * theta[None, :] + delta
            query_r = _pope((c_q @ W_qr).reshape(B_, L_, N_HEAD, D_ROPE), angles_q[None, :, None, :])
            kr_sel = (x @ W_kr)[bi, idx]
            angles_k = jnp.arange(kk, dtype=jnp.float32)[:, None] * theta[None, :] + delta
            key_r = _pope(kr_sel, angles_k[None, None, :, :])
            scale = (D_HEAD + D_ROPE) ** (-0.5)
            q_c = query_c.transpose(0, 2, 1, 3)
            q_r = query_r.transpose(0, 2, 1, 3)
            k_c = key_c.transpose(0, 3, 1, 2, 4)
            v = value.transpose(0, 3, 1, 2, 4)
            scores = (jnp.einsum('bhld,bhlkd->bhlk', q_c, k_c) + jnp.einsum('bhld,blkd->bhlk', q_r, key_r)) * scale
            attn = jax.nn.softmax(scores.astype(jnp.float32), axis=-1).astype(v.dtype)
            out = jnp.einsum('bhlk,bhlkd->bhld', attn, v)
            out = out.transpose(0, 2, 1, 3).reshape(B_, L_, N_HEAD * D_HEAD)
            return out @ W_out
        return _forward(x, W_dkv, W_uk, W_uv, W_dq, W_uq, W_qr, W_kr, W_out, idx_wq, idx_wk, idx_w, raw_delta)

    def _L0_ffn_ref(x, wqkv, q_scale, k_scale, wo, ln_g, ln_b, w1, b1, w2, b2):
        import jax, jax.numpy as jnp
        import numpy as np
        DIM = 128
        DEPTH = 2
        HEADS = 8
        DIM_HEAD = 64
        WINDOW = 64
        INNER = HEADS * DIM_HEAD
        HID = int(DIM * 4 * 2 / 3)
        B, N = (2, 1024)
        QK_SCALE = 8.0

        def shift_token(t):
            t1, t2 = jnp.split(t, 2, axis=-1)
            t2 = jnp.pad(t2, ((0, 0), (1, 0), (0, 0)))[:, :-1]
            return jnp.concatenate([t1, t2], axis=-1)

        def l2norm(t):
            return t / jnp.clip(jnp.linalg.norm(t, axis=-1, keepdims=True), 1e-12)

        def rotate_half(x):
            x1, x2 = jnp.split(x, 2, axis=-1)
            return jnp.concatenate([-x2, x1], axis=-1)

        def rotary_xpos(q, k):
            n = q.shape[-2]
            half_idx = jnp.arange(0, DIM_HEAD, 2, dtype=jnp.float32)
            inv_freq = 1.0 / 10000.0 ** (half_idx / DIM_HEAD)
            t = jnp.arange(n, dtype=jnp.float32)
            freqs = t[:, None] * inv_freq[None, :]
            freqs = jnp.concatenate([freqs, freqs], axis=-1)
            base = (half_idx + 0.4 * DIM_HEAD) / (1.4 * DIM_HEAD)
            power = (t - n // 2) / float(WINDOW // 2)
            scale = base[None, :] ** power[:, None]
            scale = jnp.concatenate([scale, scale], axis=-1)
            cos, sin = (jnp.cos(freqs), jnp.sin(freqs))
            q = q * cos * scale + rotate_half(q) * sin * scale
            k = k * cos / scale + rotate_half(k) * sin / scale
            return (q, k)

        def local_attention(q, k, v):
            b, h, n, d = q.shape
            w = n // WINDOW
            bq = q.reshape(b, h, w, WINDOW, d) * QK_SCALE
            bk = k.reshape(b, h, w, WINDOW, d)
            bv = v.reshape(b, h, w, WINDOW, d)

            def look_around(t):
                p = jnp.pad(t, ((0, 0), (0, 0), (1, 0), (0, 0), (0, 0)))
                return jnp.concatenate([p[:, :, :w], p[:, :, 1:]], axis=3)
            bk, bv = (look_around(bk), look_around(bv))
            bt = jnp.arange(n).reshape(w, WINDOW)
            btp = jnp.pad(bt, ((1, 0), (0, 0)), constant_values=-1)
            btk = jnp.concatenate([btp[:w], btp[1:]], axis=1)
            sim = jnp.einsum('bhwid,bhwjd->bhwij', bq, bk)
            i = bt[:, :, None]
            j = btk[:, None, :]
            mask = (i < j) | (i > j + WINDOW) | (j == -1)
            sim = jnp.where(mask, -jnp.finfo(sim.dtype).max, sim)
            attn = jax.nn.softmax(sim, axis=-1)
            out = jnp.einsum('bhwij,bhwjd->bhwid', attn, bv)
            return out.reshape(b, h, n, d)

        def _layer(x, wqkv, qs, ksc, wo, lg, lb, w1, b1, w2, b2):
            b, n, _ = x.shape
            h = shift_token(x)
            qkv = h @ wqkv
            q, k, v = jnp.split(qkv, 3, axis=-1)
            to_heads = lambda t: t.reshape(b, n, HEADS, DIM_HEAD).transpose(0, 2, 1, 3)
            q, k, v = (to_heads(q), to_heads(k), to_heads(v))
            q = l2norm(q) * qs
            k = l2norm(k) * ksc
            q, k = rotary_xpos(q, k)
            o = local_attention(q, k, v)
            o = o.transpose(0, 2, 1, 3).reshape(b, n, INNER)
            x = x + o @ wo
            h = shift_token(x)
            mu = h.mean(-1, keepdims=True)
            var = h.var(-1, keepdims=True)
            h = (h - mu) / jnp.sqrt(var + 1e-05) * lg + lb
            h = h @ w1 + b1
            a, g = jnp.split(h, 2, axis=-1)
            h = a * jax.nn.gelu(g, approximate=False)
            x = x + h @ w2 + b2
            return x
        for l in range(DEPTH):
            x = _layer(x, wqkv[l], q_scale[l], k_scale[l], wo[l], ln_g[l], ln_b[l], w1[l], b1[l], w2[l], b2[l])
        return x

    def _L1_attn_ref(x, W_qkv, b_qkv, W_out, b_out):
        import jax, jax.numpy as jnp
        import numpy as np
        import math
        FEATURE_DIM = 128
        NUM_HEADS = 16
        HEAD_SIZE = FEATURE_DIM // NUM_HEADS
        B, T, C = x.shape
        H, hs = (NUM_HEADS, HEAD_SIZE)
        qkv = x @ W_qkv.T + b_qkv
        qkv = qkv.reshape(B, T, H, 3 * hs)
        q = qkv[..., :hs]
        k = qkv[..., hs:2 * hs]
        v = qkv[..., 2 * hs:]
        att = jnp.einsum('bthd,bshd->bhts', q, k) / math.sqrt(hs)
        att_prob = jax.nn.softmax(att, axis=-1)
        att_v = jnp.einsum('bhts,bshd->bthd', att_prob, v)
        att_v = att_v.reshape(B, T, C)
        return att_v @ W_out.T + b_out

    def _L1_ffn_ref(x, gate_w, expert_bias, w_gate, w_up, w_down, shared_gate_w, shared_up_w, shared_down_w):
        import jax, jax.numpy as jnp
        import numpy as np
        B, S, D = (2, 64, 128)
        E, K, I = (16, 8, 128)
        I_SH = 128
        ROUTE_SCALE = 2.826
        gates = jnp.einsum('bsd,ed->bse', x, gate_w)
        scores = jax.nn.sigmoid(gates.astype(jnp.float32))
        sel_scores = scores + expert_bias
        _, inds = jax.lax.top_k(sel_scores, K)
        selected = jnp.take_along_axis(scores, inds, axis=-1)
        selected = selected / selected.sum(axis=-1, keepdims=True)
        selected = selected * ROUTE_SCALE
        onehot = jax.nn.one_hot(inds, E, dtype=selected.dtype)
        combine = jnp.einsum('bske,bsk->bse', onehot, selected)
        hg = jnp.einsum('bsd,eid->bsei', x, w_gate)
        hu = jnp.einsum('bsd,eid->bsei', x, w_up)
        h = jax.nn.silu(hg) * hu
        ye = jnp.einsum('bsei,edi->bsed', h, w_down)
        y = jnp.einsum('bsed,bse->bsd', ye, combine).astype(x.dtype)
        g = jnp.einsum('bsd,id->bsi', x, shared_gate_w)
        u = jnp.einsum('bsd,id->bsi', x, shared_up_w)
        y = y + jnp.einsum('bsi,di->bsd', jax.nn.silu(g) * u, shared_down_w)
        return y
    x = L0_attn_x
    mod = (_silu(L0_c) @ L0_wmod).reshape(L0_c.shape[0], 6, 1, -1)
    sa, ca, ga, sb, cb, gb = (mod[:, 0], mod[:, 1], mod[:, 2], mod[:, 3], mod[:, 4], mod[:, 5])
    ga = (2 * (ga >= 0) - 1) * jnp.maximum(jnp.abs(ga), 0.25)
    gb = (2 * (gb >= 0) - 1) * jnp.maximum(jnp.abs(gb), 0.25)
    h = _layernorm(x, axis=-1) * (1 + ca) + sa
    x = x + ga * _L0_attn_ref(h, L0_attn_W_dkv, L0_attn_W_uk, L0_attn_W_uv, L0_attn_W_dq, L0_attn_W_uq, L0_attn_W_qr, L0_attn_W_kr, L0_attn_W_out, L0_attn_idx_wq, L0_attn_idx_wk, L0_attn_idx_w, L0_attn_raw_delta)
    h = _layernorm(x, axis=-1) * (1 + cb) + sb
    x = x + gb * _L0_ffn_ref(h, L0_ffn_wqkv, L0_ffn_q_scale, L0_ffn_k_scale, L0_ffn_wo, L0_ffn_ln_g, L0_ffn_ln_b, L0_ffn_w1, L0_ffn_b1, L0_ffn_w2, L0_ffn_b2)
    mod = (_silu(L1_c) @ L1_wmod).reshape(L1_c.shape[0], 6, 1, -1)
    sa, ca, ga, sb, cb, gb = (mod[:, 0], mod[:, 1], mod[:, 2], mod[:, 3], mod[:, 4], mod[:, 5])
    ga = (2 * (ga >= 0) - 1) * jnp.maximum(jnp.abs(ga), 0.25)
    gb = (2 * (gb >= 0) - 1) * jnp.maximum(jnp.abs(gb), 0.25)
    h = _layernorm(x, axis=-1) * (1 + ca) + sa
    x = x + ga * _L1_attn_ref(h, L1_attn_W_qkv, L1_attn_b_qkv, L1_attn_W_out, L1_attn_b_out)
    h = _layernorm(x, axis=-1) * (1 + cb) + sb
    x = x + gb * _L1_ffn_ref(h, L1_ffn_gate_w, L1_ffn_expert_bias, L1_ffn_w_gate, L1_ffn_w_up, L1_ffn_w_down, L1_ffn_shared_gate_w, L1_ffn_shared_up_w, L1_ffn_shared_down_w)
    return x

_drawn_inputs = setup_inputs


def setup_inputs(seed=0):
    import zlib

    import numpy as np

    out = dict(_drawn_inputs(seed))
    spreads = {'L0_attn_idx_w': (1.0, 0.6),
     'L0_ffn_q_scale': (1.0, 0.6),
     'L0_ffn_k_scale': (1.0, 0.6),
     'L0_ffn_ln_g': (1.0, 0.6),
     'L0_ffn_ln_b': (0.0, 0.8),
     'L0_ffn_b1': (0.0, 0.8),
     'L0_ffn_b2': (0.0, 0.604),
     'L1_ffn_expert_bias': (0.0, 0.8)}
    factors = {'L0_attn_W_qr': 6.237,
     'L0_attn_W_kr': 4.385,
     'L0_attn_idx_wq': 3.373,
     'L0_attn_idx_wk': 3.373,
     'L0_attn_raw_delta': 64.0,
     'L0_ffn_wqkv': 6.915,
     'L0_ffn_wo': 6.91,
     'L0_ffn_w1': 8.0,
     'L0_ffn_w2': 8.0,
     'L1_attn_W_qkv': 7.31,
     'L1_attn_b_qkv': 8.0,
     'L1_attn_W_out': 5.334,
     'L1_attn_b_out': 35.584,
     'L1_ffn_gate_w': 8.0,
     'L1_ffn_w_gate': 8.0,
     'L1_ffn_w_up': 8.0,
     'L1_ffn_w_down': 8.0,
     'L1_ffn_shared_gate_w': 8.0,
     'L1_ffn_shared_up_w': 8.0,
     'L1_ffn_shared_down_w': 8.0,
     'L1_c': 3.63,
     'L1_wmod': 3.527}
    for name, (base, spread) in spreads.items():
        noise = np.random.default_rng([zlib.crc32(name.encode()), seed]).standard_normal(out[name].shape)
        drawn = base * np.exp(spread * noise) if base else spread * noise
        out[name] = jnp.asarray(drawn.astype(out[name].dtype))
    for name, factor in factors.items():
        out[name] = (out[name] * factor).astype(out[name].dtype)
    return out
```

```python
import math
from contextlib import ExitStack

import numpy as np

import concourse.bass as bass
from concourse import mybir

F32 = mybir.dt.float32
BF16 = mybir.dt.bfloat16
U32 = mybir.dt.uint32
ALU = mybir.AluOpType
ACT = mybir.ActivationFunctionType
AX = mybir.AxisListType

P = 128
B, L, D = 8, 256, 128
NB = 2
PASSES = B // NB
NT = NB * L // P
W = NB * L
H, DH, DR, DC, DQ = 8, 64, 32, 32, 64
IH = 4
LW, RANKS = 64, 32
GT = L - LW
GP = 4
NG = GT // GP
GF = DC + 2 * DR
WIN = 64
HID = 341
SETUP = ("weights_loaded", "cols_set", "setup_exp", "c_act_ready", "delta_ready", "delta_sin", "mod_mm", "absorb_mm",
         "setup_done", "dve_setup_step", "act_setup_step")
HC = [128, 128, 85]
E1, TOPK = 16, 8
H1, D1 = 16, 8
WMAX = 192
EXCLUDED, FORWARD, TAKEN = -3.0e38, -1.0e30, -3.4e38
MASKED = -1.0e30
SCALE_A = float(DH + DR) ** -0.5
SCALE_1 = 1.0 / math.sqrt(D1)
ROUTE = 2.826
LN_SHIFT = 65536.0


def shape_constants():
    f = np.float32
    c = {}
    c["ident"] = np.eye(P, dtype=f)
    theta = (1.0 / np.float32(10000.0) ** (2.0 * np.arange(DR // 2, dtype=f) / DR)).astype(f)
    pos = np.arange(L)
    turned = np.where(pos < LW, pos, 2 * pos - (LW - 1))
    ang = np.stack([turned, pos, pos]).astype(f)[:, :, None] * theta
    ang = ang.reshape(3, 2, P, DR // 2).transpose(2, 0, 1, 3).reshape(P, 6, DR // 2).astype(np.float64)
    c["rope_cos"], c["rope_sin"] = np.cos(ang).astype(f), np.sin(ang).astype(f)
    rank = np.arange(LW, LW + RANKS).astype(f)[None, :] * np.tile(theta, 2)[:, None]
    rank = rank.astype(np.float64)
    one = np.ones((DC, RANKS))
    c["rank_a"] = np.concatenate([one, np.cos(rank), np.sin(rank)]).astype(f)
    c["rank_b"] = np.concatenate([one, -np.sin(rank), np.cos(rank)]).astype(f)
    half = np.arange(0, DH, 2, dtype=f)
    inv = (1.0 / np.float32(10000.0) ** (half / DH)).astype(f)
    fr = (np.arange(L, dtype=f)[:, None] * inv[None, :]).astype(np.float64)
    fr = np.concatenate([fr, fr], 1)
    base = ((half + 0.4 * DH) / (1.4 * DH)).astype(np.float64)
    power = (np.arange(L) - L // 2) / float(WIN // 2)
    sc = base[None, :] ** power[:, None]
    sc = np.concatenate([sc, sc], 1)
    sign = np.concatenate([-np.ones(DH // 2), np.ones(DH // 2)])
    x = np.stack([np.cos(fr) * sc, np.cos(fr) / sc, np.sin(fr) * sc * sign, np.sin(fr) / sc * sign], 1)
    c["xpos"] = x.reshape(2, P, 4 * DH).transpose(1, 0, 2).astype(f)
    i = np.arange(P)[:, None]
    j0, j1 = np.arange(P)[None, :], LW + np.arange(WMAX)[None, :]
    ok0 = np.where(i < LW, j0 < LW + RANKS, (j0 <= i) & (j0 > i - LW))
    ok1 = (j1 <= i + P) & (j1 > i + P - LW)
    c["mask_a"] = np.where(np.concatenate([ok0, ok1], 1), 0, MASKED).astype(f)
    ok0 = (j0 <= i) & (j0 >= i - WIN)
    ok1 = (j1 <= i + P) & (j1 >= i + P - WIN)
    c["mask_w"] = np.where(np.concatenate([ok0, ok1], 1), 0, MASKED).astype(f)
    s0, s1 = np.arange(LW + RANKS)[None, :], np.arange(WMAX)[None, :]
    m0 = np.where(s0 < LW, np.where(s0 <= i - LW, 0, EXCLUDED), np.where(s0 > i, FORWARD, EXCLUDED))
    m0[:LW] = 0
    m1 = np.where(s1 <= i + P - LW, 0, EXCLUDED)
    c["mask_i"] = np.concatenate([m0, m1], 1).astype(f)
    c["source"] = (np.arange(P)[:, None] + np.array([[0, P]])).astype(f)
    return c


class Steps:

    def __init__(self, eng, sem):
        self.eng, self.sem, self.n = eng, sem, 0

    def mark(self, ins):
        ins.then_inc(self.sem, 1)
        self.n += 1
        return self.n

    def wait(self, n=None):
        self.eng.wait_ge(self.sem, self.n if n is None else n)

    def link(self, ins):
        self.mark(ins)
        self.wait()


def program(nc, A, out, idx_scratch, score_scratch):
    ctx = ExitStack()
    with ctx:
        def sb(name, shape, dt=F32):
            return ctx.enter_context(nc.sbuf_tensor(name, shape, dt))

        done = ctx.enter_context(nc.semaphore("pass_done"))
        go = {n: ctx.enter_context(nc.semaphore("go_" + n)) for n in ("sp", "act", "dve", "pe")}
        sems = {}

        def sig(name):
            if name not in sems:
                sems[name] = ctx.enter_context(nc.semaphore(name))
            return sems[name]

        SAf = sb("SAf", [P, 4096])
        loads = []

        def weight(name, shape, src=None):
            t = sb("w_" + name, shape)
            loads.append((t[tuple(slice(None) for _ in shape)], A[name] if src is None else src))
            return t

        ident = weight("ident", [P, P])
        rank_a = weight("rank_a", [GF, RANKS])
        rank_b = weight("rank_b", [GF, RANKS])
        mask_a = weight("mask_a", [P, P + WMAX])
        mask_w = weight("mask_w", [P, P + WMAX])
        mask_i = weight("mask_i", [P, LW + RANKS + WMAX])
        source = weight("source", [P, 2])
        cT = weight("cT", [P, 2, B])
        w_kv = weight("w_kv", [D, DC + DR])
        w_ki = weight("w_ki", [D, 2 * DH])
        w_qi = weight("w_qi", [D, IH * DH])
        w_dq = weight("w_dq", [D, DQ])
        w_q2 = weight("w_q2", [DQ, H * DC + H * DR])
        idx_w = sb("idx_w", [P, IH])
        delta_row = sb("delta_row", [P, DR // 2])
        delta_col = weight("delta_col", [GF, 1])
        wqkv = weight("wqkv", [P, 2, 3 * H * DH])
        wo = weight("wo", [P, 2, 4, D])
        ln_gb = weight("ln_gb", [P, 2, 2])
        w1 = weight("w1", [P, 2, 2 * HID])
        b1 = weight("b1", [P, 2, 2, 3])
        w2 = weight("w2", [P, 2, 3, D])
        b2 = weight("b2", [P, 2])
        w1q = weight("w1q", [P, 4, P])
        w1k = weight("w1k", [P, 4, P])
        b1q = weight("b1q", [P, 4])
        b1k = weight("b1k", [P, 4])
        w1v = weight("w1v", [P, D])
        b1v = weight("b1v", [P, 1])
        w1o = weight("w1o", [P, D])
        b1o = weight("b1o", [P, 1])
        gate_w = weight("gate_w", [P, E1])
        e_bias = sb("e_bias", [P, E1])
        region = sb("region", [P, 3 * (E1 + 1) * P])
        experts = region[:, :].rearrange("p (s e n) -> p s e n", s=3, e=E1 + 1)
        parts = np.cumsum([0, NB * NG * DC, NG * GP * H, 3 * 512, 3 * P]).tolist()
        gathT = region[:, parts[0]:parts[1]].rearrange("p (b g c) -> p b g c", b=NB, g=NG)
        pdiag = region[:, parts[1]:parts[2]].rearrange("p (g t h) -> p g t h", g=NG, t=GP)
        gsc = region[:, parts[2]:parts[3]].rearrange("p (i n) -> p i n", i=3)
        xg = region[:, parts[3]:parts[4]].rearrange("p (i n) -> p i n", i=3)
        big = sb("big", [P, 2048])
        wmod = SAf[:, 0:12 * D].rearrange("p (l n) -> p l n", l=2)
        uqT = SAf[0:DH, 1536:2048].rearrange("p (h n) -> p h n", h=H)
        ukT = SAf[0:DH, 2048:2304].rearrange("p (h n) -> p h n", h=H)
        uvT = SAf[0:DH, 2304:2560].rearrange("p (h n) -> p h n", h=H)
        w_out0 = SAf[0:DH, 2560:3584].rearrange("p (h n) -> p h n", h=H)
        xpos = SAf[:, 3584:4096].rearrange("p (t n) -> p t n", t=2)
        qk_scale = big[:, 0:512].rearrange("p (l n) -> p l n", l=2)
        rope_cos = big[:, 512:608].rearrange("p (i n) -> p i n", i=6)
        rope_sin = big[:, 608:704].rearrange("p (i n) -> p i n", i=6)
        rope_t = big[:, 704:896].rearrange("p (s i n) -> p s i n", s=2, i=6)
        for name, t in (("xpos", xpos), ("rope_cos", rope_cos), ("rope_sin", rope_sin), ("wmod", wmod), ("uqT", uqT), ("ukT", ukT), ("uvT", uvT), ("w_out0", w_out0)):
            loads.append((t, A[name]))
        rows = [(idx_w, A["idx_w"]), (delta_row, A["raw_delta"]), (qk_scale, A["qk_scale"]), (e_bias, A["e_bias"])]

        mean_mat = sb("mean_mat", [P, P])
        eps_col = sb("eps_col", [P, 1])
        one_col = sb("one_col", [P, 1])
        shift_col = sb("shift_col", [P, 1])
        modT = sb("modT", [P, 12, B])
        c_act = sb("c_act", [P, 2, B])
        c_den = sb("c_den", [P, 2, B])
        mod_tmp = sb("mod_tmp", [P, 2, B])
        ang = sb("ang", [P, 8, DR // 2])
        ropeC = sb("ropeC", [P, 6, DR])
        ropeS = sb("ropeS", [P, 6, DR])
        dcol = sb("dcol", [GF, 8])
        rank_tab = sb("rank_tab", [GF, RANKS])
        rank_t = sb("rank_t", [GF, RANKS])
        xtab = sb("xtab", [P, 2, 2, 4 * DH])
        w_vo = sb("w_vo", [DC, H, D])
        w_vo4 = sb("w_vo4", [P, 2, D])

        x_tok = sb("x_tok", [P, NT, D])
        y_tok = big[:, 0:W].rearrange("p (k n) -> p k n", k=NT)
        xT = sb("xT", [P, W])
        fT = sb("fT", [P, W])
        hT = sb("hT", [P, W])
        sh = sb("sh", [P, NB, L])
        mod = sb("mod", [P, 12, NB])
        cqT = sb("cqT", [DQ, W])
        kvsrc = sb("kvsrc", [P, NT, GF])
        ckv_b = sb("ckv_b", [P, NB, DC])
        ckv_c = sb("ckv_c", [LW, NB, DC])
        kr_abs = sb("kr_abs", [P, NT, DR])
        kr_raw = sb("kr_raw", [P, NT, DR])
        ka = sb("ka", [P, NT, 2, DC + DR])
        kaT = sb("kaT", [P, W])
        kv_part = [sb(n, [P, NT, GF], BF16) for n in ("kv_hi", "kv_mid", "kv_lo")]
        kv_rem = SAf[:, 0:2 * NT * GF].rearrange("p (s k n) -> p s k n", s=2, k=NT)
        xc, sq, rstd = big[:, 0:W], big[:, W:2 * W], big[:, 2 * W:3 * W]
        irel = big[:, 0:2 * IH * WMAX].rearrange("p (s h n) -> p s h n", s=2, h=IH)
        qa = sb("qa", [P, H, DC + DR])
        qb = sb("qb", [P, H, GF])
        qaT = sb("qaT", [P, 4, W])
        qbT = sb("qbT", [GF, NB, GT, H])
        iscore = sb("iscore", [P, NB, LW + RANKS + WMAX])
        top8 = sb("top8", [P, NT, RANKS])
        topi = sb("topi", [P, NT, RANKS], U32)
        topb = sb("topb", [P, NT, RANKS], BF16)
        kto = sb("kto", [P, 4096])
        q_abs, q_mu, q_c, q_s = (kto[:, 256 * i:256 * i + 256] for i in range(4))
        hot0 = kto[:, 0:3072].bitcast(BF16)
        oTa = kto[:, 3072:4096].rearrange("p (i n) -> p i n", i=2)
        kT = kto[:, 0:2048].rearrange("p (i n) -> p i n", i=4)
        oT = kto[:, 2048:4096].rearrange("p (i n) -> p i n", i=4)
        hot1 = big[:, 0:LW * RANKS // 2].bitcast(BF16)
        wide = sb("wide", [P, GT * RANKS])
        gath = wide[0:GF, :]
        idxb = wide[:, 3072:6144].bitcast(BF16)
        og = wide[0:DC, 0:GT * H].rearrange("p (t h) -> p t h", h=H)
        qiT = wide[:, 0:1024].rearrange("p (i n) -> p i n", i=2)
        kiT = wide[:, 1024:1536]
        vt = wide[:, 0:3072].rearrange("p (b c n) -> p b c n", b=NB, c=3)
        hh = wide[:, 3072:4608].rearrange("p (c n) -> p c n", c=3)
        v1 = wide[:, 0:512].rearrange("p (k n) -> p k n", k=NT)
        att1 = wide[:, 512:1024].rearrange("p (k n) -> p k n", k=NT)
        moe_g = wide[:, 1024:2048].rearrange("p (s n) -> p s n", s=2)
        moe_h = wide[:, 2048:3072].rearrange("p (s n) -> p s n", s=2)
        PT = sb("PT", [P, 4, 512])
        mx = sb("mx", [P, 16, H])
        nb = sb("nb", [P, 16, H])
        ls = sb("ls", [P, 16, H])
        rl = sb("rl", [P, 16, H])
        ssq = sb("ssq", [P, NT, 2 * H])
        rs = sb("rs", [P, NT, 2 * H])
        cqs = sb("cqs", [P, NT, H])
        rt = sb("rt", [P, 8, NT * E1])
        rsm = sb("rsm", [P, 4 * NT + 8 * NT])
        combT = sb("combT", [E1, W])
        ps = ctx.enter_context(nc.psum_tensor("ps", [P, 8, 512], F32))

        def pass_end(eng, name):
            eng.drain().then_inc(done, 1)
            eng.wait_ge(go[name], 1)
            eng.sem_clear(go[name])

        def cols(k):
            return slice(P * k, P * k + P)

        def bcols(b):
            return slice(L * b, L * b + L)

        def keys(T):
            return P if T == 0 else WMAX

        def key_cols(b, T):
            return slice(L * b, L * b + P) if T == 0 else slice(L * b + LW, L * b + L)

        def SA(T, width):
            return SAf[:, 2048 * T:2048 * T + H * width].rearrange("p (h n) -> p h n", h=H)

        def bc(ap, axis, n):
            v = ap.unsqueeze(axis)
            shape = list(v.shape)
            shape[axis] = n
            return v.broadcast_to(shape)

        SCORE_BANKS = {0: [(0, (0, 2, 4, 6)), (1, (1, 3, 5, 7))],
                       1: [(0, (0, 2)), (1, (1, 3)), (2, (4, 6)), (3, (5, 7))]}
        UNITS = {0: [(0, 0), (4, 0)], 1: [(0, 0), (0, 1), (4, 0), (4, 1)]}
        UNITS_BEFORE = [0, 2, 6, 8]

        block = ctx.enter_context(nc.Block())

        @block.sync
        def _(sp):
            for dst, src in loads:
                sp.dma_start(dst, src).then_inc(sig("weights_loaded"), 16)
            for dst, src in rows:
                n = dst.shape[-1] if len(dst.shape) == 2 else dst.shape[1] * dst.shape[2]
                flat = dst[:, :] if len(dst.shape) == 2 else dst[:, :, :].rearrange("p a n -> p (a n)")
                sp.dma_start(flat, src.to_broadcast([P, n])).then_inc(sig("weights_loaded"), 16)
            with sp.Fori(0, PASSES) as it:
                src = A["x"][bass.ds(NB * it, NB), :, :].rearrange("b (t p) d -> p (b t) d", p=P)
                sp.dma_start(x_tok[:, :, :], src).then_inc(sig("x_loaded"), 16)
                for b in range(NB):
                    sp.wait_ge(sig("top_ready"), 2 * b + 2)
                    first = LW * RANKS
                    sp.dma_start(idx_scratch[b, 0:first].rearrange("(p r) -> p r", r=RANKS),
                                 topb[LW:P, 2 * b, :]).then_inc(sig("idx_saved"), 16)
                    sp.dma_start(idx_scratch[b, first:].rearrange("(p r) -> p r", r=RANKS),
                                 topb[:, 2 * b + 1, :]).then_inc(sig("idx_saved"), 16)
                def spread(b):
                    sp.wait_ge(sig("idx_saved"), 32 * NB)
                    if b > 0:
                        sp.wait_ge(sig("gscore_mm"), 3 * b)
                        sp.wait_ge(sig("gathT_mm"), 3 * b)
                    sp.dma_start(idxb, idx_scratch[b:b + 1, :].to_broadcast([P, GT * RANKS]))\
                      .then_inc(sig("idx_spread"), 16)

                spread(0)
                for b in range(NB):
                    for n in range(3):
                        sp.wait_ge(sig("gsc_ready"), 3 * b + n + 1)
                        to = score_scratch[b, n, :].rearrange("(m q c) -> q m c", q=4, c=512)
                        sp.dma_start(to, gsc[:, n, :]).then_inc(sig("gsc_saved"), 16)
                    if b + 1 < NB:
                        spread(b + 1)
                    for n in range(3):
                        sp.wait_ge(sig("gsc_saved"), 48 * (b + 1))
                        T, p0 = (0, LW) if n == 0 else (1, LW * (n - 1))
                        if n == 0 and b > 0:
                            sp.wait_ge(sig("pt_mm"), 6 * b)
                            sp.wait_ge(sig("xg_loaded"), 192 * b)
                        dst = SA(T, keys(T) + RANKS)
                        for t in range(GP):
                            own = score_scratch[b, n, :].rearrange("(t h g u r) -> t u g h r", t=GP, h=H, g=16, u=GP)
                            sp.dma_start(dst[p0 + t:p0 + LW:GP, :, keys(T):], own[t, t])\
                              .then_inc(sig(f"gsc_back{T}"), 16)
                    for T in range(2):
                        sp.wait_ge(sig("att_prob"), 2 * b + T + 1)
                        for n in ([0] if T == 0 else [1, 2]):
                            p0 = LW if n == 0 else LW * (n - 1)
                            for t in range(GP):
                                sp.dma_start(xg[:, n, RANKS * t:RANKS * t + RANKS],
                                             SA(T, keys(T) + RANKS)[p0 + t:p0 + LW:GP, :, keys(T):])\
                                  .then_inc(sig("xg_loaded"), 16)
                sp.wait_ge(sig("a_out"), 2 * NB)
                for i in range(3):
                    sp.dma_start(experts[:, i, :, :], A["experts"][:, i, :, :]).then_inc(sig("experts_loaded"), 16)
                sp.wait_ge(sig("y_ready"), 1)
                dst = out[bass.ds(NB * it, NB), :, :].rearrange("b (t p) d -> p (b t) d", p=P)
                sp.dma_start(dst, y_tok[:, :, :]).then_inc(sig("y_stored"), 16)
                sp.wait_ge(sig("y_stored"), 16)
                pass_end(sp, "sp")

        @block.vector
        def _(dve):
            st = Steps(dve, sig("dve_setup_step"))
            dve.memset(mean_mat[:, :], 1.0 / P).then_inc(sig("cols_set"), 1)
            dve.memset(eps_col[:, :], 1e-5).then_inc(sig("cols_set"), 1)
            dve.memset(one_col[:, :], 1.0).then_inc(sig("cols_set"), 1)
            dve.memset(shift_col[:, :], 0.5 * math.log(LN_SHIFT)).then_inc(sig("cols_set"), 1)
            st.mark(dve.memset(sh[:, :, :], 0.0))
            dve.wait_ge(sig("weights_loaded"), 16 * (len(loads) + len(rows)))
            dve.wait_ge(sig("setup_exp"), 3)
            st.link(dve.tensor_scalar(c_den[:, :, :], c_den[:, :, :], 1.0, None, ALU.add))
            st.link(dve.reciprocal(c_act[:, :, :], c_den[:, :, :]))
            dve.tensor_tensor(c_act[:, :, :], c_act[:, :, :], cT[:, :, :], ALU.mult).then_inc(sig("c_act_ready"), 1)
            for t in (ang[:, 0:5, :], dcol[:, 0:5].unsqueeze(2)):
                st.link(dve.tensor_scalar(t[:, 1, :], t[:, 0, :], 1.0, None, ALU.add))
                st.link(dve.reciprocal(t[:, 2, :], t[:, 1, :]))
                st.link(dve.tensor_scalar(t[:, 3, :], t[:, 2, :], -2.0 * math.pi, math.pi, ALU.mult, ALU.add))
                dve.tensor_scalar(t[:, 4, :], t[:, 3, :], 0.5, None, ALU.mult).then_inc(sig("delta_ready"), 1)
            dve.wait_ge(sig("delta_sin"), 4)
            for t in (ang, dcol[:, :].unsqueeze(2)):
                st.link(dve.tensor_scalar(t[:, 5, :], t[:, 5, :], -1.0, None, ALU.mult))
                st.link(dve.tensor_tensor(t[:, 7, :], t[:, 6, :], t[:, 6, :], ALU.mult))
                st.link(dve.tensor_scalar(t[:, 6, :], t[:, 7, :], 2.0, -1.0, ALU.mult, ALU.add))
            sd, cd = bc(ang[:, 5, :], 1, 6), bc(ang[:, 6, :], 1, 6)
            hd = DR // 2
            st.mark(dve.tensor_tensor(rope_t[:, 0, :, :], rope_cos[:, :, :], cd, ALU.mult))
            st.link(dve.tensor_tensor(rope_t[:, 1, :, :], rope_sin[:, :, :], sd, ALU.mult))
            st.link(dve.tensor_tensor(ropeC[:, :, 0:hd], rope_t[:, 0, :, :], rope_t[:, 1, :, :], ALU.subtract))
            st.mark(dve.tensor_copy(ropeC[:, :, hd:DR], ropeC[:, :, 0:hd]))
            st.mark(dve.tensor_tensor(rope_t[:, 0, :, :], rope_sin[:, :, :], cd, ALU.mult))
            st.link(dve.tensor_tensor(rope_t[:, 1, :, :], rope_cos[:, :, :], sd, ALU.mult))
            st.link(dve.tensor_tensor(ropeS[:, :, hd:DR], rope_t[:, 0, :, :], rope_t[:, 1, :, :], ALU.add))
            st.mark(dve.tensor_scalar(ropeS[:, 0:4, 0:hd], ropeS[:, 0:4, hd:DR], -1.0, None, ALU.mult))
            st.mark(dve.tensor_copy(ropeS[:, 4:6, 0:hd], ropeS[:, 4:6, hd:DR]))
            st.link(dve.tensor_scalar(rank_t[:, :], rank_a[:, :], dcol[:, 6:7], None, ALU.mult))
            st.link(dve.scalar_tensor_tensor(rank_tab[:, :], rank_b[:, :], dcol[:, 5:6], rank_t[:, :], ALU.mult, ALU.add))
            st.mark(dve.memset(rank_tab[0:DC, :], 1.0))
            for l in range(2):
                for T in range(2):
                    st.mark(dve.tensor_tensor(xtab[:, l, T, :], xpos[:, T, :], qk_scale[:, l, :], ALU.mult))
            dve.wait_ge(sig("mod_mm"), 1)
            st.link(dve.tensor_copy(modT[:, :, :], ps[:, 0, 0:12 * B].rearrange("p (j b) -> p j b", b=B)))
            for j in (1, 4, 7, 10):
                st.mark(dve.tensor_scalar(modT[:, j, :], modT[:, j, :], 1.0, None, ALU.add))
            for j in (2, 5, 8, 11):
                st.mark(dve.tensor_scalar(mod_tmp[:, 0, :], modT[:, j, :], 0.0, None, ALU.is_ge))
                st.link(dve.scalar_tensor_tensor(mod_tmp[:, 1, :], modT[:, j, :], -1.0, modT[:, j, :], ALU.mult, ALU.max))
                st.link(dve.tensor_scalar(mod_tmp[:, 1, :], mod_tmp[:, 1, :], 0.25, None, ALU.max))
                st.link(dve.tensor_scalar(mod_tmp[:, 0, :], mod_tmp[:, 0, :], 2.0, -1.0, ALU.mult, ALU.add))
                st.link(dve.tensor_tensor(modT[:, j, :], mod_tmp[:, 0, :], mod_tmp[:, 1, :], ALU.mult))
            dve.wait_ge(sig("absorb_mm"), 3)
            st.mark(dve.tensor_copy(w_q2[:, 0:H * DC], ps[0:DQ, 1, 0:H * DC]))
            for h in range(H):
                st.mark(dve.tensor_copy(w_vo[:, h, :], ps[0:DC, 2 + h // 4, D * (h % 4):D * (h % 4) + D]))
            dve.tensor_copy(w_vo4[:, :, :], ps[:, 4, 0:2 * D].rearrange("p (i n) -> p i n", i=2))\
               .then_inc(sig("setup_done"), 1)
            dve.wait_ge(sig("setup_done"), 1)

            with dve.Fori(0, PASSES) as it:
                st = Steps(dve, sig("dve_step"))
                st.link(dve.tensor_copy(mod[:, :, :], modT[:, :, bass.ds(NB * it, NB)]))

                def layernorm(n, src, modulate, nout):
                    dve.wait_ge(sig("ln_mean"), n + 1)
                    dve.tensor_tensor(xc, src, ps[:, 0, :], ALU.subtract).then_inc(sig("ln_centered"), 1)
                    dve.wait_ge(sig("ln_centered"), n + 1)
                    dve.wait_ge(sig("ln_rstd"), n + 1)
                    st.link(dve.tensor_tensor(xc, xc, rstd, ALU.mult))
                    modulate()

                def by_batch(c, s, dst):
                    def go_():
                        for b in range(NB):
                            dve.tensor_scalar(dst[:, bcols(b)], xc[:, bcols(b)], mod[:, c, b:b + 1], mod[:, s, b:b + 1],
                                              ALU.mult, ALU.add).then_inc(sig("ln_out"), 1)
                    return go_

                def tile_max(a, T, width, factor):
                    st.link(dve.tensor_reduce(mx[:, a % 4, :], SA(T, width)[:, :, :], AX.X, ALU.max))
                    if factor is None:
                        ins = dve.tensor_scalar(nb[:, a % 4, :], mx[:, a % 4, :], -SCALE_A, None, ALU.mult)
                    else:
                        ins = dve.scalar_tensor_tensor(nb[:, a % 4, :], mx[:, a % 4, :], -1.0, factor, ALU.mult, ALU.mult)
                    ins.then_inc(sig("att_bias"), 1)

                def tile_scores(a, T, width, mask):
                    dve.wait_ge(sig("att_mm"), a + 1)
                    n, off = keys(T), P * T
                    for bank, heads in SCORE_BANKS[T]:
                        k = len(heads)
                        ins = dve.tensor_tensor(
                            SA(T, width)[:, heads[0]:heads[-1] + 1:2, 0:n],
                            ps[:, bank, 0:k * n].rearrange("p (h n) -> p h n", h=k),
                            bc(mask[:, off:off + n], 1, k), ALU.add)
                    ins.then_inc(sig("att_evac"), 1)
                    dve.wait_ge(sig("att_evac"), a + 1)

                def tile_norm(a, T, width):
                    dve.wait_ge(sig("att_exp"), a + 1)
                    st.link(dve.reciprocal(rl[:, a % 4, :], ls[:, a % 4, :]))
                    v = SA(T, width)[:, :, :]
                    dve.tensor_tensor(v, v, bc(rl[:, a % 4, :], 2, width), ALU.mult).then_inc(sig("att_prob"), 1)

                def tile_pt(a, T):
                    for u in range(len(UNITS[T])):
                        if u % 2:
                            dve.wait_ge(sig("pt_mm"), 12 * (a // 4) + UNITS_BEFORE[a % 4] + u + 1)
                            rows_ = P if UNITS[T][u][1] == 0 else LW
                            dve.tensor_copy(PT[0:rows_, u, :], ps[0:rows_, 4 + u % 3, :]).then_inc(sig("pt_dve"), 1)

                dve.wait_ge(sig("xT_copied"), 1)
                layernorm(0, xT[:, :], by_batch(1, 0, hT), 2)
                dve.wait_ge(sig("kr_abs"), 1)
                kvp = ps[:, 6, 0:NT * (DC + DR)].rearrange("p (k n) -> p k n", k=NT)
                n = NT * (DC + DR)
                st.mark(dve.tensor_copy(kr_raw[:, :, :], kvp[:, :, DC:]))
                st.mark(dve.tensor_copy(kvsrc[:, :, 0:DC], kvp[:, :, 0:DC]))
                st.mark(dve.tensor_copy(ckv_b[:, :, :], ps[:, 6, n:n + NB * DC].rearrange("p (b n) -> p b n", b=NB)))
                n += NB * DC
                st.link(dve.tensor_copy(ckv_c[:, :, :], ps[0:LW, 6, n:n + NB * DC].rearrange("p (b n) -> p b n", b=NB)))
                dve.wait_ge(sig("kr_log"), 1)
                st.link(dve.scalar_tensor_tensor(kvsrc[:, :, DC:2 * DC], kr_raw[:, :, :], 0.0, kr_abs[:, :, :],
                                                 ALU.max, ALU.add))
                st.mark(dve.tensor_scalar(kvsrc[:, :, 64:80], kvsrc[:, :, 48:64], -1.0, None, ALU.mult))
                dve.tensor_copy(kvsrc[:, :, 80:96], kvsrc[:, :, 32:48]).then_inc(sig("kvsrc_ready"), 1)
                dve.wait_ge(sig("kvsrc_ready"), 1)
                for b in range(NB):
                    kk = slice(2 * b, 2 * b + 2)
                    st.mark(dve.tensor_tensor(kr_raw[:, kk, :], kvsrc[:, kk, 32:64], ropeC[:, 4:6, :], ALU.mult))
                    st.link(dve.tensor_tensor(kr_abs[:, kk, :], kvsrc[:, kk, 64:96], ropeS[:, 4:6, :], ALU.mult))
                for j in range(2):
                    st.mark(dve.tensor_copy(ka[:, :, j, 0:DC], kvsrc[:, :, 0:DC]))
                    dve.tensor_tensor(ka[:, :, j, DC:], kr_raw[:, :, :], kr_abs[:, :, :], ALU.add)\
                       .then_inc(sig("ka_ready"), 1)

                for k in range(NT):
                    b, T = k // 2, k % 2
                    n = LW if T == 0 else WMAX
                    width = LW + RANKS if T == 0 else WMAX
                    off = 0 if T == 0 else LW + RANKS
                    iv = iscore[:, b, off:off + width]
                    dve.wait_ge(sig("irel"), 2 * k + 2)
                    for h in range(IH):
                        add = mask_i[:, off:off + n] if h == 0 else iv[:, 0:n]
                        st.link(dve.scalar_tensor_tensor(iv[:, 0:n], irel[:, k % 2, h, 0:n], idx_w[:, h:h + 1], add,
                                                         ALU.mult, ALU.add))
                    if T == 0:
                        st.link(dve.tensor_copy(iv[:, n:width], mask_i[:, n:width]))
                    for r in range(0, RANKS, 8):
                        st.link(dve.max(top8[:, k, r:r + 8], iv))
                        st.link(dve.max_index(topi[:, k, r:r + 8], top8[:, k, r:r + 8], iv))
                        st.link(dve.match_replace(iv, top8[:, k, r:r + 8], iv, TAKEN))
                    dve.tensor_copy(topb[:, k, :], topi[:, k, :]).then_inc(sig("top_ready"), 1)

                v8 = lambda ap: ap.rearrange("p (h n) -> p h n", h=H)
                for k in range(NT):
                    T = k % 2
                    raw = ps[:, 5 + k % 2, 0:H * DR]
                    dve.wait_ge(sig("q2_log"), k + 1)
                    st.link(dve.scalar_tensor_tensor(q_mu, raw, 0.0, q_abs, ALU.max, ALU.add))
                    if k > 0:
                        dve.wait_ge(sig("q_turned"), k)
                    for s, dsts in ((0, (qa[:, :, DC:],)), (1, (qb[:, :, DC:2 * DC], qb[:, :, 2 * DC:]))):
                        C, Sn = ropeC[:, 2 * s + T, :], ropeS[:, 2 * s + T, :]
                        st.mark(dve.tensor_tensor(v8(q_c), v8(q_mu), bc(C, 1, H), ALU.mult))
                        st.mark(dve.tensor_tensor(v8(q_s)[:, :, 0:16], v8(q_mu)[:, :, 16:32], bc(Sn[:, 0:16], 1, H), ALU.mult))
                        st.link(dve.tensor_tensor(v8(q_s)[:, :, 16:32], v8(q_mu)[:, :, 0:16], bc(Sn[:, 16:32], 1, H), ALU.mult))
                        for dst in dsts:
                            dve.tensor_tensor(dst, v8(q_c), v8(q_s), ALU.add).then_inc(sig("q_ready"), 1)
                        dve.wait_ge(sig("q_ready"), 3 * k + (1, 3)[s])
                    dve.wait_ge(sig("q_turned"), k + 1)
                    t0, t1, p0 = (0, LW, LW) if T == 0 else (LW, GT, 0)
                    for i in range(2):
                        src = ps[0:GF, 3 + i, :].rearrange("p (h t) -> p t h", h=4)[:, p0:P, :]
                        dve.tensor_copy(qbT[:, k // 2, t0:t1, 4 * i:4 * i + 4], src).then_inc(sig("qb_copied"), 1)

                for b in range(NB):
                    dve.wait_ge(sig("idx_spread"), 16 * (b + 1))
                    if b > 0:
                        dve.wait_ge(sig("gather_mm"), 12 * b)
                    dve.tensor_scalar(hot0[:, :], idxb, source[:, 0:1], None, ALU.is_equal).then_inc(sig("hot_ready"), 1)
                    dve.tensor_scalar(hot1[:, :], idxb[:, 2 * LW * RANKS:], source[:, 1:2], None, ALU.is_equal)\
                       .then_inc(sig("hot_ready"), 1)
                    dve.wait_ge(sig("hot_ready"), 2 * b + 2)
                    if b > 0:
                        dve.wait_ge(sig("gscore_mm"), 3 * b)
                        dve.wait_ge(sig("gathT_mm"), 3 * b)
                    for g in range(12):
                        dve.wait_ge(sig("gather_mm"), 12 * b + g + 1)
                        dve.tensor_tensor(gath[:, 512 * g:512 * g + 512].rearrange("p (t r) -> p t r", r=RANKS),
                                          ps[0:GF, 2 + g % 2, :].rearrange("p (t r) -> p t r", r=RANKS),
                                          bc(rank_tab[:, :], 1, 16), ALU.mult).then_inc(sig("gath_evac"), 1)

                for b in range(NB):
                    if b > 0:
                        dve.wait_ge(sig("xg_loaded"), 192 * b)
                        dve.wait_ge(sig("pt_mm"), 6 * b)
                        dve.wait_ge(sig("gsc_back0"), 64 * b)
                        dve.wait_ge(sig("gsc_back1"), 128 * b)
                    st.link(dve.memset(SA(0, P + RANKS)[0:LW, :, P:], MASKED))
                    for T in range(2):
                        a = 2 * b + T
                        tile_scores(a, T, keys(T) + RANKS, mask_a)
                        dve.wait_ge(sig(f"gsc_back{T}"), 64 * (1 + T) * (b + 1))
                        tile_max(a, T, keys(T) + RANKS, None)
                    for T in range(2):
                        tile_norm(2 * b + T, T, keys(T) + RANKS)
                    for T in range(2):
                        tile_pt(2 * b + T, T)
                    dve.wait_ge(sig("a_out"), 2 * b + 2)
                    xb = xT[:, bcols(b)]
                    st.link(dve.scalar_tensor_tensor(xb, ps[:, 4, 0:L], mod[:, 2, b:b + 1], xb, ALU.mult, ALU.add))
                    xl = xT[:, L * b + LW:L * b + L]
                    dve.scalar_tensor_tensor(xl, ps[:, 5, 0:GT], mod[:, 2, b:b + 1], xl, ALU.mult, ALU.add)\
                       .then_inc(sig("x_updated"), 1)

                dve.wait_ge(sig("x_updated"), 2)
                layernorm(1, xT[:, :], by_batch(4, 3, fT), 4)
                dve.wait_ge(sig("ln_out"), 4)

                def shift(n):
                    v = fT[:, :].rearrange("p (b t) -> p b t", b=NB)
                    dve.tensor_copy(sh[0:64, :, :], v[0:64, :, :]).then_inc(sig("shifted"), 1)
                    dve.tensor_copy(sh[64:P, :, 1:L], v[64:P, :, 0:L - 1]).then_inc(sig("shifted"), 1)
                    dve.wait_ge(sig("shifted"), 2 * n + 2)

                for l in range(2):
                    shift(2 * l)
                    for k in range(NT):
                        T = k % 2
                        m = NT * l + k
                        dve.wait_ge(sig("qk_squared"), m + 1)
                        pb = 2 * (k % 2)
                        v3 = lambda ap: ap.rearrange("p (s h n) -> p s h n", s=2, h=H)
                        qk = ps[:, pb:pb + 2, :].rearrange("p s (h n) -> p s h n", h=H)
                        r0, r1 = v3(big[:, 0:1024]), v3(big[:, 1024:2048])
                        tab = xtab[:, l, T, :].rearrange("p (c s n) -> p c s n", c=2, s=2)
                        if m > 0:
                            dve.wait_ge(sig("qk_turned"), m)
                        hh_ = DH // 2
                        st.mark(dve.tensor_tensor(r0, qk, bc(tab[:, 0, :, :], 2, H), ALU.mult))
                        st.mark(dve.tensor_tensor(r1[:, :, :, 0:hh_], qk[:, :, :, hh_:], bc(tab[:, 1, :, 0:hh_], 2, H), ALU.mult))
                        st.link(dve.tensor_tensor(r1[:, :, :, hh_:], qk[:, :, :, 0:hh_], bc(tab[:, 1, :, hh_:], 2, H), ALU.mult))
                        st.mark(dve.tensor_tensor(big[:, 0:1024], big[:, 0:1024], big[:, 1024:2048], ALU.add))
                        st.link(dve.tensor_reduce(ssq[:, k, :], SAf[:, 1024 * (k % 2):1024 * (k % 2) + 1024]
                                                  .rearrange("p (h n) -> p h n", n=DH), AX.X, ALU.add))
                        dve.tensor_scalar(ssq[:, k, :], ssq[:, k, :], 1e-24, None, ALU.max).then_inc(sig("ssq_ready"), 1)
                        dve.wait_ge(sig("rs_ready"), m + 1)
                        st.mark(dve.tensor_scalar(cqs[:, k, :], rs[:, k, 0:H], 8.0, None, ALU.mult))
                        kk = big[:, 512:1024].rearrange("p (h n) -> p h n", h=H)
                        dve.tensor_tensor(kk, kk, bc(rs[:, k, H:], 2, DH), ALU.mult).then_inc(sig("qk_ready"), 1)
                        dve.wait_ge(sig("qk_turned"), m + 1)
                        dve.tensor_copy(kT[:, :, cols(k)], ps[:, 7, :].rearrange("p (i n) -> p i n", i=4))\
                           .then_inc(sig("k_copied"), 1)
                    for k in range(NT):
                        T, a = k % 2, 4 + 4 * l + k
                        if k >= 2:
                            dve.wait_ge(sig("pt_mm"), 12 * (l + 1) + UNITS_BEFORE[k - 1])
                        tile_scores(a, T, keys(T), mask_w)
                        tile_max(a, T, keys(T), cqs[:, k, :])
                        if k > 0:
                            tile_norm(a - 1, 1 - T, keys(1 - T))
                            tile_pt(a - 1, 1 - T)
                    tile_norm(a, T, keys(T))
                    tile_pt(a, T)
                    dve.wait_ge(sig("f_o"), l + 1)
                    st.link(dve.tensor_tensor(fT[:, :], ps[:, 0, :], fT[:, :], ALU.add))
                    shift(2 * l + 1)

                    def affine():
                        dve.tensor_scalar(hT[:, :], xc, ln_gb[:, l, 0:1], ln_gb[:, l, 1:2], ALU.mult, ALU.add)\
                           .then_inc(sig("ln_out"), 1)

                    layernorm(2 + l, sh[:, :, :].rearrange("p b t -> p (b t)"), affine, 5 + l)
                    for c in range(3):
                        dve.wait_ge(sig("f_a"), 3 * l + c + 1)
                        dve.wait_ge(sig("f_gelu"), 3 * l + c + 1)
                        m = HC[c]
                        dve.scalar_tensor_tensor(hh[0:m, c, :], ps[0:m, c, :], b1[0:m, l, 0, c:c + 1], PT[0:m, c, :],
                                                 ALU.add, ALU.mult).then_inc(sig("f_hidden"), 1)
                    dve.wait_ge(sig("f_down"), l + 1)
                    dve.scalar_tensor_tensor(fT[:, :], ps[:, 6, :], b2[:, l:l + 1], fT[:, :], ALU.add, ALU.add)\
                       .then_inc(sig("f_done"), 1)
                    dve.wait_ge(sig("f_done"), l + 1)
                for b in range(NB):
                    dve.scalar_tensor_tensor(xT[:, bcols(b)], fT[:, bcols(b)], mod[:, 5, b:b + 1], xT[:, bcols(b)],
                                             ALU.mult, ALU.add).then_inc(sig("x_updated"), 1)

                dve.wait_ge(sig("x_updated"), 4)
                layernorm(4, xT[:, :], by_batch(7, 6, hT), 8)
                for m in range(4):
                    dve.wait_ge(sig("qk1_mm"), 2 * m + 2)
                    dve.tensor_scalar(kT[:, m, :], ps[:, 4 + m, :], b1k[:, m:m + 1], None, ALU.add).then_inc(sig("k1_copied"), 1)
                for u in range(2 * NT):
                    k, half = u // 2, u % 2
                    dve.wait_ge(sig("l1_mm"), u + 1)
                    sc = ps[:, 0:4, :].rearrange("p g (j n) -> p g j n", j=2)
                    st.link(dve.tensor_reduce(mx[:, u, :].rearrange("p (g j) -> p g j", j=2), sc, AX.X, ALU.max))
                    dve.tensor_scalar(nb[:, u, :], mx[:, u, :], -SCALE_1, None, ALU.mult).then_inc(sig("l1_bias"), 1)

                    def back(u):
                        k, half = u // 2, u % 2
                        dve.wait_ge(sig("l1_exp"), u + 1)
                        st.link(dve.reciprocal(rl[:, u, :], ls[:, u, :]))
                        for z in (1, 3):
                            dve.wait_ge(sig("l1_turned"), 4 * u + z + 1)
                            dve.tensor_copy(PT[:, z, :], ps[:, 4 + z % 3, :]).then_inc(sig("l1_pt_dve"), 1)
                        dve.wait_ge(sig("l1_pv"), u + 1)
                        o = slice(64 * half, 64 * half + 64)
                        dve.tensor_tensor(att1[:, k, o].rearrange("p (j g n) -> p g j n", j=2, g=4),
                                          ps[:, 7, P * k + 64 * half:P * k + 64 * half + 64]
                                          .rearrange("p (j g n) -> p g j n", j=2, g=4),
                                          bc(rl[:, u, :].rearrange("p (g j) -> p g j", j=2), 3, D1), ALU.mult)\
                           .then_inc(sig("att1_ready"), 1)
                    if u > 0:
                        back(u - 1)
                back(u)
                dve.wait_ge(sig("l1_out"), 1)
                for b in range(NB):
                    st.link(dve.tensor_scalar(xc[:, bcols(b)], ps[:, 1, bcols(b)], b1o[:, 0:1], mod[:, 8, b:b + 1],
                                              ALU.add, ALU.mult))
                    dve.tensor_tensor(xT[:, bcols(b)], xT[:, bcols(b)], xc[:, bcols(b)], ALU.add).then_inc(sig("x_updated"), 1)

                dve.wait_ge(sig("x_updated"), 6)
                layernorm(5, xT[:, :], by_batch(10, 9, hT), 10)
                v4 = lambda ap: ap.rearrange("p (k e) -> p k e", e=E1)
                den, sc, sel, rep, msk, wgt = (rt[:, i, :] for i in range(6))
                dve.wait_ge(sig("route_exp"), 1)
                st.link(dve.tensor_scalar(den, den, 1.0, None, ALU.add))
                st.link(dve.reciprocal(sc, den))
                st.link(dve.tensor_tensor(v4(sel), v4(sc), bc(e_bias[:, :], 1, NT), ALU.add))
                for k in range(NT):
                    st.mark(dve.max(rsm[:, 8 * k:8 * k + 8], v4(sel)[:, k, :]))
                st.wait()
                for k in range(NT):
                    st.mark(dve.match_replace(v4(rep)[:, k, :], rsm[:, 8 * k:8 * k + 8], v4(sel)[:, k, :], TAKEN))
                st.wait()
                st.link(dve.tensor_tensor(msk, rep, sel, ALU.not_equal))
                st.link(dve.tensor_tensor(wgt, msk, sc, ALU.mult))
                st.link(dve.tensor_reduce(rsm[:, 32:36], v4(wgt), AX.X, ALU.add))
                st.link(dve.reciprocal(rsm[:, 36:40], rsm[:, 32:36]))
                dve.scalar_tensor_tensor(v4(rt[:, 6, :]), v4(wgt), ROUTE, bc(rsm[:, 36:40], 2, E1), ALU.mult, ALU.mult)\
                   .then_inc(sig("comb_ready"), 1)
                for e in range(E1 + 1):
                    s = e % 2
                    dve.wait_ge(sig("e_silu"), e + 1)
                    dve.wait_ge(sig("e_up"), e + 1)
                    if e >= 2:
                        dve.wait_ge(sig("e_down"), e - 1)
                    ins = dve.tensor_tensor(moe_h[:, s, :], moe_g[:, s, :], ps[:, 2 + s, :], ALU.mult)
                    if e < E1:
                        st.link(ins)
                        dve.wait_ge(sig("e_comb"), e + 1)
                        ins = dve.tensor_tensor(moe_h[:, s, :], moe_h[:, s, :], ps[:, 4 + s, :], ALU.mult)
                    ins.then_inc(sig("e_hidden"), 1)
                dve.wait_ge(sig("e_down"), E1 + 1)
                for b in range(NB):
                    dve.scalar_tensor_tensor(xT[:, bcols(b)], ps[:, 6, bcols(b)], mod[:, 11, b:b + 1], xT[:, bcols(b)],
                                             ALU.mult, ALU.add).then_inc(sig("x_updated"), 1)
                pass_end(dve, "dve")

        @block.scalar
        def _(act):
            st = Steps(act, sig("act_setup_step"))
            act.wait_ge(sig("weights_loaded"), 16 * (len(loads) + len(rows)))
            act.wait_ge(sig("cols_set"), 4)
            act.activation(c_den[:, :, :], cT[:, :, :], ACT.Exp, scale=-1.0).then_inc(sig("setup_exp"), 1)
            act.activation(ang[:, 0, :], delta_row[:, :], ACT.Exp, scale=-1.0).then_inc(sig("setup_exp"), 1)
            act.activation(dcol[:, 0:1], delta_col[:, :], ACT.Exp, scale=-1.0).then_inc(sig("setup_exp"), 1)
            act.wait_ge(sig("delta_ready"), 2)
            for t in (ang, dcol[:, :].unsqueeze(2)):
                for i in range(2):
                    act.activation(t[:, 5 + i, :], t[:, 3 + i, :], ACT.Sin).then_inc(sig("delta_sin"), 1)
            act.wait_ge(sig("setup_done"), 1)

            with act.Fori(0, PASSES) as it:
                st = Steps(act, sig("act_step"))
                act.wait_ge(sig("x_turned"), 1)
                act.activation(xT[:, :], ps[:, 0, :], ACT.Copy).then_inc(sig("xT_copied"), 1)

                def layernorm(n):
                    act.wait_ge(sig("ln_centered"), n + 1)
                    act.activation(sq, xc, ACT.Square).then_inc(sig("ln_squared"), 1)
                    act.wait_ge(sig("ln_var"), n + 1)
                    st.link(act.activation(rstd, ps[:, 1, :], ACT.Ln, bias=eps_col[:, :]))
                    act.activation(rstd, rstd, ACT.Exp, scale=-0.5).then_inc(sig("ln_rstd"), 1)

                def tile_exp(a, T, width, scale):
                    act.wait_ge(sig("att_bias"), a + 1)
                    for h in range(H):
                        v = SA(T, width)[:, h, :]
                        ins = act.activation(v, v, ACT.Exp, bias=nb[:, a % 4, h:h + 1],
                                             scale=SCALE_A if scale is None else scale[:, h:h + 1],
                                             accum_out=ls[:, a % 4, h:h + 1])
                    ins.then_inc(sig("att_exp"), 1)

                def tile_pt(a, T):
                    for u in range(0, len(UNITS[T]), 2):
                        act.wait_ge(sig("pt_mm"), 12 * (a // 4) + UNITS_BEFORE[a % 4] + u + 1)
                        act.activation(PT[:, u, :], ps[:, 4 + u % 3, :], ACT.Copy).then_inc(sig("pt_act"), 1)

                def tile_out(a, dst):
                    act.wait_ge(sig("att_pv"), a + 1)
                    n = dst.shape[1]
                    act.activation(dst[:, :, cols(a % 4)], ps[:, 7, 0:n * P].rearrange("p (i n) -> p i n", i=n), ACT.Copy)\
                       .then_inc(sig("o_copied"), 1)

                layernorm(0)
                for i, (dst, bank) in enumerate(((kiT, 3), (qiT[:, 0, :], 4), (qiT[:, 1, :], 5))):
                    act.wait_ge(sig("a_proj"), i + 1)
                    act.activation(dst, ps[:, bank, :], ACT.Copy).then_inc(sig("a_copied"), 1)
                act.wait_ge(sig("a_proj"), 4)
                act.activation(cqT[:, :], ps[0:DQ, 2, :], ACT.Copy).then_inc(sig("a_copied"), 1)
                act.wait_ge(sig("kv_proj"), 1)
                kvp = ps[:, 6, 0:NT * (DC + DR)].rearrange("p (k n) -> p k n", k=NT)
                act.activation(kr_abs[:, :, :], kvp[:, :, DC:], ACT.Abs).then_inc(sig("kr_abs"), 1)
                act.wait_ge(sig("kr_abs"), 1)
                st.link(act.activation(kr_abs[:, :, :], kr_abs[:, :, :], ACT.Exp, scale=-1.0))
                act.activation(kr_abs[:, :, :], kr_abs[:, :, :], ACT.Ln, bias=one_col[:, :]).then_inc(sig("kr_log"), 1)
                for k in range(NT):
                    n = LW if k % 2 == 0 else WMAX
                    act.wait_ge(sig("iscore_mm"), k + 1)
                    if k >= 2:
                        act.wait_ge(sig("top_ready"), k - 1)
                    for j in range(2):
                        act.activation(irel[:, k % 2, j:j + 3:2, 0:n],
                                       ps[:, 2 + 2 * (k % 2) + j, 0:2 * n].rearrange("p (h n) -> p h n", h=2),
                                       ACT.Relu).then_inc(sig("irel"), 1)
                act.wait_ge(sig("kaT_turned"), 1)
                act.activation(kaT[:, :], ps[:, 7, :], ACT.Copy).then_inc(sig("ka_copied"), 1)
                for k in range(NT):
                    act.wait_ge(sig("q2_mm"), k + 1)
                    if k > 0:
                        act.wait_ge(sig("q_ready"), 3 * k)
                    st.link(act.activation(q_abs, ps[:, 5 + k % 2, 0:H * DR], ACT.Abs))
                    st.link(act.activation(q_abs, q_abs, ACT.Exp, scale=-1.0))
                    act.activation(q_abs, q_abs, ACT.Ln, bias=one_col[:, :]).then_inc(sig("q2_log"), 1)
                    if k > 0:
                        act.wait_ge(sig("q_turned"), k)
                    lat = ps[:, k % 2, 0:256].rearrange("p (h n) -> p h n", h=H)
                    act.activation(qa[:, :, 0:DC], lat, ACT.Copy).then_inc(sig("q_latent"), 1)
                    act.activation(qb[:, :, 0:DC], lat, ACT.Copy).then_inc(sig("q_latent"), 1)
                    act.wait_ge(sig("q_turned"), k + 1)
                    act.activation(qaT[:, :, cols(k)], ps[:, 2, :].rearrange("p (i n) -> p i n", i=4), ACT.Copy)\
                       .then_inc(sig("qa_copied"), 1)
                for b in range(NB):
                    if b > 0:
                        act.wait_ge(sig("gsc_saved"), 48 * b)
                    for n in range(3):
                        act.wait_ge(sig("gathT_mm"), 3 * b + n + 1)
                        act.activation(gathT[:, b, 16 * n:16 * n + 16, :],
                                       ps[:, n % 2, :].rearrange("p (j c) -> p j c", c=DC), ACT.Copy)\
                           .then_inc(sig("gathT_ready"), 1)
                        act.wait_ge(sig("gscore_mm"), 3 * b + n + 1)
                        act.activation(gsc[:, n, :], ps[:, 5 + n, :], ACT.Copy).then_inc(sig("gsc_ready"), 1)
                for b in range(NB):
                    for T in range(2):
                        tile_exp(2 * b + T, T, keys(T) + RANKS, None)
                    for T in range(2):
                        tile_pt(2 * b + T, T)
                        tile_out(2 * b + T, oTa)
                    act.wait_ge(sig("xg_turned"), b + 1)
                    act.wait_ge(sig("pdiag_zero"), 1)
                    for t in range(GP):
                        part = slice(RANKS * t, RANKS * t + RANKS)
                        act.activation(pdiag[part, :, t, :], ps[part, 0, 0:3 * P].rearrange("p (j h) -> p j h", h=H),
                                       ACT.Copy).then_inc(sig("pdiag_ready"), 1)
                    for n in range(3):
                        act.wait_ge(sig("og_mm"), 3 * b + n + 1)
                        act.activation(og[:, 64 * n:64 * n + 64, :],
                                       ps[0:DC, 1 + n, :].rearrange("p (t h) -> p t h", h=H), ACT.Copy)\
                           .then_inc(sig("og_ready"), 1)

                layernorm(1)
                for l in range(2):
                    def values(b, c):
                        act.wait_ge(sig("v_mm"), 6 * l + 3 * b + c + 1)
                        r = LW if c == 2 else P
                        act.activation(vt[0:r, b, c, :], ps[0:r, 4 + c % 2, :], ACT.Copy).then_inc(sig("v_copied"), 1)

                    for k in range(NT):
                        m = NT * l + k
                        act.wait_ge(sig("qk_mm"), m + 1)
                        if k >= 2:
                            act.wait_ge(sig("ssq_ready"), m - 1)
                        act.activation(SAf[:, 1024 * (k % 2):1024 * (k % 2) + 1024]
                                       .rearrange("p (s n) -> p s n", s=2),
                                       ps[:, 2 * (k % 2):2 * (k % 2) + 2, :], ACT.Square).then_inc(sig("qk_squared"), 1)
                        act.wait_ge(sig("ssq_ready"), m + 1)
                        st.link(act.activation(rs[:, k, :], ssq[:, k, :], ACT.Ln, scale=LN_SHIFT))
                        act.activation(rs[:, k, :], rs[:, k, :], ACT.Exp, scale=-0.5, bias=shift_col[:, :])\
                           .then_inc(sig("rs_ready"), 1)
                        for j in range(2 * k, 2 * k + 2):
                            if j < 6:
                                values(j // 3, j % 3)
                        act.wait_ge(sig("qk_turned"), m + 1)
                        act.activation(qaT[:, :, cols(k)], ps[:, 6, :].rearrange("p (i n) -> p i n", i=4), ACT.Copy)\
                           .then_inc(sig("q_copied"), 1)
                    for k in range(NT):
                        a, T = 4 + 4 * l + k, k % 2
                        tile_exp(a, T, keys(T), cqs[:, k, :])
                        if k > 0:
                            tile_pt(a - 1, 1 - T)
                            tile_out(a - 1, oT)
                    tile_pt(a, T)
                    tile_out(a, oT)
                    layernorm(2 + l)
                    for c in range(3):
                        m = HC[c]
                        act.wait_ge(sig("f_g"), 3 * l + c + 1)
                        act.activation(PT[0:m, c, :], ps[0:m, 3 + c, :], ACT.Gelu, bias=b1[0:m, l, 1, c:c + 1])\
                           .then_inc(sig("f_gelu"), 1)

                layernorm(4)
                for m in range(4):
                    act.wait_ge(sig("qk1_mm"), 2 * m + 1)
                    act.activation(qaT[:, m, :], ps[:, m, :], ACT.Identity, bias=b1q[:, m:m + 1]).then_inc(sig("q1_copied"), 1)
                act.wait_ge(sig("v1_mm"), 1)
                act.activation(v1[:, :, :], ps[:, 4, :].rearrange("p (k n) -> p k n", k=NT), ACT.Copy).then_inc(sig("v1_copied"), 1)

                def probs(u):
                    return SAf[:, 2048 * (u % 2):2048 * (u % 2) + 2048].rearrange("p (e n) -> p e n", e=8)

                for u in range(2 * NT):
                    act.wait_ge(sig("l1_bias"), u + 1)
                    if u >= 2:
                        act.wait_ge(sig("l1_turned"), 4 * (u - 1))
                    for e in range(8):
                        ins = act.activation(probs(u)[:, e, :], ps[:, e // 2, L * (e % 2):L * (e % 2) + L], ACT.Exp,
                                             bias=nb[:, u, e:e + 1], scale=SCALE_1, accum_out=ls[:, u, e:e + 1])
                    ins.then_inc(sig("l1_exp"), 1)

                    def back(u):
                        for z in (0, 2):
                            act.wait_ge(sig("l1_turned"), 4 * u + z + 1)
                            act.activation(PT[:, z, :], ps[:, 4 + z % 3, :], ACT.Copy).then_inc(sig("l1_pt_act"), 1)
                    if u > 0:
                        back(u - 1)
                back(u)
                act.wait_ge(sig("att1_turned"), 1)
                act.activation(hT[:, :], ps[:, 0, :], ACT.Identity, bias=b1v[:, :]).then_inc(sig("att1_copied"), 1)

                layernorm(5)
                act.wait_ge(sig("route_mm"), 1)
                act.activation(rt[:, 0, :], ps[:, 7, 0:NT * E1], ACT.Exp, scale=-1.0).then_inc(sig("route_exp"), 1)
                act.wait_ge(sig("comb_turned"), 1)
                act.activation(combT[:, :], ps[0:E1, 7, :], ACT.Copy).then_inc(sig("comb_copied"), 1)
                for e in range(E1 + 1):
                    act.wait_ge(sig("e_gate"), e + 1)
                    if e >= 2:
                        act.wait_ge(sig("e_hidden"), e - 1)
                    act.activation(moe_g[:, e % 2, :], ps[:, e % 2, :], ACT.Silu).then_inc(sig("e_silu"), 1)
                act.wait_ge(sig("y_turned"), 1)
                act.activation(y_tok[:, :, :], ps[:, 7, :].rearrange("p (k n) -> p k n", k=NT), ACT.Copy).then_inc(sig("y_ready"), 1)
                pass_end(act, "act")

        @block.tensor
        def _(pe):
            mm = pe.matmul
            pe.wait_ge(sig("weights_loaded"), 16 * (len(loads) + len(rows)))
            for h in range(H):
                last = mm(ps[0:DQ, 1, DC * h:DC * h + DC], uqT[:, h, :], ukT[:, h, :], start=True, stop=True)
            last.then_inc(sig("absorb_mm"), 1)
            for h in range(H):
                last = mm(ps[0:DC, 2 + h // 4, D * (h % 4):D * (h % 4) + D], uvT[:, h, :], w_out0[:, h, :],
                          start=True, stop=True)
            last.then_inc(sig("absorb_mm"), 1)
            for h in range(H):
                q = DC * (h % 4)
                last = mm(ps[q:q + DC, 4, D * (h // 4):D * (h // 4) + D], uvT[:, h, :], w_out0[:, h, :],
                          start=True, stop=True)
            last.then_inc(sig("absorb_mm"), 1)
            pe.wait_ge(sig("c_act_ready"), 1)
            for j in range(12):
                last = mm(ps[:, 0, B * j:B * j + B], wmod[:, j // 6, D * (j % 6):D * (j % 6) + D], c_act[:, j // 6, :],
                          start=True, stop=True)
            last.then_inc(sig("mod_mm"), 1)
            pe.wait_ge(sig("setup_done"), 1)

            with pe.Fori(0, PASSES) as it:
                pe.wait_ge(sig("x_loaded"), 16)
                for k in range(NT):
                    last = pe.transpose(ps[:, 0, cols(k)], x_tok[:, k, :], ident[:, :])
                last.then_inc(sig("x_turned"), 1)

                def layernorm(n, src):
                    mm(ps[:, 0, :], mean_mat[:, :], src, start=True, stop=True).then_inc(sig("ln_mean"), 1)
                    pe.wait_ge(sig("ln_squared"), n + 1)
                    mm(ps[:, 1, :], mean_mat[:, :], sq, start=True, stop=True).then_inc(sig("ln_var"), 1)

                def tile_scores(a, T, kk):
                    b, k = (a % 4) // 2, a % 4
                    n = keys(T)
                    for bank, heads in SCORE_BANKS[T]:
                        for j, h in enumerate(heads):
                            r = slice(DH * (h % 2), DH * (h % 2) + DH)
                            last = mm(ps[:, bank, n * j:n * j + n], qaT[r, h // 2, cols(k)], kk(r, h, key_cols(b, T)),
                                      start=True, stop=True)
                    last.then_inc(sig("att_mm"), 1)

                def tile_pt(a, T, width):
                    for u, (h0, c) in enumerate(UNITS[T]):
                        first, n = (0, P) if c == 0 else (P, LW)
                        if u == 3:
                            pe.wait_ge(sig("pt_act"), pt_act(a) + 1)
                        for i in range(4):
                            last = pe.transpose(ps[0:n, 4 + u % 3, P * i:P * i + P],
                                                SA(T, width)[:, h0 + i, first:first + n], ident[:, :])
                        last.then_inc(sig("pt_mm"), 1)

                def pt_act(a):
                    return 6 * (a // 4) + UNITS_BEFORE[a % 4] // 2

                def tile_pv(a, T, m, lhs):
                    per = P // m
                    chunks = 1 + T
                    if a > 0:
                        pe.wait_ge(sig("o_copied"), a)
                    for h in range(H):
                        for c in range(chunks):
                            u = (h // 4) * chunks + c
                            who = "pt_act" if u % 2 == 0 else "pt_dve"
                            if h % 4 == 0:
                                pe.wait_ge(sig(who), pt_act(a) + u // 2 + 1)
                            n = P if c == 0 else LW
                            q = m * (h % per)
                            last = mm(ps[q:q + m, 7, P * (h // per):P * (h // per) + P], lhs(h, c),
                                      PT[0:n, u, P * (h % 4):P * (h % 4) + P], start=(c == 0), stop=(c == chunks - 1))
                    last.then_inc(sig("att_pv"), 1)

                pe.wait_ge(sig("xT_copied"), 1)
                layernorm(0, xT[:, :])
                pe.wait_ge(sig("ln_out"), 2)
                for w, bank, r in ((w_ki[:, :], 3, P), (w_qi[:, 0:P], 4, P), (w_qi[:, P:], 5, P), (w_dq[:, :], 2, DQ)):
                    mm(ps[0:r, bank, :], w, hT[:, :], start=True, stop=True).then_inc(sig("a_proj"), 1)
                n = DC + DR
                for k in range(NT):
                    mm(ps[:, 6, n * k:n * k + n], hT[:, cols(k)], w_kv[:, :], start=True, stop=True)
                for b in range(NB):
                    mm(ps[:, 6, n * NT + DC * b:n * NT + DC * b + DC], hT[:, L * b + LW:L * b + LW + P], w_kv[:, 0:DC],
                       start=True, stop=True)
                for b in range(NB):
                    c0 = n * NT + DC * NB + DC * b
                    last = mm(ps[0:LW, 6, c0:c0 + DC], hT[:, L * b + L - LW:L * b + L], w_kv[:, 0:DC], start=True, stop=True)
                last.then_inc(sig("kv_proj"), 1)
                pe.wait_ge(sig("a_copied"), 4)
                for k in range(NT):
                    b, T = k // 2, k % 2
                    n = LW if T == 0 else WMAX
                    if k >= 2:
                        pe.wait_ge(sig("irel"), 2 * k - 2)
                    for h in (0, 2, 1, 3):
                        r = slice(DH * (h % 2), DH * (h % 2) + DH)
                        last = mm(ps[:, 2 + 2 * (k % 2) + h % 2, n * (h // 2):n * (h // 2) + n], qiT[r, h // 2, cols(k)],
                                  kiT[r, L * b:L * b + n], start=True, stop=True)
                    last.then_inc(sig("iscore_mm"), 1)
                pe.wait_ge(sig("ka_ready"), 2)
                for k in range(NT):
                    last = pe.transpose(ps[:, 7, cols(k)], ka[:, k, :, :].rearrange("p s n -> p (s n)"), ident[:, :])
                last.then_inc(sig("kaT_turned"), 1)
                pe.wait_ge(sig("irel"), 2 * NT)
                for k in range(NT):
                    if k >= 2:
                        pe.wait_ge(sig("q_ready"), 3 * k - 3)
                        pe.wait_ge(sig("q_latent"), 2 * k - 2)
                    mm(ps[:, k % 2, 0:H * DC], cqT[:, cols(k)], w_q2[:, 0:H * DC], start=True, stop=True)
                    mm(ps[:, 5 + k % 2, 0:H * DR], cqT[:, cols(k)], w_q2[:, H * DC:], start=True, stop=True)\
                      .then_inc(sig("q2_mm"), 1)
                    pe.wait_ge(sig("q_ready"), 3 * k + 3)
                    pe.wait_ge(sig("q_latent"), 2 * k + 2)
                    if k > 0:
                        pe.wait_ge(sig("qa_copied"), k)
                        pe.wait_ge(sig("qb_copied"), 2 * k)
                    for i in range(4):
                        pe.transpose(ps[:, 2, P * i:P * i + P], qa[:, 2 * i:2 * i + 2, :].rearrange("p h n -> p (h n)"),
                                     ident[:, :])
                    for h in range(H):
                        last = pe.transpose(ps[0:GF, 3 + h // 4, P * (h % 4):P * (h % 4) + P], qb[:, h, :], ident[:, :])
                    last.then_inc(sig("q_turned"), 1)
                pe.wait_ge(sig("kv_split"), 5)
                pe.wait_ge(sig("qa_copied"), NT)
                pe.wait_ge(sig("qb_copied"), 2 * NT)
                for b in range(NB):
                    pe.wait_ge(sig("hot_ready"), 2 * b + 2)
                    for g in range(12):
                        if 12 * b + g >= 2:
                            pe.wait_ge(sig("gath_evac"), 12 * b + g - 1)
                        terms = [(kv_part[i][:, 2 * b, :], hot0[:, 512 * g:512 * g + 512]) for i in range(3)]
                        if g >= 8:
                            terms += [(kv_part[i][:, 2 * b + 1, :], hot1[:, 512 * (g - 8):512 * (g - 8) + 512])
                                      for i in range(3)]
                        for i, (l_, r_) in enumerate(terms):
                            last = mm(ps[0:GF, 2 + g % 2, :], l_, r_, start=(i == 0), stop=(i == len(terms) - 1))
                        last.then_inc(sig("gather_mm"), 1)
                    for n in range(3):
                        pe.wait_ge(sig("gath_evac"), 12 * b + 4 * n + 4)
                        if b > 0:
                            pe.wait_ge(sig("gsc_ready"), 3 * (b - 1) + n + 1)
                        for q in range(4):
                            for blk in range(4):
                                t = 64 * n + 16 * q + 4 * blk
                                last = mm(ps[32 * q:32 * q + 32, 5 + n, P * blk:P * blk + P],
                                          qbT[:, b, t:t + GP, :].rearrange("p t h -> p (t h)"),
                                          gath[:, RANKS * t:RANKS * t + P], start=True, stop=True)
                        last.then_inc(sig("gscore_mm"), 1)
                        if 3 * b + n >= 2:
                            pe.wait_ge(sig("gathT_ready"), 3 * b + n - 1)
                        for j in range(16):
                            c0 = P * (16 * n + j)
                            last = pe.transpose(ps[:, n % 2, DC * j:DC * j + DC], gath[0:DC, c0:c0 + P], ident[0:DC, 0:DC])
                        last.then_inc(sig("gathT_mm"), 1)
                pe.wait_ge(sig("gathT_ready"), 6)
                pe.wait_ge(sig("ka_copied"), 1)
                for b in range(NB):
                    for T in range(2):
                        a = 2 * b + T
                        if a > 0:
                            pe.wait_ge(sig("att_evac"), a)
                        if b > 0:
                            pe.wait_ge(sig("pdiag_ready"), 4 * b)
                            pe.wait_ge(sig("og_ready"), 3 * b)
                            pe.wait_ge(sig("x_updated"), b)
                        tile_scores(a, T, lambda r, h, c: kaT[r, c])
                    for T in range(2):
                        a = 2 * b + T
                        pe.wait_ge(sig("att_prob"), a + 1)
                        if a > 0:
                            pe.wait_ge(sig("att_pv"), a)
                        tile_pt(a, T, keys(T) + RANKS)
                        lat = {(0, 0): kvsrc[:, 2 * b, 0:DC], (1, 0): ckv_b[:, b, :], (1, 1): ckv_c[:, b, :]}
                        tile_pv(a, T, DC, lambda h, c: lat[T, c])
                    pe.wait_ge(sig("xg_loaded"), 192 * (b + 1))
                    pe.wait_ge(sig("att_evac"), 2 * b + 2)
                    for n in range(3):
                        last = pe.transpose(ps[:, 0, P * n:P * n + P], xg[:, n, :], ident[:, :])
                    last.then_inc(sig("xg_turned"), 1)
                    pe.wait_ge(sig("pdiag_ready"), 4 * b + 4)
                    for n in range(3):
                        for j in range(16 * n, 16 * n + 16):
                            c0 = RANKS * (j - 16 * n)
                            last = mm(ps[0:DC, 1 + n, c0:c0 + GP * H], gathT[:, b, j, :],
                                      pdiag[:, j, :, :].rearrange("p t h -> p (t h)"), start=True, stop=True)
                        last.then_inc(sig("og_mm"), 1)
                    pe.wait_ge(sig("o_copied"), 2 * b + 2)
                    pe.wait_ge(sig("og_ready"), 3 * b + 3)
                    for i in range(2):
                        last = mm(ps[:, 4, 0:L], w_vo4[:, i, :], oTa[:, i, bcols(b)], start=(i == 0), stop=(i == 1))
                    last.then_inc(sig("a_out"), 1)
                    for h in range(H):
                        last = mm(ps[:, 5, 0:GT], w_vo[:, h, :], og[:, :, h], start=(h == 0), stop=(h == H - 1))
                    last.then_inc(sig("a_out"), 1)

                pe.wait_ge(sig("x_updated"), 2)
                layernorm(1, xT[:, :])
                for l in range(2):
                    pe.wait_ge(sig("shifted"), 4 * l + 2)

                    def values(b, c):
                        n = 6 * l + 3 * b + c
                        if n > 0:
                            pe.wait_ge(sig("v_copied"), n)
                        first, m = ((0, P), (LW, P), (L - LW, LW))[c]
                        mm(ps[0:m, 4 + c % 2, :], sh[:, b, first:first + m], wqkv[:, l, 1024:], start=True, stop=True)\
                          .then_inc(sig("v_mm"), 1)

                    for k in range(NT):
                        m = NT * l + k
                        if k >= 2:
                            pe.wait_ge(sig("qk_ready"), m - 1)
                            pe.wait_ge(sig("qk_squared"), m - 1)
                        x = sh[:, k // 2, P * (k % 2):P * (k % 2) + P]
                        bank = 2 * (k % 2)
                        mm(ps[:, bank, :], x, wqkv[:, l, 0:512], start=True, stop=True)
                        mm(ps[:, bank + 1, :], x, wqkv[:, l, 512:1024], start=True, stop=True).then_inc(sig("qk_mm"), 1)
                        for j in range(2 * k, 2 * k + 2):
                            if j < 6:
                                values(j // 3, j % 3)
                        pe.wait_ge(sig("qk_ready"), m + 1)
                        if m > 0:
                            pe.wait_ge(sig("q_copied"), m)
                            pe.wait_ge(sig("k_copied"), m)
                        for i in range(4):
                            pe.transpose(ps[:, 6, P * i:P * i + P], big[:, P * i:P * i + P], ident[:, :])
                        for i in range(4):
                            last = pe.transpose(ps[:, 7, P * i:P * i + P], big[:, 512 + P * i:512 + P * i + P], ident[:, :])
                        last.then_inc(sig("qk_turned"), 1)
                    pe.wait_ge(sig("q_copied"), NT * (l + 1))
                    pe.wait_ge(sig("k_copied"), NT * (l + 1))
                    pe.wait_ge(sig("v_copied"), 6 * (l + 1))

                    def back(a, T):
                        pe.wait_ge(sig("att_prob"), a + 1)
                        pe.wait_ge(sig("att_pv"), a)
                        tile_pt(a, T, keys(T))
                        b = (a % 4) // 2
                        tile_pv(a, T, DH, lambda h, c: vt[0:(P if c == 0 else LW), b, T + c, DH * h:DH * h + DH])

                    for k in range(NT):
                        a, T = 4 + 4 * l + k, k % 2
                        if k > 0:
                            pe.wait_ge(sig("att_evac"), a)
                        tile_scores(a, T, lambda r, h, c: kT[r, h // 2, c])
                        if k > 0:
                            back(a - 1, 1 - T)
                    back(a, T)
                    pe.wait_ge(sig("o_copied"), a + 1)
                    for i in range(4):
                        last = mm(ps[:, 0, :], wo[:, l, i, :], oT[:, i, :], start=(i == 0), stop=(i == 3))
                    last.then_inc(sig("f_o"), 1)
                    pe.wait_ge(sig("shifted"), 4 * l + 4)
                    layernorm(2 + l, sh[:, :, :].rearrange("p b t -> p (b t)"))
                    pe.wait_ge(sig("ln_out"), 5 + l)
                    for c in range(3):
                        m, c0 = HC[c], P * c
                        mm(ps[0:m, 3 + c, :], w1[:, l, HID + c0:HID + c0 + m], hT[:, :], start=True, stop=True)\
                          .then_inc(sig("f_g"), 1)
                        mm(ps[0:m, c, :], w1[:, l, c0:c0 + m], hT[:, :], start=True, stop=True).then_inc(sig("f_a"), 1)
                    for c in range(3):
                        m = HC[c]
                        pe.wait_ge(sig("f_hidden"), 3 * l + c + 1)
                        last = mm(ps[:, 6, :], w2[0:m, l, c, :], hh[0:m, c, :], start=(c == 0), stop=(c == 2))
                    last.then_inc(sig("f_down"), 1)

                pe.wait_ge(sig("x_updated"), 4)
                layernorm(4, xT[:, :])
                pe.wait_ge(sig("ln_out"), 8)
                for m in range(4):
                    mm(ps[:, m, :], w1q[:, m, :], hT[:, :], start=True, stop=True).then_inc(sig("qk1_mm"), 1)
                    mm(ps[:, 4 + m, :], w1k[:, m, :], hT[:, :], start=True, stop=True).then_inc(sig("qk1_mm"), 1)
                pe.wait_ge(sig("k1_copied"), 4)
                pe.wait_ge(sig("q1_copied"), 4)
                for k in range(NT):
                    last = mm(ps[:, 4, cols(k)], hT[:, cols(k)], w1v[:, :], start=True, stop=True)
                last.then_inc(sig("v1_mm"), 1)

                def probs(u):
                    return SAf[:, 2048 * (u % 2):2048 * (u % 2) + 2048].rearrange("p (e n) -> p e n", e=8)

                def back1(u):
                    k, half = u // 2, u % 2
                    b = k // 2
                    for z in range(4):
                        if z < 3 and u > 0:
                            pe.wait_ge(sig("l1_pt_act"), 2 * u)
                            pe.wait_ge(sig("l1_pt_dve"), 2 * u)
                            pe.wait_ge(sig("l1_pv"), u)
                        if z == 3:
                            pe.wait_ge(sig("l1_pt_act"), 2 * u + 1)
                        for i in range(4):
                            e, c = 2 * z + i // 2, i % 2
                            last = pe.transpose(ps[:, 4 + z % 3, P * i:P * i + P], probs(u)[:, e, P * c:P * c + P], ident[:, :])
                        last.then_inc(sig("l1_turned"), 1)
                    if u > 0:
                        pe.wait_ge(sig("att1_ready"), u)
                    for z in range(4):
                        pe.wait_ge(sig("l1_pt_act" if z % 2 == 0 else "l1_pt_dve"), 2 * u + z // 2 + 1)
                        for i in range(4):
                            e, c = 2 * z + i // 2, i % 2
                            head = 8 * half + 4 * (e % 2) + e // 2
                            last = mm(ps[:, 7, P * k + D1 * head:P * k + D1 * head + D1], PT[:, z, P * i:P * i + P],
                                      v1[:, 2 * b + c, D1 * head:D1 * head + D1], start=(c == 0), stop=(c == 1))
                    last.then_inc(sig("l1_pv"), 1)

                pe.wait_ge(sig("v1_copied"), 1)
                for u in range(2 * NT):
                    k, half = u // 2, u % 2
                    if u > 0:
                        pe.wait_ge(sig("l1_exp"), u)
                    for g in range(4):
                        for j in range(2):
                            m = 2 * half + j
                            r = slice(32 * g, 32 * g + D1)
                            last = mm(ps[:, g, L * j:L * j + L], qaT[r, m, cols(k)], kT[r, m, bcols(k // 2)],
                                      start=True, stop=True)
                    last.then_inc(sig("l1_mm"), 1)
                    if u > 0:
                        back1(u - 1)
                pe.wait_ge(sig("l1_exp"), u + 1)
                back1(u)
                pe.wait_ge(sig("att1_ready"), 2 * NT)
                for k in range(NT):
                    last = pe.transpose(ps[:, 0, cols(k)], att1[:, k, :], ident[:, :])
                last.then_inc(sig("att1_turned"), 1)
                pe.wait_ge(sig("att1_copied"), 1)
                mm(ps[:, 1, :], w1o[:, :], hT[:, :], start=True, stop=True).then_inc(sig("l1_out"), 1)

                pe.wait_ge(sig("x_updated"), 6)
                layernorm(5, xT[:, :])
                pe.wait_ge(sig("ln_out"), 10)
                for k in range(NT):
                    last = mm(ps[:, 7, E1 * k:E1 * k + E1], hT[:, cols(k)], gate_w[:, :], start=True, stop=True)
                last.then_inc(sig("route_mm"), 1)

                def expert_in(e):
                    s = e % 2
                    if e >= 2:
                        pe.wait_ge(sig("e_silu"), e - 1)
                    mm(ps[:, s, :], experts[:, 0, e, :], hT[:, :], start=True, stop=True).then_inc(sig("e_gate"), 1)
                    if e >= 2:
                        pe.wait_ge(sig("e_hidden"), e - 1)
                    mm(ps[:, 2 + s, :], experts[:, 1, e, :], hT[:, :], start=True, stop=True).then_inc(sig("e_up"), 1)

                def expert_weight(e):
                    if e < E1:
                        mm(ps[:, 4 + e % 2, :], bc(ident[0:E1, e], 1, P), combT[:, :], start=True, stop=True)\
                          .then_inc(sig("e_comb"), 1)

                pe.wait_ge(sig("experts_loaded"), 48)
                expert_in(0)
                expert_in(1)
                pe.wait_ge(sig("comb_ready"), 1)
                for k in range(NT):
                    last = pe.transpose(ps[0:E1, 7, cols(k)], rt[:, 6, E1 * k:E1 * k + E1], ident[:, :])
                last.then_inc(sig("comb_turned"), 1)
                pe.wait_ge(sig("comb_copied"), 1)
                expert_weight(0)
                expert_weight(1)
                for e in range(E1 + 1):
                    pe.wait_ge(sig("e_hidden"), e + 1)
                    mm(ps[:, 6, :], experts[:, 2, e, :], moe_h[:, e % 2, :], start=(e == 0), stop=(e == E1))\
                      .then_inc(sig("e_down"), 1)
                    if e + 2 <= E1:
                        expert_in(e + 2)
                        expert_weight(e + 2)
                pe.wait_ge(sig("x_updated"), 8)
                for k in range(NT):
                    last = pe.transpose(ps[:, 7, cols(k)], xT[:, cols(k)], ident[:, :])
                last.then_inc(sig("y_turned"), 1)
                pass_end(pe, "pe")

        @block.gpsimd
        def _(pool):
            pool.wait_ge(sig("setup_done"), 1)
            with pool.Fori(0, PASSES) as it:
                pool.memset(pdiag[:, :, :, :], 0.0).then_inc(sig("pdiag_zero"), 1)
                pool.wait_ge(sig("kvsrc_ready"), 1)
                hi, mid, lo = kv_part
                pool.tensor_copy(hi[:, :, :], kvsrc[:, :, :]).then_inc(sig("kv_split"), 1)
                pool.wait_ge(sig("kv_split"), 1)
                pool.tensor_tensor(kv_rem[:, 0, :, :], kvsrc[:, :, :], hi[:, :, :], ALU.subtract).then_inc(sig("kv_split"), 1)
                pool.wait_ge(sig("kv_split"), 2)
                pool.tensor_copy(mid[:, :, :], kv_rem[:, 0, :, :]).then_inc(sig("kv_split"), 1)
                pool.wait_ge(sig("kv_split"), 3)
                pool.tensor_tensor(kv_rem[:, 1, :, :], kv_rem[:, 0, :, :], mid[:, :, :], ALU.subtract)\
                    .then_inc(sig("kv_split"), 1)
                pool.wait_ge(sig("kv_split"), 4)
                pool.tensor_copy(lo[:, :, :], kv_rem[:, 1, :, :]).then_inc(sig("kv_split"), 1)
                pool.drain().then_inc(done, 1)
                pool.wait_ge(done, 5)
                pool.sem_clear(done)
                for name in sorted(sems):
                    if name not in SETUP:
                        pool.sem_clear(sems[name])
                for name in sorted(go):
                    pool.sem_inc(go[name], 1)


def lay_out(a):
    f = np.float32
    n = {k: np.asarray(v) for k, v in a.items()}
    o = dict(shape_constants())
    o["x"] = n["L0_attn_x"]
    o["cT"] = np.stack([n["L0_c"].T, n["L1_c"].T], 1)
    o["wmod"] = np.stack([n["L0_wmod"], n["L1_wmod"]], 1)
    o["w_kv"] = np.concatenate([n["L0_attn_W_dkv"], n["L0_attn_W_kr"]], 1)
    o["w_ki"] = np.concatenate([n["L0_attn_idx_wk"]] * 2, 1)
    o["w_qi"] = n["L0_attn_idx_wq"]
    o["w_dq"] = n["L0_attn_W_dq"]
    o["uqT"] = n["L0_attn_W_uq"].reshape(DQ, H, DH).transpose(2, 1, 0)
    o["ukT"] = n["L0_attn_W_uk"].reshape(DC, H, DH).transpose(2, 1, 0)
    o["uvT"] = n["L0_attn_W_uv"].reshape(DC, H, DH).transpose(2, 1, 0)
    o["w_out0"] = n["L0_attn_W_out"].reshape(H, DH, D).transpose(1, 0, 2)
    o["w_q2"] = np.concatenate([n["L0_attn_W_qr"], n["L0_attn_W_qr"]], 1)
    o["idx_w"] = n["L0_attn_idx_w"].reshape(1, IH)
    o["raw_delta"] = n["L0_attn_raw_delta"].reshape(1, DR // 2)
    o["delta_col"] = np.tile(n["L0_attn_raw_delta"], GF // (DR // 2)).reshape(GF, 1)
    qs, ks = n["L0_ffn_q_scale"], n["L0_ffn_k_scale"]
    roll = lambda s: np.roll(s, DH // 2, 1)
    o["qk_scale"] = np.concatenate([qs, ks, roll(qs), roll(ks)], 1).reshape(1, 2 * 4 * DH)
    o["wqkv"] = n["L0_ffn_wqkv"].transpose(1, 0, 2)
    o["wo"] = n["L0_ffn_wo"].reshape(2, 4, P, D).transpose(2, 0, 1, 3)
    o["ln_gb"] = np.stack([n["L0_ffn_ln_g"], n["L0_ffn_ln_b"]], 1).transpose(2, 0, 1)
    o["w1"] = n["L0_ffn_w1"].transpose(1, 0, 2)
    pad = np.zeros((2, 2, 3 * P), f)
    pad[:, :, :HID] = n["L0_ffn_b1"].reshape(2, 2, HID)
    o["b1"] = pad.reshape(2, 2, 3, P).transpose(3, 0, 1, 2)
    pad = np.zeros((2, 3 * P, D), f)
    pad[:, :HID] = n["L0_ffn_w2"]
    o["w2"] = pad.reshape(2, 3, P, D).transpose(2, 0, 1, 3)
    o["b2"] = n["L0_ffn_b2"].T
    w = n["L1_attn_W_qkv"].reshape(H1, 3, D1, D)
    bias = n["L1_attn_b_qkv"].reshape(H1, 3, D1)
    for i, name in ((0, "q"), (1, "k")):
        pad = np.zeros((D, 4, 4, 32), f)
        pad[:, :, :, :D1] = w[:, i].reshape(4, 4, D1, D).transpose(3, 0, 1, 2)
        o["w1" + name] = pad.reshape(D, 4, P)
        pad = np.zeros((4, 4, 32), f)
        pad[:, :, :D1] = bias[:, i].reshape(4, 4, D1)
        o["b1" + name] = pad.reshape(4, P).T
    o["w1v"] = w[:, 2].reshape(D, D).T
    o["b1v"] = bias[:, 2].reshape(D, 1)
    o["w1o"] = n["L1_attn_W_out"].T
    o["b1o"] = n["L1_attn_b_out"].reshape(D, 1)
    o["gate_w"] = n["L1_ffn_gate_w"].T
    o["e_bias"] = n["L1_ffn_expert_bias"].reshape(1, E1)
    both = [np.concatenate([n["L1_ffn_w_" + name], n[f"L1_ffn_shared_{name}_w"][None]], 0)
            for name in ("gate", "up", "down")]
    o["experts"] = np.stack(both, 0).transpose(3, 0, 1, 2)
    return {k: np.ascontiguousarray(v) for k, v in o.items()}


def kernel(**inputs):
    import concourse.bacc as bacc
    from concourse.bass_utils import run_bass_kernel_spmd

    nc = bacc.Bacc("TRN2", target_bir_lowering=False, num_devices=1)
    arrays = lay_out(inputs)
    A = {k: nc.dram_tensor("in_" + k, v.shape, mybir.dt.from_np(v.dtype), kind="ExternalInput").ap()
         for k, v in arrays.items()}
    out = nc.dram_tensor("out_x", (B, L, D), F32, kind="ExternalOutput").ap()
    idx = nc.dram_tensor("idx_scratch", (NB, GT * RANKS), BF16, kind="Internal").ap()
    scores = nc.dram_tensor("score_scratch", (NB, 3, P * 512), F32, kind="Internal").ap()
    program(nc, A, out, idx, scores)
    r = run_bass_kernel_spmd(nc, [{"in_" + k: v for k, v in arrays.items()}], core_ids=[0])
    return r.results[0]["out_x"]
```

```python
import math
from contextlib import ExitStack

import numpy as np

import concourse.bass as bass
from concourse import mybir

F32 = mybir.dt.float32
BF16 = mybir.dt.bfloat16
U32 = mybir.dt.uint32
ALU = mybir.AluOpType
ACT = mybir.ActivationFunctionType
AX = mybir.AxisListType

P = 128
B, L, D = 8, 256, 128
NB = 2
PASSES = B // NB
NT = NB * L // P
W = NB * L
H, DH, DR, DC, DQ = 8, 64, 32, 32, 64
IH = 4
LW, RANKS = 64, 32
GT = L - LW
GP = 4
NG = GT // GP
GF = DC + 2 * DR
WIN = 64
HID = 341
SETUP = ("weights_loaded", "cols_set", "setup_exp", "c_act_ready", "delta_ready", "delta_sin", "mod_mm", "absorb_mm",
         "setup_done", "dve_setup_step", "act_setup_step")
HC = [128, 128, 85]
E1, TOPK = 16, 8
H1, D1 = 16, 8
WMAX = 192
EXCLUDED, FORWARD, TAKEN = -3.0e38, -1.0e30, -3.4e38
MASKED = -1.0e30
SCALE_A = float(DH + DR) ** -0.5
SCALE_1 = 1.0 / math.sqrt(D1)
ROUTE = 2.826
LN_AND_EXP = "natural_log_exp_and_others"
LN_SHIFT = 65536.0


def shape_constants():
    f = np.float32
    c = {}
    c["ident"] = np.eye(P, dtype=f)
    theta = (1.0 / np.float32(10000.0) ** (2.0 * np.arange(DR // 2, dtype=f) / DR)).astype(f)
    pos = np.arange(L)
    turned = np.where(pos < LW, pos, 2 * pos - (LW - 1))
    ang = np.stack([turned, pos, pos]).astype(f)[:, :, None] * theta
    ang = ang.reshape(3, 2, P, DR // 2).transpose(2, 0, 1, 3).reshape(P, 6, DR // 2).astype(np.float64)
    c["rope_cos"], c["rope_sin"] = np.cos(ang).astype(f), np.sin(ang).astype(f)
    rank = np.arange(LW, LW + RANKS).astype(f)[None, :] * np.tile(theta, 2)[:, None]
    rank = rank.astype(np.float64)
    one = np.ones((DC, RANKS))
    c["rank_a"] = np.concatenate([one, np.cos(rank), np.sin(rank)]).astype(f)
    c["rank_b"] = np.concatenate([one, -np.sin(rank), np.cos(rank)]).astype(f)
    half = np.arange(0, DH, 2, dtype=f)
    inv = (1.0 / np.float32(10000.0) ** (half / DH)).astype(f)
    fr = (np.arange(L, dtype=f)[:, None] * inv[None, :]).astype(np.float64)
    fr = np.concatenate([fr, fr], 1)
    base = ((half + 0.4 * DH) / (1.4 * DH)).astype(np.float64)
    power = (np.arange(L) - L // 2) / float(WIN // 2)
    sc = base[None, :] ** power[:, None]
    sc = np.concatenate([sc, sc], 1)
    sign = np.concatenate([-np.ones(DH // 2), np.ones(DH // 2)])
    x = np.stack([np.cos(fr) * sc, np.cos(fr) / sc, np.sin(fr) * sc * sign, np.sin(fr) / sc * sign], 1)
    c["xpos"] = x.reshape(2, P, 4 * DH).transpose(1, 0, 2).astype(f)
    i = np.arange(P)[:, None]
    j0, j1 = np.arange(P)[None, :], LW + np.arange(WMAX)[None, :]
    ok0 = np.where(i < LW, j0 < LW + RANKS, (j0 <= i) & (j0 > i - LW))
    ok1 = (j1 <= i + P) & (j1 > i + P - LW)
    c["mask_a"] = np.where(np.concatenate([ok0, ok1], 1), 0, MASKED).astype(f)
    ok0 = (j0 <= i) & (j0 >= i - WIN)
    ok1 = (j1 <= i + P) & (j1 >= i + P - WIN)
    c["mask_w"] = np.where(np.concatenate([ok0, ok1], 1), 0, MASKED).astype(f)
    s0, s1 = np.arange(LW + RANKS)[None, :], np.arange(WMAX)[None, :]
    m0 = np.where(s0 < LW, np.where(s0 <= i - LW, 0, EXCLUDED), np.where(s0 > i, FORWARD, EXCLUDED))
    m0[:LW] = 0
    m1 = np.where(s1 <= i + P - LW, 0, EXCLUDED)
    c["mask_i"] = np.concatenate([m0, m1], 1).astype(f)
    head = (np.arange(P)[:, None] // D1 == np.arange(H1)[None, :]).astype(f)
    c["own_head"], c["head_rows"] = head, head.T
    c["source"] = (np.arange(P)[:, None] + np.array([[0, P]])).astype(f)
    return c


class Steps:

    def __init__(self, eng, sem):
        self.eng, self.sem, self.n = eng, sem, 0

    def mark(self, ins):
        ins.then_inc(self.sem, 1)
        self.n += 1
        return self.n

    def wait(self, n=None):
        self.eng.wait_ge(self.sem, self.n if n is None else n)

    def link(self, ins):
        self.mark(ins)
        self.wait()


def program(nc, A, out, idx_scratch, score_scratch):
    ctx = ExitStack()
    with ctx:
        def sb(name, shape, dt=F32):
            return ctx.enter_context(nc.sbuf_tensor(name, shape, dt))

        done = ctx.enter_context(nc.semaphore("pass_done"))
        go = {n: ctx.enter_context(nc.semaphore("go_" + n)) for n in ("sp", "act", "dve", "pe")}
        sems = {}

        def sig(name):
            if name not in sems:
                sems[name] = ctx.enter_context(nc.semaphore(name))
            return sems[name]

        SAf = sb("SAf", [P, 4096])
        loads = []

        def weight(name, shape, src=None):
            t = sb("w_" + name, shape)
            loads.append((t[tuple(slice(None) for _ in shape)], A[name] if src is None else src))
            return t

        ident = weight("ident", [P, P])
        rank_a = weight("rank_a", [GF, RANKS])
        rank_b = weight("rank_b", [GF, RANKS])
        mask_a = weight("mask_a", [P, P + WMAX])
        mask_w = weight("mask_w", [P, P + WMAX])
        mask_i = weight("mask_i", [P, LW + RANKS + WMAX])
        source = weight("source", [P, 2])
        cT = weight("cT", [P, 2, B])
        w_kv = weight("w_kv", [D, DC + DR])
        w_ki = weight("w_ki", [D, 2 * DH])
        w_qi = weight("w_qi", [D, IH * DH])
        w_dq = weight("w_dq", [D, DQ])
        w_q2 = weight("w_q2", [DQ, H * DC + H * DR])
        idx_w = sb("idx_w", [P, IH])
        delta_row = sb("delta_row", [P, DR // 2])
        delta_col = weight("delta_col", [GF, 1])
        wqkv = weight("wqkv", [P, 2, 3 * H * DH])
        wo = weight("wo", [P, 2, 4, D])
        ln_gb = weight("ln_gb", [P, 2, 2])
        w1 = weight("w1", [P, 2, 2 * HID])
        b1 = weight("b1", [P, 2, 2, 3])
        w2 = weight("w2", [P, 2, 3, D])
        b2 = weight("b2", [P, 2])
        w1q = weight("w1q", [P, P])
        w1k = weight("w1k", [P, P])
        b1q = weight("b1q", [P, 1])
        b1k = weight("b1k", [P, 1])
        own_head = weight("own_head", [P, H1])
        head_rows = weight("head_rows", [H1, P])
        w1v = weight("w1v", [P, D])
        b1v = weight("b1v", [P, 1])
        w1o = weight("w1o", [P, D])
        b1o = weight("b1o", [P, 1])
        gate_w = weight("gate_w", [P, E1])
        e_bias = sb("e_bias", [P, E1])
        region = sb("region", [P, 3 * (E1 + 1) * P])
        experts = region[:, :].rearrange("p (s e n) -> p s e n", s=3, e=E1 + 1)
        parts = np.cumsum([0, NB * NG * DC, NG * GP * H, 3 * 512, 3 * P]).tolist()
        gathT = region[:, parts[0]:parts[1]].rearrange("p (b g c) -> p b g c", b=NB, g=NG)
        pdiag = region[:, parts[1]:parts[2]].rearrange("p (g t h) -> p g t h", g=NG, t=GP)
        gsc = region[:, parts[2]:parts[3]].rearrange("p (i n) -> p i n", i=3)
        xg = region[:, parts[3]:parts[4]].rearrange("p (i n) -> p i n", i=3)
        big = sb("big", [P, 2048])
        wmod = SAf[:, 0:12 * D].rearrange("p (l n) -> p l n", l=2)
        uqT = SAf[0:DH, 1536:2048].rearrange("p (h n) -> p h n", h=H)
        ukT = SAf[0:DH, 2048:2304].rearrange("p (h n) -> p h n", h=H)
        uvT = SAf[0:DH, 2304:2560].rearrange("p (h n) -> p h n", h=H)
        w_out0 = SAf[0:DH, 2560:3584].rearrange("p (h n) -> p h n", h=H)
        xpos = SAf[:, 3584:4096].rearrange("p (t n) -> p t n", t=2)
        qk_scale = big[:, 0:512].rearrange("p (l n) -> p l n", l=2)
        rope_cos = big[:, 512:608].rearrange("p (i n) -> p i n", i=6)
        rope_sin = big[:, 608:704].rearrange("p (i n) -> p i n", i=6)
        rope_t = big[:, 704:896].rearrange("p (s i n) -> p s i n", s=2, i=6)
        for name, t in (("xpos", xpos), ("rope_cos", rope_cos), ("rope_sin", rope_sin), ("wmod", wmod), ("uqT", uqT), ("ukT", ukT), ("uvT", uvT), ("w_out0", w_out0)):
            loads.append((t, A[name]))
        rows = [(idx_w, A["idx_w"]), (delta_row, A["raw_delta"]), (qk_scale, A["qk_scale"]), (e_bias, A["e_bias"])]

        b1out = sb("b1out", [P, 1])
        mean_mat = sb("mean_mat", [P, P])
        eps_col = sb("eps_col", [P, 1])
        one_col = sb("one_col", [P, 1])
        shift_col = sb("shift_col", [P, 1])
        modT = sb("modT", [P, 12, B])
        c_act = sb("c_act", [P, 2, B])
        c_den = sb("c_den", [P, 2, B])
        mod_tmp = sb("mod_tmp", [P, 2, B])
        ang = sb("ang", [P, 8, DR // 2])
        ropeC = sb("ropeC", [P, 6, DR])
        ropeS = sb("ropeS", [P, 6, DR])
        dcol = sb("dcol", [GF, 8])
        rank_tab = sb("rank_tab", [GF, RANKS])
        rank_t = sb("rank_t", [GF, RANKS])
        xtab = sb("xtab", [P, 2, 2, 4 * DH])
        w_vo = sb("w_vo", [DC, H, D])
        w_vo4 = sb("w_vo4", [P, 2, D])

        x_tok = sb("x_tok", [P, NT, D])
        y_tok = big[:, 0:W].rearrange("p (k n) -> p k n", k=NT)
        xT = sb("xT", [P, W])
        fT = sb("fT", [P, W])
        hT = sb("hT", [P, W])
        sh = sb("sh", [P, NB, L])
        mod = sb("mod", [P, 12, NB])
        cqT = sb("cqT", [DQ, W])
        kvsrc = sb("kvsrc", [P, NT, GF])
        ckv_b = sb("ckv_b", [P, NB, DC])
        ckv_c = sb("ckv_c", [LW, NB, DC])
        kr_abs = sb("kr_abs", [P, NT, DR])
        kr_raw = sb("kr_raw", [P, NT, DR])
        ka = sb("ka", [P, NT, 2, DC + DR])
        kaT = sb("kaT", [P, W])
        kv_part = [sb(n, [P, NT, GF], BF16) for n in ("kv_hi", "kv_mid", "kv_lo")]
        kv_rem = SAf[:, 0:2 * NT * GF].rearrange("p (s k n) -> p s k n", s=2, k=NT)
        xc, sq, rstd = big[:, 0:W], big[:, W:2 * W], big[:, 2 * W:3 * W]
        irel = big[:, 0:2 * IH * WMAX].rearrange("p (s h n) -> p s h n", s=2, h=IH)
        qa = sb("qa", [P, H, DC + DR])
        qb = sb("qb", [P, H, GF])
        queries = sb("queries", [P, 4 * W + NB * GT * H])
        qaT = queries[:, 0:4 * W].rearrange("p (i n) -> p i n", i=4)
        qbT = queries[0:GF, 4 * W:].rearrange("p (b t h) -> p b t h", b=NB, h=H)
        q_half = queries[:, 0:H * W].rearrange("p (i s n) -> p i s n", i=4, s=2)
        iscore = sb("iscore", [P, NB, LW + RANKS + WMAX])
        top8 = sb("top8", [P, NT, RANKS])
        topi = sb("topi", [P, NT, RANKS], U32)
        topb = sb("topb", [P, NT, RANKS], BF16)
        kto = sb("kto", [P, 4096])
        q_abs, q_mu, q_c, q_s = (kto[:, 256 * i:256 * i + 256] for i in range(4))
        hot0 = kto[:, 0:3072].bitcast(BF16)
        oTa = kto[:, 3072:4096].rearrange("p (i n) -> p i n", i=2)
        kT = kto[:, 0:2048].rearrange("p (i n) -> p i n", i=4)
        k1T, q1T = kto[:, 0:W], kto[:, W:2 * W]
        q_own = kto[:, 2 * W:6 * W].rearrange("p (s h n) -> p s h n", s=4, h=4)
        oT = kto[:, 2048:4096].rearrange("p (i n) -> p i n", i=4)
        hot1 = big[:, 0:LW * RANKS // 2].bitcast(BF16)
        wide = sb("wide", [P, GT * RANKS])
        gath = wide[0:GF, :]
        idxb = wide[:, 3072:6144].bitcast(BF16)
        og = wide[0:DC, 0:GT * H].rearrange("p (t h) -> p t h", h=H)
        qiT = wide[:, 0:1024].rearrange("p (i n) -> p i n", i=2)
        kiT = wide[:, 1024:1536]
        vt = wide[:, 0:3072].rearrange("p (b c n) -> p b c n", b=NB, c=3)
        hh = wide[:, 3072:4608].rearrange("p (c n) -> p c n", c=3)
        qk_ring = [big[:, 0:1024], wide[:, 5120:6144]]
        v_own = wide[:, 0:NT * H1 * 32].rearrange("p (k g j n) -> p k g j n", k=NT, g=4, j=4)
        moe_g = wide[:, 2048:3072].rearrange("p (s n) -> p s n", s=2)
        moe_h = wide[:, 3072:4096].rearrange("p (s n) -> p s n", s=2)
        PT = sb("PT", [P, 4, 512])
        mx = sb("mx", [P, 16, H])
        nb = sb("nb", [P, 16, H])
        ls = sb("ls", [P, 16, H])
        rl = sb("rl", [P, 16, H])
        ssq = sb("ssq", [P, NT, 2 * H])
        rs = sb("rs", [P, NT, 2 * H])
        cqs = sb("cqs", [P, NT, H])
        rt = sb("rt", [P, 8, NT * E1])
        rsm = sb("rsm", [P, 4 * NT + 8 * NT])
        combT = sb("combT", [E1, W])
        ps = ctx.enter_context(nc.psum_tensor("ps", [P, 8, 512], F32))

        def pass_end(eng, name):
            eng.drain().then_inc(done, 1)
            eng.wait_ge(go[name], 1)
            eng.sem_clear(go[name])

        def cols(k):
            return slice(P * k, P * k + P)

        def bcols(b):
            return slice(L * b, L * b + L)

        def keys(T):
            return P if T == 0 else WMAX

        def key_cols(b, T):
            return slice(L * b, L * b + P) if T == 0 else slice(L * b + LW, L * b + L)

        def SA(T, width):
            return SAf[:, 2048 * T:2048 * T + H * width].rearrange("p (h n) -> p h n", h=H)

        def bc(ap, axis, n):
            v = ap.unsqueeze(axis)
            shape = list(v.shape)
            shape[axis] = n
            return v.broadcast_to(shape)

        ls1, rl1 = (t[:, 0:8, :].rearrange("p u h -> p (u h)") for t in (ls, rl))

        def probs1(u):
            return SAf[:, 1024 * (u % 4):1024 * (u % 4) + 1024].rearrange("p (e n) -> p e n", e=4)

        def turned_copy1(eng, u, which, done_):
            z = 2 * u + which
            eng.wait_ge(sig("l1_turned"), z + 1)
            if u >= 2:
                eng.wait_ge(sig("l1_pv"), u - 1)
            if which == 0:
                ins = eng.activation(PT[:, z % 4, :], ps[:, 4 + z % 3, :], ACT.Copy)
            else:
                ins = eng.tensor_copy(PT[:, z % 4, :], ps[:, 4 + z % 3, :])
            ins.then_inc(sig(done_), 1)

        SCORE_BANKS = {0: [(0, (0, 2, 4, 6)), (1, (1, 3, 5, 7))],
                       1: [(0, (0, 2)), (1, (1, 3)), (2, (4, 6)), (3, (5, 7))]}
        SCORE_BANKS_2 = {0: [(0, (0, 1, 2, 3)), (1, (4, 5, 6, 7))],
                         1: [(i, (2 * i, 2 * i + 1)) for i in range(4)]}
        UNITS = {0: [(0, 0), (4, 0)], 1: [(0, 0), (0, 1), (4, 0), (4, 1)]}
        UNITS_BEFORE = [0, 2, 6, 8]

        block = ctx.enter_context(nc.Block())

        @block.sync
        def _(sp):
            for dst, src in loads:
                sp.dma_start(dst, src).then_inc(sig("weights_loaded"), 16)
            for dst, src in rows:
                n = dst.shape[-1] if len(dst.shape) == 2 else dst.shape[1] * dst.shape[2]
                flat = dst[:, :] if len(dst.shape) == 2 else dst[:, :, :].rearrange("p a n -> p (a n)")
                sp.dma_start(flat, src.to_broadcast([P, n])).then_inc(sig("weights_loaded"), 16)
            with sp.Fori(0, PASSES) as it:
                src = A["x"][bass.ds(NB * it, NB), :, :].rearrange("b (t p) d -> p (b t) d", p=P)
                sp.dma_start(x_tok[:, :, :], src).then_inc(sig("x_loaded"), 16)
                for b in range(NB):
                    sp.wait_ge(sig("top_ready"), 2 * b + 2)
                    first = LW * RANKS
                    sp.dma_start(idx_scratch[b, 0:first].rearrange("(p r) -> p r", r=RANKS),
                                 topb[LW:P, 2 * b, :]).then_inc(sig("idx_saved"), 16)
                    sp.dma_start(idx_scratch[b, first:].rearrange("(p r) -> p r", r=RANKS),
                                 topb[:, 2 * b + 1, :]).then_inc(sig("idx_saved"), 16)
                def spread(b):
                    sp.wait_ge(sig("idx_saved"), 32 * NB)
                    if b > 0:
                        sp.wait_ge(sig("gscore_mm"), 3 * b)
                        sp.wait_ge(sig("gathT_mm"), 3 * b)
                    sp.dma_start(idxb, idx_scratch[b:b + 1, :].to_broadcast([P, GT * RANKS]))\
                      .then_inc(sig("idx_spread"), 16)

                spread(0)
                for b in range(NB):
                    for n in range(3):
                        sp.wait_ge(sig("gsc_ready"), 3 * b + n + 1)
                        to = score_scratch[b, n, :].rearrange("(m q c) -> q m c", q=4, c=512)
                        sp.dma_start(to, gsc[:, n, :]).then_inc(sig("gsc_saved"), 16)
                    if b + 1 < NB:
                        spread(b + 1)
                    for n in range(3):
                        sp.wait_ge(sig("gsc_saved"), 48 * (b + 1))
                        T, p0 = (0, LW) if n == 0 else (1, LW * (n - 1))
                        if n == 0 and b > 0:
                            sp.wait_ge(sig("pt_mm"), 6 * b)
                            sp.wait_ge(sig("xg_loaded"), 192 * b)
                        dst = SA(T, keys(T) + RANKS)
                        for t in range(GP):
                            own = score_scratch[b, n, :].rearrange("(t h g u r) -> t u g h r", t=GP, h=H, g=16, u=GP)
                            sp.dma_start(dst[p0 + t:p0 + LW:GP, :, keys(T):], own[t, t])\
                              .then_inc(sig(f"gsc_back{T}"), 16)
                    for T in range(2):
                        sp.wait_ge(sig("att_prob"), 2 * b + T + 1)
                        for n in ([0] if T == 0 else [1, 2]):
                            p0 = LW if n == 0 else LW * (n - 1)
                            for t in range(GP):
                                sp.dma_start(xg[:, n, RANKS * t:RANKS * t + RANKS],
                                             SA(T, keys(T) + RANKS)[p0 + t:p0 + LW:GP, :, keys(T):])\
                                  .then_inc(sig("xg_loaded"), 16)
                sp.wait_ge(sig("a_out"), 2 * NB)
                for i in range(3):
                    sp.dma_start(experts[:, i, :, :], A["experts"][:, i, :, :]).then_inc(sig("experts_loaded"), 16)
                sp.wait_ge(sig("y_ready"), 1)
                dst = out[bass.ds(NB * it, NB), :, :].rearrange("b (t p) d -> p (b t) d", p=P)
                sp.dma_start(dst, y_tok[:, :, :]).then_inc(sig("y_stored"), 16)
                sp.wait_ge(sig("y_stored"), 16)
                pass_end(sp, "sp")

        @block.vector
        def _(dve):
            st = Steps(dve, sig("dve_setup_step"))
            dve.memset(mean_mat[:, :], 1.0 / P).then_inc(sig("cols_set"), 1)
            dve.memset(eps_col[:, :], 1e-5).then_inc(sig("cols_set"), 1)
            dve.memset(one_col[:, :], 1.0).then_inc(sig("cols_set"), 1)
            dve.memset(shift_col[:, :], 0.5 * math.log(LN_SHIFT)).then_inc(sig("cols_set"), 1)
            st.mark(dve.memset(sh[:, :, :], 0.0))
            dve.wait_ge(sig("weights_loaded"), 16 * (len(loads) + len(rows)))
            dve.wait_ge(sig("setup_exp"), 3)
            st.link(dve.tensor_scalar(c_den[:, :, :], c_den[:, :, :], 1.0, None, ALU.add))
            st.link(dve.reciprocal(c_act[:, :, :], c_den[:, :, :]))
            dve.tensor_tensor(c_act[:, :, :], c_act[:, :, :], cT[:, :, :], ALU.mult).then_inc(sig("c_act_ready"), 1)
            for t in (ang[:, 0:5, :], dcol[:, 0:5].unsqueeze(2)):
                st.link(dve.tensor_scalar(t[:, 1, :], t[:, 0, :], 1.0, None, ALU.add))
                st.link(dve.reciprocal(t[:, 2, :], t[:, 1, :]))
                st.link(dve.tensor_scalar(t[:, 3, :], t[:, 2, :], -2.0 * math.pi, math.pi, ALU.mult, ALU.add))
                dve.tensor_scalar(t[:, 4, :], t[:, 3, :], 0.5, None, ALU.mult).then_inc(sig("delta_ready"), 1)
            dve.wait_ge(sig("delta_sin"), 4)
            for t in (ang, dcol[:, :].unsqueeze(2)):
                st.link(dve.tensor_scalar(t[:, 5, :], t[:, 5, :], -1.0, None, ALU.mult))
                st.link(dve.tensor_tensor(t[:, 7, :], t[:, 6, :], t[:, 6, :], ALU.mult))
                st.link(dve.tensor_scalar(t[:, 6, :], t[:, 7, :], 2.0, -1.0, ALU.mult, ALU.add))
            sd, cd = bc(ang[:, 5, :], 1, 6), bc(ang[:, 6, :], 1, 6)
            hd = DR // 2
            st.mark(dve.tensor_tensor(rope_t[:, 0, :, :], rope_cos[:, :, :], cd, ALU.mult))
            st.link(dve.tensor_tensor(rope_t[:, 1, :, :], rope_sin[:, :, :], sd, ALU.mult))
            st.link(dve.tensor_tensor(ropeC[:, :, 0:hd], rope_t[:, 0, :, :], rope_t[:, 1, :, :], ALU.subtract))
            st.mark(dve.tensor_copy(ropeC[:, :, hd:DR], ropeC[:, :, 0:hd]))
            st.mark(dve.tensor_tensor(rope_t[:, 0, :, :], rope_sin[:, :, :], cd, ALU.mult))
            st.link(dve.tensor_tensor(rope_t[:, 1, :, :], rope_cos[:, :, :], sd, ALU.mult))
            st.link(dve.tensor_tensor(ropeS[:, :, hd:DR], rope_t[:, 0, :, :], rope_t[:, 1, :, :], ALU.add))
            st.mark(dve.tensor_scalar(ropeS[:, 0:4, 0:hd], ropeS[:, 0:4, hd:DR], -1.0, None, ALU.mult))
            st.mark(dve.tensor_copy(ropeS[:, 4:6, 0:hd], ropeS[:, 4:6, hd:DR]))
            st.link(dve.tensor_scalar(rank_t[:, :], rank_a[:, :], dcol[:, 6:7], None, ALU.mult))
            st.link(dve.scalar_tensor_tensor(rank_tab[:, :], rank_b[:, :], dcol[:, 5:6], rank_t[:, :], ALU.mult, ALU.add))
            st.mark(dve.memset(rank_tab[0:DC, :], 1.0))
            for l in range(2):
                for T in range(2):
                    st.mark(dve.tensor_tensor(xtab[:, l, T, :], xpos[:, T, :], qk_scale[:, l, :], ALU.mult))
            dve.wait_ge(sig("mod_mm"), 1)
            st.link(dve.tensor_copy(modT[:, :, :], ps[:, 0, 0:12 * B].rearrange("p (j b) -> p j b", b=B)))
            for j in (1, 4, 7, 10):
                st.mark(dve.tensor_scalar(modT[:, j, :], modT[:, j, :], 1.0, None, ALU.add))
            for j in (2, 5, 8, 11):
                st.mark(dve.tensor_scalar(mod_tmp[:, 0, :], modT[:, j, :], 0.0, None, ALU.is_ge))
                st.link(dve.scalar_tensor_tensor(mod_tmp[:, 1, :], modT[:, j, :], -1.0, modT[:, j, :], ALU.mult, ALU.max))
                st.link(dve.tensor_scalar(mod_tmp[:, 1, :], mod_tmp[:, 1, :], 0.25, None, ALU.max))
                st.link(dve.tensor_scalar(mod_tmp[:, 0, :], mod_tmp[:, 0, :], 2.0, -1.0, ALU.mult, ALU.add))
                st.link(dve.tensor_tensor(modT[:, j, :], mod_tmp[:, 0, :], mod_tmp[:, 1, :], ALU.mult))
            dve.wait_ge(sig("absorb_mm"), 4)
            st.mark(dve.tensor_tensor(b1out[:, :], ps[:, 5, 0:1], b1o[:, :], ALU.add))
            st.mark(dve.tensor_copy(w_q2[:, 0:H * DC], ps[0:DQ, 1, 0:H * DC]))
            for h in range(H):
                st.mark(dve.tensor_copy(w_vo[:, h, :], ps[0:DC, 2 + h // 4, D * (h % 4):D * (h % 4) + D]))
            dve.tensor_copy(w_vo4[:, :, :], ps[:, 4, 0:2 * D].rearrange("p (i n) -> p i n", i=2))\
               .then_inc(sig("setup_done"), 1)
            dve.wait_ge(sig("setup_done"), 1)

            with dve.Fori(0, PASSES) as it:
                st = Steps(dve, sig("dve_step"))
                st.link(dve.tensor_copy(mod[:, :, :], modT[:, :, bass.ds(NB * it, NB)]))

                def layernorm(n, src, modulate, nout):
                    dve.wait_ge(sig("ln_mean"), n + 1)
                    dve.tensor_tensor(xc, src, ps[:, 0, :], ALU.subtract).then_inc(sig("ln_centered"), 1)
                    dve.wait_ge(sig("ln_centered"), n + 1)
                    dve.wait_ge(sig("ln_rstd"), n + 1)
                    st.link(dve.tensor_tensor(xc, xc, rstd, ALU.mult))
                    modulate()

                def by_batch(c, s, dst):
                    def go_():
                        for b in range(NB):
                            dve.tensor_scalar(dst[:, bcols(b)], xc[:, bcols(b)], mod[:, c, b:b + 1], mod[:, s, b:b + 1],
                                              ALU.mult, ALU.add).then_inc(sig("ln_out"), 1)
                    return go_

                def tile_max(a, T, width, factor):
                    st.link(dve.tensor_reduce(mx[:, a % 4, :], SA(T, width)[:, :, :], AX.X, ALU.max))
                    if factor is None:
                        ins = dve.tensor_scalar(nb[:, a % 4, :], mx[:, a % 4, :], -SCALE_A, None, ALU.mult)
                    else:
                        ins = dve.scalar_tensor_tensor(nb[:, a % 4, :], mx[:, a % 4, :], -1.0, factor, ALU.mult, ALU.mult)
                    ins.then_inc(sig("att_bias"), 1)

                def tile_scores(a, T, width, mask):
                    dve.wait_ge(sig("att_mm"), a + 1)
                    n, off = keys(T), P * T
                    for bank, heads in (SCORE_BANKS if a < 4 else SCORE_BANKS_2)[T]:
                        k = len(heads)
                        ins = dve.tensor_tensor(
                            SA(T, width)[:, heads[0]:heads[-1] + 1:heads[1] - heads[0], 0:n],
                            ps[:, bank, 0:k * n].rearrange("p (h n) -> p h n", h=k),
                            bc(mask[:, off:off + n], 1, k), ALU.add)
                    ins.then_inc(sig("att_evac"), 1)
                    dve.wait_ge(sig("att_evac"), a + 1)

                def tile_norm(a, T, width):
                    dve.wait_ge(sig("att_exp"), a + 1)
                    st.link(dve.reciprocal(rl[:, a % 4, :], ls[:, a % 4, :]))
                    v = SA(T, width)[:, :, :]
                    dve.tensor_tensor(v, v, bc(rl[:, a % 4, :], 2, width), ALU.mult).then_inc(sig("att_prob"), 1)

                def tile_pt(a, T):
                    for u in range(len(UNITS[T])):
                        if u % 2:
                            dve.wait_ge(sig("pt_mm"), 12 * (a // 4) + UNITS_BEFORE[a % 4] + u + 1)
                            rows_ = P if UNITS[T][u][1] == 0 else LW
                            dve.tensor_copy(PT[0:rows_, u, :], ps[0:rows_, 4 + u % 3, :]).then_inc(sig("pt_dve"), 1)

                dve.wait_ge(sig("xT_copied"), 1)
                layernorm(0, xT[:, :], by_batch(1, 0, hT), 2)
                dve.wait_ge(sig("kr_abs"), 1)
                kvp = ps[:, 6, 0:NT * (DC + DR)].rearrange("p (k n) -> p k n", k=NT)
                n = NT * (DC + DR)
                st.mark(dve.tensor_copy(kr_raw[:, :, :], kvp[:, :, DC:]))
                st.mark(dve.tensor_copy(kvsrc[:, :, 0:DC], kvp[:, :, 0:DC]))
                st.mark(dve.tensor_copy(ckv_b[:, :, :], ps[:, 6, n:n + NB * DC].rearrange("p (b n) -> p b n", b=NB)))
                n += NB * DC
                st.link(dve.tensor_copy(ckv_c[:, :, :], ps[0:LW, 6, n:n + NB * DC].rearrange("p (b n) -> p b n", b=NB)))
                dve.wait_ge(sig("kr_log"), 1)
                st.link(dve.scalar_tensor_tensor(kvsrc[:, :, DC:2 * DC], kr_raw[:, :, :], 0.0, kr_abs[:, :, :],
                                                 ALU.max, ALU.add))
                st.mark(dve.tensor_scalar(kvsrc[:, :, 64:80], kvsrc[:, :, 48:64], -1.0, None, ALU.mult))
                dve.tensor_copy(kvsrc[:, :, 80:96], kvsrc[:, :, 32:48]).then_inc(sig("kvsrc_ready"), 1)
                dve.wait_ge(sig("kvsrc_ready"), 1)
                for b in range(NB):
                    kk = slice(2 * b, 2 * b + 2)
                    st.mark(dve.tensor_tensor(kr_raw[:, kk, :], kvsrc[:, kk, 32:64], ropeC[:, 4:6, :], ALU.mult))
                    st.link(dve.tensor_tensor(kr_abs[:, kk, :], kvsrc[:, kk, 64:96], ropeS[:, 4:6, :], ALU.mult))
                for j in range(2):
                    st.mark(dve.tensor_copy(ka[:, :, j, 0:DC], kvsrc[:, :, 0:DC]))
                    dve.tensor_tensor(ka[:, :, j, DC:], kr_raw[:, :, :], kr_abs[:, :, :], ALU.add)\
                       .then_inc(sig("ka_ready"), 1)

                for k in range(NT):
                    b, T = k // 2, k % 2
                    n = LW if T == 0 else WMAX
                    width = LW + RANKS if T == 0 else WMAX
                    off = 0 if T == 0 else LW + RANKS
                    iv = iscore[:, b, off:off + width]
                    dve.wait_ge(sig("irel"), 2 * k + 2)
                    for h in range(IH):
                        add = mask_i[:, off:off + n] if h == 0 else iv[:, 0:n]
                        st.link(dve.scalar_tensor_tensor(iv[:, 0:n], irel[:, k % 2, h, 0:n], idx_w[:, h:h + 1], add,
                                                         ALU.mult, ALU.add))
                    if T == 0:
                        st.link(dve.tensor_copy(iv[:, n:width], mask_i[:, n:width]))
                    for r in range(0, RANKS, 8):
                        st.link(dve.max(top8[:, k, r:r + 8], iv))
                        st.link(dve.max_index(topi[:, k, r:r + 8], top8[:, k, r:r + 8], iv))
                        st.link(dve.match_replace(iv, top8[:, k, r:r + 8], iv, TAKEN))
                    dve.tensor_copy(topb[:, k, :], topi[:, k, :]).then_inc(sig("top_ready"), 1)

                v8 = lambda ap: ap.rearrange("p (h n) -> p h n", h=H)
                for k in range(NT):
                    T = k % 2
                    raw = ps[:, 5 + k % 2, 0:H * DR]
                    dve.wait_ge(sig("q2_log"), k + 1)
                    st.link(dve.scalar_tensor_tensor(q_mu, raw, 0.0, q_abs, ALU.max, ALU.add))
                    if k > 0:
                        dve.wait_ge(sig("q_turned"), k)
                    for s, dsts in ((0, (qa[:, :, DC:],)), (1, (qb[:, :, DC:2 * DC], qb[:, :, 2 * DC:]))):
                        C, Sn = ropeC[:, 2 * s + T, :], ropeS[:, 2 * s + T, :]
                        st.mark(dve.tensor_tensor(v8(q_c), v8(q_mu), bc(C, 1, H), ALU.mult))
                        st.mark(dve.tensor_tensor(v8(q_s)[:, :, 0:16], v8(q_mu)[:, :, 16:32], bc(Sn[:, 0:16], 1, H), ALU.mult))
                        st.link(dve.tensor_tensor(v8(q_s)[:, :, 16:32], v8(q_mu)[:, :, 0:16], bc(Sn[:, 16:32], 1, H), ALU.mult))
                        for dst in dsts:
                            dve.tensor_tensor(dst, v8(q_c), v8(q_s), ALU.add).then_inc(sig("q_ready"), 1)
                        dve.wait_ge(sig("q_ready"), 3 * k + (1, 3)[s])
                    dve.wait_ge(sig("q_turned"), k + 1)
                    t0, t1, p0 = (0, LW, LW) if T == 0 else (LW, GT, 0)
                    for i in range(2):
                        src = ps[0:GF, 3 + i, :].rearrange("p (h t) -> p t h", h=4)[:, p0:P, :]
                        dve.tensor_copy(qbT[:, k // 2, t0:t1, 4 * i:4 * i + 4], src).then_inc(sig("qb_copied"), 1)

                for b in range(NB):
                    dve.wait_ge(sig("idx_spread"), 16 * (b + 1))
                    if b > 0:
                        dve.wait_ge(sig("gather_mm"), 12 * b)
                    dve.tensor_scalar(hot0[:, :], idxb, source[:, 0:1], None, ALU.is_equal).then_inc(sig("hot_ready"), 1)
                    dve.tensor_scalar(hot1[:, :], idxb[:, 2 * LW * RANKS:], source[:, 1:2], None, ALU.is_equal)\
                       .then_inc(sig("hot_ready"), 1)
                    dve.wait_ge(sig("hot_ready"), 2 * b + 2)
                    if b > 0:
                        dve.wait_ge(sig("gscore_mm"), 3 * b)
                        dve.wait_ge(sig("gathT_mm"), 3 * b)
                    for g in range(12):
                        dve.wait_ge(sig("gather_mm"), 12 * b + g + 1)
                        dve.tensor_tensor(gath[:, 512 * g:512 * g + 512].rearrange("p (t r) -> p t r", r=RANKS),
                                          ps[0:GF, 2 + g % 2, :].rearrange("p (t r) -> p t r", r=RANKS),
                                          bc(rank_tab[:, :], 1, 16), ALU.mult).then_inc(sig("gath_evac"), 1)

                for b in range(NB):
                    if b > 0:
                        dve.wait_ge(sig("xg_loaded"), 192 * b)
                        dve.wait_ge(sig("pt_mm"), 6 * b)
                        dve.wait_ge(sig("gsc_back0"), 64 * b)
                        dve.wait_ge(sig("gsc_back1"), 128 * b)
                    st.link(dve.memset(SA(0, P + RANKS)[0:LW, :, P:], MASKED))
                    for T in range(2):
                        a = 2 * b + T
                        tile_scores(a, T, keys(T) + RANKS, mask_a)
                        dve.wait_ge(sig(f"gsc_back{T}"), 64 * (1 + T) * (b + 1))
                        tile_max(a, T, keys(T) + RANKS, None)
                    for T in range(2):
                        tile_norm(2 * b + T, T, keys(T) + RANKS)
                    for T in range(2):
                        tile_pt(2 * b + T, T)
                    dve.wait_ge(sig("a_out"), 2 * b + 2)
                    xb = xT[:, bcols(b)]
                    st.link(dve.scalar_tensor_tensor(xb, ps[:, 4, 0:L], mod[:, 2, b:b + 1], xb, ALU.mult, ALU.add))
                    xl = xT[:, L * b + LW:L * b + L]
                    dve.scalar_tensor_tensor(xl, ps[:, 5, 0:GT], mod[:, 2, b:b + 1], xl, ALU.mult, ALU.add)\
                       .then_inc(sig("x_updated"), 1)

                dve.wait_ge(sig("x_updated"), 2)
                layernorm(1, xT[:, :], by_batch(4, 3, fT), 4)
                dve.wait_ge(sig("ln_out"), 4)

                def shift(n):
                    v = fT[:, :].rearrange("p (b t) -> p b t", b=NB)
                    dve.tensor_copy(sh[0:64, :, :], v[0:64, :, :]).then_inc(sig("shifted"), 1)
                    dve.tensor_copy(sh[64:P, :, 1:L], v[64:P, :, 0:L - 1]).then_inc(sig("shifted"), 1)
                    dve.wait_ge(sig("shifted"), 2 * n + 2)

                for l in range(2):
                    shift(2 * l)
                    for k in range(NT):
                        T = k % 2
                        m = NT * l + k
                        dve.wait_ge(sig("qk_squared"), m + 1)
                        pb = 2 * (k % 2)
                        v3 = lambda ap: ap.rearrange("p (s h n) -> p s h n", s=2, h=H)
                        qk = ps[:, pb:pb + 2, :].rearrange("p s (h n) -> p s h n", h=H)
                        ring = qk_ring[k % 2]
                        r0, r1 = v3(ring), v3(big[:, 1024:2048])
                        tab = xtab[:, l, T, :].rearrange("p (c s n) -> p c s n", c=2, s=2)
                        if m > 1:
                            dve.wait_ge(sig("qk_turned"), m - 1)
                        hh_ = DH // 2
                        st.mark(dve.tensor_tensor(r0, qk, bc(tab[:, 0, :, :], 2, H), ALU.mult))
                        st.mark(dve.tensor_tensor(r1[:, :, :, 0:hh_], qk[:, :, :, hh_:], bc(tab[:, 1, :, 0:hh_], 2, H), ALU.mult))
                        st.link(dve.tensor_tensor(r1[:, :, :, hh_:], qk[:, :, :, 0:hh_], bc(tab[:, 1, :, hh_:], 2, H), ALU.mult))
                        st.mark(dve.tensor_tensor(ring, ring, big[:, 1024:2048], ALU.add))
                        st.link(dve.tensor_reduce(ssq[:, k, :], SAf[:, 1024 * (k % 2):1024 * (k % 2) + 1024]
                                                  .rearrange("p (h n) -> p h n", n=DH), AX.X, ALU.add))
                        dve.tensor_scalar(ssq[:, k, :], ssq[:, k, :], 1e-24, None, ALU.max).then_inc(sig("ssq_ready"), 1)
                        dve.wait_ge(sig("rs_ready"), m + 1)
                        nt = nb[:, 14:16, :].rearrange("p u h -> p (u h)")
                        st.link(dve.tensor_tensor(nt, ssq[:, k, :], rs[:, k, :], ALU.mult))
                        st.link(dve.scalar_tensor_tensor(nt, nt, -0.5, rs[:, k, :], ALU.mult, ALU.mult))
                        st.link(dve.scalar_tensor_tensor(rs[:, k, :], nt, 1.5, rs[:, k, :], ALU.add, ALU.mult))
                        st.mark(dve.tensor_scalar(cqs[:, k, :], rs[:, k, 0:H], 8.0, None, ALU.mult))
                        kk = ring[:, 512:1024].rearrange("p (h n) -> p h n", h=H)
                        dve.tensor_tensor(kk, kk, bc(rs[:, k, H:], 2, DH), ALU.mult).then_inc(sig("qk_ready"), 1)
                    for k in range(NT):
                        T, a = k % 2, 4 + 4 * l + k
                        if k >= 2:
                            dve.wait_ge(sig("pt_mm"), 12 * (l + 1) + UNITS_BEFORE[k - 1])
                        tile_scores(a, T, keys(T), mask_w)
                        if k > 1:
                            tile_pt(a - 2, T)
                        tile_max(a, T, keys(T), cqs[:, k, :])
                        if k > 0:
                            tile_norm(a - 1, 1 - T, keys(1 - T))
                    tile_pt(a - 1, 1 - T)
                    tile_norm(a, T, keys(T))
                    tile_pt(a, T)
                    dve.wait_ge(sig("f_o"), l + 1)
                    st.link(dve.tensor_tensor(fT[:, :], ps[:, 0, :], fT[:, :], ALU.add))
                    shift(2 * l + 1)

                    def affine():
                        dve.tensor_scalar(hT[:, :], xc, ln_gb[:, l, 0:1], ln_gb[:, l, 1:2], ALU.mult, ALU.add)\
                           .then_inc(sig("ln_out"), 1)

                    layernorm(2 + l, sh[:, :, :].rearrange("p b t -> p (b t)"), affine, 5 + l)
                    for c in range(3):
                        dve.wait_ge(sig("f_a"), 3 * l + c + 1)
                        dve.wait_ge(sig("f_gelu"), 3 * l + c + 1)
                        m = HC[c]
                        dve.scalar_tensor_tensor(hh[0:m, c, :], ps[0:m, c, :], b1[0:m, l, 0, c:c + 1], PT[0:m, c, :],
                                                 ALU.add, ALU.mult).then_inc(sig("f_hidden"), 1)
                    dve.wait_ge(sig("f_down"), l + 1)
                    dve.scalar_tensor_tensor(fT[:, :], ps[:, 6, :], b2[:, l:l + 1], fT[:, :], ALU.add, ALU.add)\
                       .then_inc(sig("f_done"), 1)
                    dve.wait_ge(sig("f_done"), l + 1)
                for b in range(NB):
                    dve.scalar_tensor_tensor(xT[:, bcols(b)], fT[:, bcols(b)], mod[:, 5, b:b + 1], xT[:, bcols(b)],
                                             ALU.mult, ALU.add).then_inc(sig("x_updated"), 1)

                dve.wait_ge(sig("x_updated"), 4)
                layernorm(4, xT[:, :], by_batch(7, 6, hT), 8)
                dve.wait_ge(sig("qk1_mm"), 2)
                dve.tensor_scalar(k1T, ps[:, 1, :], b1k[:, 0:1], None, ALU.add).then_inc(sig("k1_copied"), 1)
                for u in range(4 * NT):
                    dve.wait_ge(sig("l1_mm"), u + 1)
                    b0 = 2 * (u % 2)
                    st.link(dve.tensor_reduce(mx[:, u, 0:4].rearrange("p (g j) -> p g j", j=2),
                                              ps[:, b0:b0 + 2, :].rearrange("p g (j n) -> p g j n", j=2), AX.X, ALU.max))
                    dve.tensor_scalar(nb[:, u, 0:4], mx[:, u, 0:4], -SCALE_1, None, ALU.mult).then_inc(sig("l1_bias"), 1)
                    if u > 0:
                        turned_copy1(dve, u - 1, 1, "l1_pt_dve")
                turned_copy1(dve, u, 1, "l1_pt_dve")
                dve.wait_ge(sig("l1_exp"), 4 * NT)
                dve.reciprocal(rl1, ls1).then_inc(sig("l1_recip"), 1)
                dve.wait_ge(sig("l1_recip_wide"), 1)
                dve.wait_ge(sig("l1_pv"), 4 * NT)
                dve.tensor_tensor(hT[:, :], ps[:, 7, :], xc, ALU.mult).then_inc(sig("att1_ready"), 1)
                dve.wait_ge(sig("l1_out"), 1)
                for b in range(NB):
                    st.link(dve.tensor_scalar(xc[:, bcols(b)], ps[:, 1, bcols(b)], b1out[:, 0:1], mod[:, 8, b:b + 1],
                                              ALU.add, ALU.mult))
                    dve.tensor_tensor(xT[:, bcols(b)], xT[:, bcols(b)], xc[:, bcols(b)], ALU.add).then_inc(sig("x_updated"), 1)

                dve.wait_ge(sig("x_updated"), 6)
                layernorm(5, xT[:, :], by_batch(10, 9, hT), 10)
                v4 = lambda ap: ap.rearrange("p (k e) -> p k e", e=E1)
                den, sc, sel, rep, msk, wgt = (rt[:, i, :] for i in range(6))
                dve.wait_ge(sig("route_exp"), 1)
                st.link(dve.tensor_scalar(den, den, 1.0, None, ALU.add))
                st.link(dve.reciprocal(sc, den))
                st.link(dve.tensor_tensor(v4(sel), v4(sc), bc(e_bias[:, :], 1, NT), ALU.add))
                for k in range(NT):
                    st.mark(dve.max(rsm[:, 8 * k:8 * k + 8], v4(sel)[:, k, :]))
                st.wait()
                for k in range(NT):
                    st.mark(dve.match_replace(v4(rep)[:, k, :], rsm[:, 8 * k:8 * k + 8], v4(sel)[:, k, :], TAKEN))
                st.wait()
                st.link(dve.tensor_tensor(msk, rep, sel, ALU.not_equal))
                st.link(dve.tensor_tensor(wgt, msk, sc, ALU.mult))
                st.link(dve.tensor_reduce(rsm[:, 32:36], v4(wgt), AX.X, ALU.add))
                st.link(dve.reciprocal(rsm[:, 36:40], rsm[:, 32:36]))
                dve.scalar_tensor_tensor(v4(rt[:, 6, :]), v4(wgt), ROUTE, bc(rsm[:, 36:40], 2, E1), ALU.mult, ALU.mult)\
                   .then_inc(sig("comb_ready"), 1)
                for e in range(E1 + 1):
                    s = e % 2
                    dve.wait_ge(sig("e_silu"), e + 1)
                    dve.wait_ge(sig("e_up"), e + 1)
                    if e >= 2:
                        dve.wait_ge(sig("e_down"), e - 1)
                    ins = dve.tensor_tensor(moe_h[:, s, :], moe_g[:, s, :], ps[:, 2 + s, :], ALU.mult)
                    if e < E1:
                        st.link(ins)
                        dve.wait_ge(sig("e_comb"), e + 1)
                        ins = dve.tensor_tensor(moe_h[:, s, :], moe_h[:, s, :], ps[:, 4 + s, :], ALU.mult)
                    ins.then_inc(sig("e_hidden"), 1)
                dve.wait_ge(sig("e_down"), E1 + 1)
                for b in range(NB):
                    dve.scalar_tensor_tensor(xT[:, bcols(b)], ps[:, 6, bcols(b)], mod[:, 11, b:b + 1], xT[:, bcols(b)],
                                             ALU.mult, ALU.add).then_inc(sig("x_updated"), 1)
                pass_end(dve, "dve")

        @block.scalar
        def _(act):
            st = Steps(act, sig("act_setup_step"))
            act.wait_ge(sig("weights_loaded"), 16 * (len(loads) + len(rows)))
            act.wait_ge(sig("cols_set"), 4)
            act.activation(c_den[:, :, :], cT[:, :, :], ACT.Exp, scale=-1.0).then_inc(sig("setup_exp"), 1)
            act.activation(ang[:, 0, :], delta_row[:, :], ACT.Exp, scale=-1.0).then_inc(sig("setup_exp"), 1)
            act.activation(dcol[:, 0:1], delta_col[:, :], ACT.Exp, scale=-1.0).then_inc(sig("setup_exp"), 1)
            act.wait_ge(sig("delta_ready"), 2)
            for t in (ang, dcol[:, :].unsqueeze(2)):
                for i in range(2):
                    act.activation(t[:, 5 + i, :], t[:, 3 + i, :], ACT.Sin).then_inc(sig("delta_sin"), 1)
            act.wait_ge(sig("setup_done"), 1)

            with act.Fori(0, PASSES) as it:
                st = Steps(act, sig("act_step"))
                act.preload_act_table_set(LN_AND_EXP)
                act.wait_ge(sig("x_turned"), 1)
                act.activation(xT[:, :], ps[:, 0, :], ACT.Copy).then_inc(sig("xT_copied"), 1)

                def layernorm(n):
                    act.wait_ge(sig("ln_centered"), n + 1)
                    act.activation(sq, xc, ACT.Square).then_inc(sig("ln_squared"), 1)
                    act.wait_ge(sig("ln_var"), n + 1)
                    st.link(act.activation(rstd, ps[:, 1, :], ACT.Ln, bias=eps_col[:, :]))
                    act.activation(rstd, rstd, ACT.Exp, scale=-0.5).then_inc(sig("ln_rstd"), 1)

                def tile_exp(a, T, width, scale):
                    act.wait_ge(sig("att_bias"), a + 1)
                    for h in range(H):
                        v = SA(T, width)[:, h, :]
                        ins = act.activation(v, v, ACT.Exp, bias=nb[:, a % 4, h:h + 1],
                                             scale=SCALE_A if scale is None else scale[:, h:h + 1],
                                             accum_out=ls[:, a % 4, h:h + 1])
                    ins.then_inc(sig("att_exp"), 1)

                def tile_pt(a, T):
                    for u in range(0, len(UNITS[T]), 2):
                        act.wait_ge(sig("pt_mm"), 12 * (a // 4) + UNITS_BEFORE[a % 4] + u + 1)
                        act.activation(PT[:, u, :], ps[:, 4 + u % 3, :], ACT.Copy).then_inc(sig("pt_act"), 1)

                def tile_out(a, dst):
                    act.wait_ge(sig("att_pv"), a + 1)
                    n = dst.shape[1]
                    act.activation(dst[:, :, cols(a % 4)], ps[:, 7, 0:n * P].rearrange("p (i n) -> p i n", i=n), ACT.Copy)\
                       .then_inc(sig("o_copied"), 1)

                layernorm(0)
                for i, (dst, bank) in enumerate(((kiT, 3), (qiT[:, 0, :], 4), (qiT[:, 1, :], 5))):
                    act.wait_ge(sig("a_proj"), i + 1)
                    act.activation(dst, ps[:, bank, :], ACT.Copy).then_inc(sig("a_copied"), 1)
                act.wait_ge(sig("a_proj"), 4)
                act.activation(cqT[:, :], ps[0:DQ, 2, :], ACT.Copy).then_inc(sig("a_copied"), 1)
                act.wait_ge(sig("kv_proj"), 1)
                kvp = ps[:, 6, 0:NT * (DC + DR)].rearrange("p (k n) -> p k n", k=NT)
                act.activation(kr_abs[:, :, :], kvp[:, :, DC:], ACT.Abs).then_inc(sig("kr_abs"), 1)
                act.wait_ge(sig("kr_abs"), 1)
                st.link(act.activation(kr_abs[:, :, :], kr_abs[:, :, :], ACT.Exp, scale=-1.0))
                act.activation(kr_abs[:, :, :], kr_abs[:, :, :], ACT.Ln, bias=one_col[:, :]).then_inc(sig("kr_log"), 1)
                for k in range(NT):
                    n = LW if k % 2 == 0 else WMAX
                    act.wait_ge(sig("iscore_mm"), k + 1)
                    if k >= 2:
                        act.wait_ge(sig("top_ready"), k - 1)
                    for j in range(2):
                        act.activation(irel[:, k % 2, j:j + 3:2, 0:n],
                                       ps[:, 2 + 2 * (k % 2) + j, 0:2 * n].rearrange("p (h n) -> p h n", h=2),
                                       ACT.Relu).then_inc(sig("irel"), 1)
                act.wait_ge(sig("kaT_turned"), 1)
                act.activation(kaT[:, :], ps[:, 7, :], ACT.Copy).then_inc(sig("ka_copied"), 1)
                for k in range(NT):
                    act.wait_ge(sig("q2_mm"), k + 1)
                    if k > 0:
                        act.wait_ge(sig("q_ready"), 3 * k)
                    st.link(act.activation(q_abs, ps[:, 5 + k % 2, 0:H * DR], ACT.Abs))
                    st.link(act.activation(q_abs, q_abs, ACT.Exp, scale=-1.0))
                    act.activation(q_abs, q_abs, ACT.Ln, bias=one_col[:, :]).then_inc(sig("q2_log"), 1)
                    if k > 0:
                        act.wait_ge(sig("q_turned"), k)
                    lat = ps[:, k % 2, 0:256].rearrange("p (h n) -> p h n", h=H)
                    act.activation(qa[:, :, 0:DC], lat, ACT.Copy).then_inc(sig("q_latent"), 1)
                    act.activation(qb[:, :, 0:DC], lat, ACT.Copy).then_inc(sig("q_latent"), 1)
                    act.wait_ge(sig("q_turned"), k + 1)
                    act.activation(qaT[:, :, cols(k)], ps[:, 2, :].rearrange("p (i n) -> p i n", i=4), ACT.Copy)\
                       .then_inc(sig("qa_copied"), 1)
                for b in range(NB):
                    if b > 0:
                        act.wait_ge(sig("gsc_saved"), 48 * b)
                    for n in range(3):
                        act.wait_ge(sig("gathT_mm"), 3 * b + n + 1)
                        act.activation(gathT[:, b, 16 * n:16 * n + 16, :],
                                       ps[:, n % 2, :].rearrange("p (j c) -> p j c", c=DC), ACT.Copy)\
                           .then_inc(sig("gathT_ready"), 1)
                        act.wait_ge(sig("gscore_mm"), 3 * b + n + 1)
                        act.activation(gsc[:, n, :], ps[:, 5 + n, :], ACT.Copy).then_inc(sig("gsc_ready"), 1)
                for b in range(NB):
                    for T in range(2):
                        tile_exp(2 * b + T, T, keys(T) + RANKS, None)
                    for T in range(2):
                        tile_pt(2 * b + T, T)
                        tile_out(2 * b + T, oTa)
                    act.wait_ge(sig("xg_turned"), b + 1)
                    act.wait_ge(sig("pdiag_zero"), 1)
                    for t in range(GP):
                        part = slice(RANKS * t, RANKS * t + RANKS)
                        act.activation(pdiag[part, :, t, :], ps[part, 0, 0:3 * P].rearrange("p (j h) -> p j h", h=H),
                                       ACT.Copy).then_inc(sig("pdiag_ready"), 1)
                    for n in range(3):
                        act.wait_ge(sig("og_mm"), 3 * b + n + 1)
                        act.activation(og[:, 64 * n:64 * n + 64, :],
                                       ps[0:DC, 1 + n, :].rearrange("p (t h) -> p t h", h=H), ACT.Copy)\
                           .then_inc(sig("og_ready"), 1)

                layernorm(1)
                for l in range(2):
                    def values(b, c):
                        act.wait_ge(sig("v_mm"), 6 * l + 3 * b + c + 1)
                        r = LW if c == 2 else P
                        act.activation(vt[0:r, b, c, :], ps[0:r, 4 + c % 2, :], ACT.Copy).then_inc(sig("v_copied"), 1)

                    def squares(k):
                        m = NT * l + k
                        act.wait_ge(sig("qk_mm"), m + 1)
                        if k >= 2:
                            act.wait_ge(sig("ssq_ready"), m - 1)
                        act.activation(SAf[:, 1024 * (k % 2):1024 * (k % 2) + 1024]
                                       .rearrange("p (s n) -> p s n", s=2),
                                       ps[:, 2 * (k % 2):2 * (k % 2) + 2, :], ACT.Square).then_inc(sig("qk_squared"), 1)

                    squares(0)
                    for k in range(NT):
                        m = NT * l + k
                        if k + 1 < NT:
                            squares(k + 1)
                        act.wait_ge(sig("ssq_ready"), m + 1)
                        st.link(act.activation(rs[:, k, :], ssq[:, k, :], ACT.Ln, scale=LN_SHIFT))
                        act.activation(rs[:, k, :], rs[:, k, :], ACT.Exp, scale=-0.5, bias=shift_col[:, :])\
                           .then_inc(sig("rs_ready"), 1)
                        for j in range(2 * k, 2 * k + 2):
                            if j < 6:
                                values(j // 3, j % 3)
                        act.wait_ge(sig("qk_turned"), m + 1)
                        if m == 0:
                            act.wait_ge(sig("q_zero"), 2)
                        qt = ps[:, 6, :].rearrange("p (i n) -> p i n", i=4)
                        act.activation(q_half[0:DH, :, 0, cols(k)], qt[0:DH], ACT.Copy).then_inc(sig("q_copied"), 1)
                        act.activation(q_half[DH:P, :, 1, cols(k)], qt[DH:P], ACT.Copy).then_inc(sig("q_copied"), 1)
                        act.activation(kT[:, :, cols(k)], ps[:, 7, :].rearrange("p (i n) -> p i n", i=4), ACT.Copy)\
                           .then_inc(sig("k_copied"), 1)
                    for k in range(NT):
                        a, T = 4 + 4 * l + k, k % 2
                        tile_exp(a, T, keys(T), cqs[:, k, :])
                        if k > 1:
                            tile_out(a - 2, oT)
                        if k > 0:
                            tile_pt(a - 1, 1 - T)
                    tile_out(a - 1, oT)
                    tile_pt(a, T)
                    tile_out(a, oT)
                    layernorm(2 + l)
                    for c in range(3):
                        m = HC[c]
                        act.wait_ge(sig("f_g"), 3 * l + c + 1)
                        act.activation(PT[0:m, c, :], ps[0:m, 3 + c, :], ACT.Gelu, bias=b1[0:m, l, 1, c:c + 1])\
                           .then_inc(sig("f_gelu"), 1)
                    act.preload_act_table_set(LN_AND_EXP)

                layernorm(4)
                act.wait_ge(sig("qk1_mm"), 1)
                act.activation(q1T, ps[:, 0, :], ACT.Identity, bias=b1q[:, :]).then_inc(sig("q1_copied"), 1)
                act.wait_ge(sig("v1_mm"), 1)
                act.wait_ge(sig("v_zero"), 1)
                for j in range(4):
                    src = ps[:, 2, :].rearrange("p (k g j n) -> p k g j n", k=NT, g=4, j=4)
                    for k in range(NT):
                        act.activation(v_own[:, k, :, j, D1 * j:D1 * j + D1], src[:, k, :, j, :], ACT.Copy)\
                           .then_inc(sig("v1_copied"), 1)
                for u in range(4 * NT):
                    act.wait_ge(sig("l1_bias"), u + 1)
                    if u >= 4:
                        act.wait_ge(sig("l1_turned"), 2 * u - 6)
                    for e in range(4):
                        ins = act.activation(probs1(u)[:, e, :], ps[:, 2 * (u % 2) + e // 2, L * (e % 2):L * (e % 2) + L],
                                             ACT.Exp, bias=nb[:, u, e:e + 1], scale=SCALE_1,
                                             accum_out=ls1[:, 4 * u + e:4 * u + e + 1])
                    ins.then_inc(sig("l1_exp"), 1)
                    if u > 0:
                        turned_copy1(act, u - 1, 0, "l1_pt_act")
                turned_copy1(act, u, 0, "l1_pt_act")
                act.wait_ge(sig("l1_recip_turned"), 1)
                act.activation(combT[:, :], ps[0:H1, 0, :], ACT.Copy).then_inc(sig("l1_recip_copied"), 1)
                act.wait_ge(sig("l1_recip_mm"), 1)
                act.activation(xc, ps[:, 1, :], ACT.Copy).then_inc(sig("l1_recip_wide"), 1)

                layernorm(5)
                act.wait_ge(sig("route_mm"), 1)
                act.activation(rt[:, 0, :], ps[:, 7, 0:NT * E1], ACT.Exp, scale=-1.0).then_inc(sig("route_exp"), 1)
                act.wait_ge(sig("comb_turned"), 1)
                act.activation(combT[:, :], ps[0:E1, 7, :], ACT.Copy).then_inc(sig("comb_copied"), 1)
                for e in range(E1 + 1):
                    act.wait_ge(sig("e_gate"), e + 1)
                    if e >= 2:
                        act.wait_ge(sig("e_hidden"), e - 1)
                    act.activation(moe_g[:, e % 2, :], ps[:, e % 2, :], ACT.Silu).then_inc(sig("e_silu"), 1)
                act.wait_ge(sig("y_turned"), 1)
                act.activation(y_tok[:, :, :], ps[:, 7, :].rearrange("p (k n) -> p k n", k=NT), ACT.Copy).then_inc(sig("y_ready"), 1)
                pass_end(act, "act")

        @block.tensor
        def _(pe):
            mm = pe.matmul
            pe.wait_ge(sig("weights_loaded"), 16 * (len(loads) + len(rows)))
            for h in range(H):
                last = mm(ps[0:DQ, 1, DC * h:DC * h + DC], uqT[:, h, :], ukT[:, h, :], start=True, stop=True)
            last.then_inc(sig("absorb_mm"), 1)
            for h in range(H):
                last = mm(ps[0:DC, 2 + h // 4, D * (h % 4):D * (h % 4) + D], uvT[:, h, :], w_out0[:, h, :],
                          start=True, stop=True)
            last.then_inc(sig("absorb_mm"), 1)
            for h in range(H):
                q = DC * (h % 4)
                last = mm(ps[q:q + DC, 4, D * (h // 4):D * (h // 4) + D], uvT[:, h, :], w_out0[:, h, :],
                          start=True, stop=True)
            last.then_inc(sig("absorb_mm"), 1)
            mm(ps[:, 5, 0:1], w1o[:, :], b1v[:, :], start=True, stop=True).then_inc(sig("absorb_mm"), 1)
            pe.wait_ge(sig("c_act_ready"), 1)
            for j in range(12):
                last = mm(ps[:, 0, B * j:B * j + B], wmod[:, j // 6, D * (j % 6):D * (j % 6) + D], c_act[:, j // 6, :],
                          start=True, stop=True)
            last.then_inc(sig("mod_mm"), 1)
            pe.wait_ge(sig("setup_done"), 1)

            with pe.Fori(0, PASSES) as it:
                pe.wait_ge(sig("x_loaded"), 16)
                for k in range(NT):
                    last = pe.transpose(ps[:, 0, cols(k)], x_tok[:, k, :], ident[:, :])
                last.then_inc(sig("x_turned"), 1)

                def layernorm(n, src):
                    mm(ps[:, 0, :], mean_mat[:, :], src, start=True, stop=True).then_inc(sig("ln_mean"), 1)
                    pe.wait_ge(sig("ln_squared"), n + 1)
                    mm(ps[:, 1, :], mean_mat[:, :], sq, start=True, stop=True).then_inc(sig("ln_var"), 1)

                def tile_scores(a, T, kk):
                    b, k = (a % 4) // 2, a % 4
                    n = keys(T)
                    for bank, heads in SCORE_BANKS[T]:
                        for j, h in enumerate(heads):
                            r = slice(DH * (h % 2), DH * (h % 2) + DH)
                            last = mm(ps[:, bank, n * j:n * j + n], qaT[r, h // 2, cols(k)], kk(r, h, key_cols(b, T)),
                                      start=True, stop=True)
                    last.then_inc(sig("att_mm"), 1)

                def tile_pt(a, T, width):
                    for u, (h0, c) in enumerate(UNITS[T]):
                        first, n = (0, P) if c == 0 else (P, LW)
                        if u == 3:
                            pe.wait_ge(sig("pt_act"), pt_act(a) + 1)
                        for i in range(4):
                            last = pe.transpose(ps[0:n, 4 + u % 3, P * i:P * i + P],
                                                SA(T, width)[:, h0 + i, first:first + n], ident[:, :])
                        last.then_inc(sig("pt_mm"), 1)

                def pt_act(a):
                    return 6 * (a // 4) + UNITS_BEFORE[a % 4] // 2

                def tile_pv(a, T, m, lhs):
                    per = P // m
                    chunks = 1 + T
                    if a > 0:
                        pe.wait_ge(sig("o_copied"), a)
                    for h in range(H):
                        for c in range(chunks):
                            u = (h // 4) * chunks + c
                            who = "pt_act" if u % 2 == 0 else "pt_dve"
                            if h % 4 == 0:
                                pe.wait_ge(sig(who), pt_act(a) + u // 2 + 1)
                            n = P if c == 0 else LW
                            q = m * (h % per)
                            last = mm(ps[q:q + m, 7, P * (h // per):P * (h // per) + P], lhs(h, c),
                                      PT[0:n, u, P * (h % 4):P * (h % 4) + P], start=(c == 0), stop=(c == chunks - 1))
                    last.then_inc(sig("att_pv"), 1)

                pe.wait_ge(sig("xT_copied"), 1)
                layernorm(0, xT[:, :])
                pe.wait_ge(sig("ln_out"), 2)
                for w, bank, r in ((w_ki[:, :], 3, P), (w_qi[:, 0:P], 4, P), (w_qi[:, P:], 5, P), (w_dq[:, :], 2, DQ)):
                    mm(ps[0:r, bank, :], w, hT[:, :], start=True, stop=True).then_inc(sig("a_proj"), 1)
                n = DC + DR
                for k in range(NT):
                    mm(ps[:, 6, n * k:n * k + n], hT[:, cols(k)], w_kv[:, :], start=True, stop=True)
                for b in range(NB):
                    mm(ps[:, 6, n * NT + DC * b:n * NT + DC * b + DC], hT[:, L * b + LW:L * b + LW + P], w_kv[:, 0:DC],
                       start=True, stop=True)
                for b in range(NB):
                    c0 = n * NT + DC * NB + DC * b
                    last = mm(ps[0:LW, 6, c0:c0 + DC], hT[:, L * b + L - LW:L * b + L], w_kv[:, 0:DC], start=True, stop=True)
                last.then_inc(sig("kv_proj"), 1)
                pe.wait_ge(sig("a_copied"), 4)
                for k in range(NT):
                    b, T = k // 2, k % 2
                    n = LW if T == 0 else WMAX
                    if k >= 2:
                        pe.wait_ge(sig("irel"), 2 * k - 2)
                    for h in (0, 2, 1, 3):
                        r = slice(DH * (h % 2), DH * (h % 2) + DH)
                        last = mm(ps[:, 2 + 2 * (k % 2) + h % 2, n * (h // 2):n * (h // 2) + n], qiT[r, h // 2, cols(k)],
                                  kiT[r, L * b:L * b + n], start=True, stop=True)
                    last.then_inc(sig("iscore_mm"), 1)
                pe.wait_ge(sig("ka_ready"), 2)
                for k in range(NT):
                    last = pe.transpose(ps[:, 7, cols(k)], ka[:, k, :, :].rearrange("p s n -> p (s n)"), ident[:, :])
                last.then_inc(sig("kaT_turned"), 1)
                pe.wait_ge(sig("irel"), 2 * NT)
                for k in range(NT):
                    if k >= 2:
                        pe.wait_ge(sig("q_ready"), 3 * k - 3)
                        pe.wait_ge(sig("q_latent"), 2 * k - 2)
                    mm(ps[:, k % 2, 0:H * DC], cqT[:, cols(k)], w_q2[:, 0:H * DC], start=True, stop=True)
                    mm(ps[:, 5 + k % 2, 0:H * DR], cqT[:, cols(k)], w_q2[:, H * DC:], start=True, stop=True)\
                      .then_inc(sig("q2_mm"), 1)
                    pe.wait_ge(sig("q_ready"), 3 * k + 3)
                    pe.wait_ge(sig("q_latent"), 2 * k + 2)
                    if k > 0:
                        pe.wait_ge(sig("qa_copied"), k)
                        pe.wait_ge(sig("qb_copied"), 2 * k)
                    for i in range(4):
                        pe.transpose(ps[:, 2, P * i:P * i + P], qa[:, 2 * i:2 * i + 2, :].rearrange("p h n -> p (h n)"),
                                     ident[:, :])
                    for h in range(H):
                        last = pe.transpose(ps[0:GF, 3 + h // 4, P * (h % 4):P * (h % 4) + P], qb[:, h, :], ident[:, :])
                    last.then_inc(sig("q_turned"), 1)
                pe.wait_ge(sig("kv_split"), 5)
                pe.wait_ge(sig("qa_copied"), NT)
                pe.wait_ge(sig("qb_copied"), 2 * NT)
                for b in range(NB):
                    pe.wait_ge(sig("hot_ready"), 2 * b + 2)
                    for g in range(12):
                        if 12 * b + g >= 2:
                            pe.wait_ge(sig("gath_evac"), 12 * b + g - 1)
                        terms = [(kv_part[i][:, 2 * b, :], hot0[:, 512 * g:512 * g + 512]) for i in range(3)]
                        if g >= 8:
                            terms += [(kv_part[i][:, 2 * b + 1, :], hot1[:, 512 * (g - 8):512 * (g - 8) + 512])
                                      for i in range(3)]
                        for i, (l_, r_) in enumerate(terms):
                            last = mm(ps[0:GF, 2 + g % 2, :], l_, r_, start=(i == 0), stop=(i == len(terms) - 1))
                        last.then_inc(sig("gather_mm"), 1)
                    for n in range(3):
                        pe.wait_ge(sig("gath_evac"), 12 * b + 4 * n + 4)
                        if b > 0:
                            pe.wait_ge(sig("gsc_ready"), 3 * (b - 1) + n + 1)
                        for q in range(4):
                            for blk in range(4):
                                t = 64 * n + 16 * q + 4 * blk
                                last = mm(ps[32 * q:32 * q + 32, 5 + n, P * blk:P * blk + P],
                                          qbT[:, b, t:t + GP, :].rearrange("p t h -> p (t h)"),
                                          gath[:, RANKS * t:RANKS * t + P], start=True, stop=True)
                        last.then_inc(sig("gscore_mm"), 1)
                        if 3 * b + n >= 2:
                            pe.wait_ge(sig("gathT_ready"), 3 * b + n - 1)
                        for j in range(16):
                            c0 = P * (16 * n + j)
                            last = pe.transpose(ps[:, n % 2, DC * j:DC * j + DC], gath[0:DC, c0:c0 + P], ident[0:DC, 0:DC])
                        last.then_inc(sig("gathT_mm"), 1)
                pe.wait_ge(sig("gathT_ready"), 6)
                pe.wait_ge(sig("ka_copied"), 1)
                for b in range(NB):
                    for T in range(2):
                        a = 2 * b + T
                        if a > 0:
                            pe.wait_ge(sig("att_evac"), a)
                        if b > 0:
                            pe.wait_ge(sig("pdiag_ready"), 4 * b)
                            pe.wait_ge(sig("og_ready"), 3 * b)
                            pe.wait_ge(sig("x_updated"), b)
                        tile_scores(a, T, lambda r, h, c: kaT[r, c])
                    for T in range(2):
                        a = 2 * b + T
                        pe.wait_ge(sig("att_prob"), a + 1)
                        if a > 0:
                            pe.wait_ge(sig("att_pv"), a)
                        tile_pt(a, T, keys(T) + RANKS)
                        lat = {(0, 0): kvsrc[:, 2 * b, 0:DC], (1, 0): ckv_b[:, b, :], (1, 1): ckv_c[:, b, :]}
                        tile_pv(a, T, DC, lambda h, c: lat[T, c])
                    pe.wait_ge(sig("xg_loaded"), 192 * (b + 1))
                    pe.wait_ge(sig("att_evac"), 2 * b + 2)
                    for n in range(3):
                        last = pe.transpose(ps[:, 0, P * n:P * n + P], xg[:, n, :], ident[:, :])
                    last.then_inc(sig("xg_turned"), 1)
                    pe.wait_ge(sig("pdiag_ready"), 4 * b + 4)
                    for n in range(3):
                        for j in range(16 * n, 16 * n + 16):
                            c0 = RANKS * (j - 16 * n)
                            last = mm(ps[0:DC, 1 + n, c0:c0 + GP * H], gathT[:, b, j, :],
                                      pdiag[:, j, :, :].rearrange("p t h -> p (t h)"), start=True, stop=True)
                        last.then_inc(sig("og_mm"), 1)
                    pe.wait_ge(sig("o_copied"), 2 * b + 2)
                    pe.wait_ge(sig("og_ready"), 3 * b + 3)
                    for i in range(2):
                        last = mm(ps[:, 4, 0:L], w_vo4[:, i, :], oTa[:, i, bcols(b)], start=(i == 0), stop=(i == 1))
                    last.then_inc(sig("a_out"), 1)
                    for h in range(H):
                        last = mm(ps[:, 5, 0:GT], w_vo[:, h, :], og[:, :, h], start=(h == 0), stop=(h == H - 1))
                    last.then_inc(sig("a_out"), 1)

                pe.wait_ge(sig("x_updated"), 2)
                layernorm(1, xT[:, :])
                for l in range(2):
                    pe.wait_ge(sig("shifted"), 4 * l + 2)

                    def values(b, c):
                        n = 6 * l + 3 * b + c
                        if n > 0:
                            pe.wait_ge(sig("v_copied"), n)
                        first, m = ((0, P), (LW, P), (L - LW, LW))[c]
                        mm(ps[0:m, 4 + c % 2, :], sh[:, b, first:first + m], wqkv[:, l, 1024:], start=True, stop=True)\
                          .then_inc(sig("v_mm"), 1)

                    def queries_keys(k):
                        m = NT * l + k
                        if k >= 2:
                            pe.wait_ge(sig("qk_ready"), m - 1)
                            pe.wait_ge(sig("qk_squared"), m - 1)
                        x = sh[:, k // 2, P * (k % 2):P * (k % 2) + P]
                        bank = 2 * (k % 2)
                        mm(ps[:, bank, :], x, wqkv[:, l, 0:512], start=True, stop=True)
                        mm(ps[:, bank + 1, :], x, wqkv[:, l, 512:1024], start=True, stop=True).then_inc(sig("qk_mm"), 1)

                    queries_keys(0)
                    for k in range(NT):
                        m = NT * l + k
                        if k + 1 < NT:
                            queries_keys(k + 1)
                        for j in range(2 * k, 2 * k + 2):
                            if j < 6:
                                values(j // 3, j % 3)
                        pe.wait_ge(sig("qk_ready"), m + 1)
                        if m > 0:
                            pe.wait_ge(sig("q_copied"), 2 * m)
                            pe.wait_ge(sig("k_copied"), m)
                        for i in range(4):
                            pe.transpose(ps[:, 6, P * i:P * i + P], qk_ring[k % 2][:, P * i:P * i + P], ident[:, :])
                        for i in range(4):
                            last = pe.transpose(ps[:, 7, P * i:P * i + P], qk_ring[k % 2][:, 512 + P * i:512 + P * i + P],
                                                ident[:, :])
                        last.then_inc(sig("qk_turned"), 1)
                    pe.wait_ge(sig("q_copied"), 2 * NT * (l + 1))
                    pe.wait_ge(sig("k_copied"), NT * (l + 1))
                    pe.wait_ge(sig("v_copied"), 6 * (l + 1))

                    def scores0(a, T):
                        k, n = a % 4, keys(T)
                        for h in range(H):
                            bank, j = (h // 4, h % 4) if T == 0 else (h // 2, h % 2)
                            last = mm(ps[:, bank, n * j:n * j + n], q_half[:, h // 2, h % 2, cols(k)],
                                      kT[:, h // 2, key_cols(k // 2, T)], start=True, stop=True)
                        last.then_inc(sig("att_mm"), 1)

                    def values0(a, T):
                        b = (a % 4) // 2
                        tile_pv(a, T, DH, lambda h, c: vt[0:(P if c == 0 else LW), b, T + c, DH * h:DH * h + DH])

                    for k in range(NT + 2):
                        a, T = 4 + 4 * l + k, k % 2
                        if k < NT:
                            if k > 0:
                                pe.wait_ge(sig("att_evac"), a)
                            scores0(a, T)
                        if k >= 2:
                            values0(a - 2, T)
                        if 0 < k <= NT:
                            pe.wait_ge(sig("att_prob"), a)
                            pe.wait_ge(sig("pt_act"), pt_act(a - 1))
                            pe.wait_ge(sig("pt_dve"), pt_act(a - 1))
                            tile_pt(a - 1, 1 - T, keys(1 - T))
                    a = 4 + 4 * l + NT - 1
                    pe.wait_ge(sig("o_copied"), a + 1)
                    for i in range(4):
                        last = mm(ps[:, 0, :], wo[:, l, i, :], oT[:, i, :], start=(i == 0), stop=(i == 3))
                    last.then_inc(sig("f_o"), 1)
                    pe.wait_ge(sig("shifted"), 4 * l + 4)
                    layernorm(2 + l, sh[:, :, :].rearrange("p b t -> p (b t)"))
                    pe.wait_ge(sig("ln_out"), 5 + l)
                    for c in range(3):
                        m, c0 = HC[c], P * c
                        mm(ps[0:m, 3 + c, :], w1[:, l, HID + c0:HID + c0 + m], hT[:, :], start=True, stop=True)\
                          .then_inc(sig("f_g"), 1)
                        mm(ps[0:m, c, :], w1[:, l, c0:c0 + m], hT[:, :], start=True, stop=True).then_inc(sig("f_a"), 1)
                    for c in range(3):
                        m = HC[c]
                        pe.wait_ge(sig("f_hidden"), 3 * l + c + 1)
                        last = mm(ps[:, 6, :], w2[0:m, l, c, :], hh[0:m, c, :], start=(c == 0), stop=(c == 2))
                    last.then_inc(sig("f_down"), 1)

                pe.wait_ge(sig("x_updated"), 4)
                layernorm(4, xT[:, :])
                pe.wait_ge(sig("ln_out"), 8)
                mm(ps[:, 0, :], w1q[:, :], hT[:, :], start=True, stop=True).then_inc(sig("qk1_mm"), 1)
                mm(ps[:, 1, :], w1k[:, :], hT[:, :], start=True, stop=True).then_inc(sig("qk1_mm"), 1)
                for k in range(NT):
                    last = mm(ps[:, 2, cols(k)], hT[:, cols(k)], w1v[:, :], start=True, stop=True)
                last.then_inc(sig("v1_mm"), 1)

                def scores1(u):
                    k = u // 4
                    pe.wait_ge(sig("q_own"), u + 1)
                    if u >= 2:
                        pe.wait_ge(sig("l1_exp"), u - 1)
                    for e in range(4):
                        last = mm(ps[:, 2 * (u % 2) + e // 2, L * (e % 2):L * (e % 2) + L], q_own[:, u % 4, e, :],
                                  k1T[:, bcols(k // 2)], start=True, stop=True)
                    last.then_inc(sig("l1_mm"), 1)

                def turn1(u):
                    pe.wait_ge(sig("l1_exp"), u + 1)
                    for z in (2 * u, 2 * u + 1):
                        if z >= 3:
                            pe.wait_ge(sig("l1_pt_act" if (z - 3) % 2 == 0 else "l1_pt_dve"), (z - 3) // 2 + 1)
                        for i in range(4):
                            e, c = 2 * (z % 2) + i // 2, i % 2
                            last = pe.transpose(ps[:, 4 + z % 3, P * i:P * i + P], probs1(u)[:, e, P * c:P * c + P], ident[:, :])
                        last.then_inc(sig("l1_turned"), 1)

                def values1(u):
                    k, g = u // 4, u % 4
                    pe.wait_ge(sig("l1_pt_act"), u + 1)
                    pe.wait_ge(sig("l1_pt_dve"), u + 1)
                    for e in range(4):
                        for c in range(2):
                            z, i = 2 * u + e // 2, 2 * (e % 2) + c
                            last = mm(ps[32 * g:32 * g + 32, 7, cols(k)], v_own[:, 2 * (k // 2) + c, g, e, :],
                                      PT[:, z % 4, P * i:P * i + P], start=(e == 0 and c == 0), stop=(e == 3 and c == 1))
                    last.then_inc(sig("l1_pv"), 1)

                pe.wait_ge(sig("k1_copied"), 1)
                pe.wait_ge(sig("v1_copied"), 4 * NT)
                for u in range(4 * NT + 2):
                    if u < 4 * NT:
                        scores1(u)
                    if 0 < u <= 4 * NT:
                        turn1(u - 1)
                    if u > 1:
                        values1(u - 2)
                pe.wait_ge(sig("l1_recip"), 1)
                for k in range(NT):
                    last = pe.transpose(ps[0:H1, 0, cols(k)], rl1[:, H1 * k:H1 * k + H1], ident[:, :])
                last.then_inc(sig("l1_recip_turned"), 1)
                pe.wait_ge(sig("l1_recip_copied"), 1)
                mm(ps[:, 1, :], head_rows[:, :], combT[:, :], start=True, stop=True).then_inc(sig("l1_recip_mm"), 1)
                pe.wait_ge(sig("att1_ready"), 1)
                mm(ps[:, 1, :], w1o[:, :], hT[:, :], start=True, stop=True).then_inc(sig("l1_out"), 1)

                pe.wait_ge(sig("x_updated"), 6)
                layernorm(5, xT[:, :])
                pe.wait_ge(sig("ln_out"), 10)
                for k in range(NT):
                    last = mm(ps[:, 7, E1 * k:E1 * k + E1], hT[:, cols(k)], gate_w[:, :], start=True, stop=True)
                last.then_inc(sig("route_mm"), 1)

                def expert_in(e):
                    s = e % 2
                    if e >= 2:
                        pe.wait_ge(sig("e_silu"), e - 1)
                    mm(ps[:, s, :], experts[:, 0, e, :], hT[:, :], start=True, stop=True).then_inc(sig("e_gate"), 1)
                    if e >= 2:
                        pe.wait_ge(sig("e_hidden"), e - 1)
                    mm(ps[:, 2 + s, :], experts[:, 1, e, :], hT[:, :], start=True, stop=True).then_inc(sig("e_up"), 1)

                def expert_weight(e):
                    if e < E1:
                        mm(ps[:, 4 + e % 2, :], bc(ident[0:E1, e], 1, P), combT[:, :], start=True, stop=True)\
                          .then_inc(sig("e_comb"), 1)

                pe.wait_ge(sig("experts_loaded"), 48)
                expert_in(0)
                expert_in(1)
                pe.wait_ge(sig("comb_ready"), 1)
                for k in range(NT):
                    last = pe.transpose(ps[0:E1, 7, cols(k)], rt[:, 6, E1 * k:E1 * k + E1], ident[:, :])
                last.then_inc(sig("comb_turned"), 1)
                pe.wait_ge(sig("comb_copied"), 1)
                expert_weight(0)
                expert_weight(1)
                for e in range(E1 + 1):
                    pe.wait_ge(sig("e_hidden"), e + 1)
                    mm(ps[:, 6, :], experts[:, 2, e, :], moe_h[:, e % 2, :], start=(e == 0), stop=(e == E1))\
                      .then_inc(sig("e_down"), 1)
                    if e + 2 <= E1:
                        expert_in(e + 2)
                        expert_weight(e + 2)
                pe.wait_ge(sig("x_updated"), 8)
                for k in range(NT):
                    last = pe.transpose(ps[:, 7, cols(k)], xT[:, cols(k)], ident[:, :])
                last.then_inc(sig("y_turned"), 1)
                pass_end(pe, "pe")

        @block.gpsimd
        def _(pool):
            pool.wait_ge(sig("setup_done"), 1)
            with pool.Fori(0, PASSES) as it:
                pool.memset(pdiag[:, :, :, :], 0.0).then_inc(sig("pdiag_zero"), 1)
                pool.wait_ge(sig("kvsrc_ready"), 1)
                hi, mid, lo = kv_part
                pool.tensor_copy(hi[:, :, :], kvsrc[:, :, :]).then_inc(sig("kv_split"), 1)
                pool.wait_ge(sig("kv_split"), 1)
                pool.tensor_tensor(kv_rem[:, 0, :, :], kvsrc[:, :, :], hi[:, :, :], ALU.subtract).then_inc(sig("kv_split"), 1)
                pool.wait_ge(sig("kv_split"), 2)
                pool.tensor_copy(mid[:, :, :], kv_rem[:, 0, :, :]).then_inc(sig("kv_split"), 1)
                pool.wait_ge(sig("kv_split"), 3)
                pool.tensor_tensor(kv_rem[:, 1, :, :], kv_rem[:, 0, :, :], mid[:, :, :], ALU.subtract)\
                    .then_inc(sig("kv_split"), 1)
                pool.wait_ge(sig("kv_split"), 4)
                pool.tensor_copy(lo[:, :, :], kv_rem[:, 1, :, :]).then_inc(sig("kv_split"), 1)
                pool.wait_ge(sig("a_out"), 2 * NB)
                pool.memset(q_half[DH:P, :, 0, :], 0.0).then_inc(sig("q_zero"), 1)
                pool.memset(q_half[0:DH, :, 1, :], 0.0).then_inc(sig("q_zero"), 1)
                pool.wait_ge(sig("f_done"), 2)
                pool.memset(v_own[:, :, :, :, :], 0.0).then_inc(sig("v_zero"), 1)
                pool.wait_ge(sig("q1_copied"), 1)
                for u in range(4 * NT):
                    k, g = u // 4, u % 4
                    if u >= 4:
                        pool.wait_ge(sig("l1_mm"), u - 3)
                    pool.tensor_tensor(q_own[:, u % 4, :, :], bc(q1T[:, cols(k)], 1, 4),
                                       bc(own_head[:, 4 * g:4 * g + 4], 2, P), ALU.mult).then_inc(sig("q_own"), 1)
                pool.drain().then_inc(done, 1)
                pool.wait_ge(done, 5)
                pool.sem_clear(done)
                for name in sorted(sems):
                    if name not in SETUP:
                        pool.sem_clear(sems[name])
                for name in sorted(go):
                    pool.sem_inc(go[name], 1)


def lay_out(a):
    f = np.float32
    n = {k: np.asarray(v) for k, v in a.items()}
    o = dict(shape_constants())
    o["x"] = n["L0_attn_x"]
    o["cT"] = np.stack([n["L0_c"].T, n["L1_c"].T], 1)
    o["wmod"] = np.stack([n["L0_wmod"], n["L1_wmod"]], 1)
    o["w_kv"] = np.concatenate([n["L0_attn_W_dkv"], n["L0_attn_W_kr"]], 1)
    o["w_ki"] = np.concatenate([n["L0_attn_idx_wk"]] * 2, 1)
    o["w_qi"] = n["L0_attn_idx_wq"]
    o["w_dq"] = n["L0_attn_W_dq"]
    o["uqT"] = n["L0_attn_W_uq"].reshape(DQ, H, DH).transpose(2, 1, 0)
    o["ukT"] = n["L0_attn_W_uk"].reshape(DC, H, DH).transpose(2, 1, 0)
    o["uvT"] = n["L0_attn_W_uv"].reshape(DC, H, DH).transpose(2, 1, 0)
    o["w_out0"] = n["L0_attn_W_out"].reshape(H, DH, D).transpose(1, 0, 2)
    o["w_q2"] = np.concatenate([n["L0_attn_W_qr"], n["L0_attn_W_qr"]], 1)
    o["idx_w"] = n["L0_attn_idx_w"].reshape(1, IH)
    o["raw_delta"] = n["L0_attn_raw_delta"].reshape(1, DR // 2)
    o["delta_col"] = np.tile(n["L0_attn_raw_delta"], GF // (DR // 2)).reshape(GF, 1)
    qs, ks = n["L0_ffn_q_scale"], n["L0_ffn_k_scale"]
    roll = lambda s: np.roll(s, DH // 2, 1)
    o["qk_scale"] = np.concatenate([qs, ks, roll(qs), roll(ks)], 1).reshape(1, 2 * 4 * DH)
    o["wqkv"] = n["L0_ffn_wqkv"].transpose(1, 0, 2)
    o["wo"] = n["L0_ffn_wo"].reshape(2, 4, P, D).transpose(2, 0, 1, 3)
    o["ln_gb"] = np.stack([n["L0_ffn_ln_g"], n["L0_ffn_ln_b"]], 1).transpose(2, 0, 1)
    o["w1"] = n["L0_ffn_w1"].transpose(1, 0, 2)
    pad = np.zeros((2, 2, 3 * P), f)
    pad[:, :, :HID] = n["L0_ffn_b1"].reshape(2, 2, HID)
    o["b1"] = pad.reshape(2, 2, 3, P).transpose(3, 0, 1, 2)
    pad = np.zeros((2, 3 * P, D), f)
    pad[:, :HID] = n["L0_ffn_w2"]
    o["w2"] = pad.reshape(2, 3, P, D).transpose(2, 0, 1, 3)
    o["b2"] = n["L0_ffn_b2"].T
    w = n["L1_attn_W_qkv"].reshape(H1, 3, D1, D)
    bias = n["L1_attn_b_qkv"].reshape(H1, 3, D1)
    for i, name in ((0, "q"), (1, "k")):
        o["w1" + name] = w[:, i].reshape(D, D).T
        o["b1" + name] = bias[:, i].reshape(D, 1)
    o["w1v"] = w[:, 2].reshape(D, D).T
    o["b1v"] = bias[:, 2].reshape(D, 1)
    o["w1o"] = n["L1_attn_W_out"].T
    o["b1o"] = n["L1_attn_b_out"].reshape(D, 1)
    o["gate_w"] = n["L1_ffn_gate_w"].T
    o["e_bias"] = n["L1_ffn_expert_bias"].reshape(1, E1)
    both = [np.concatenate([n["L1_ffn_w_" + name], n[f"L1_ffn_shared_{name}_w"][None]], 0)
            for name in ("gate", "up", "down")]
    o["experts"] = np.stack(both, 0).transpose(3, 0, 1, 2)
    return {k: np.ascontiguousarray(v) for k, v in o.items()}


def kernel(**inputs):
    import concourse.bacc as bacc
    from concourse.bass_utils import run_bass_kernel_spmd

    nc = bacc.Bacc("TRN2", target_bir_lowering=False, num_devices=1)
    arrays = lay_out(inputs)
    A = {k: nc.dram_tensor("in_" + k, v.shape, mybir.dt.from_np(v.dtype), kind="ExternalInput").ap()
         for k, v in arrays.items()}
    out = nc.dram_tensor("out_x", (B, L, D), F32, kind="ExternalOutput").ap()
    idx = nc.dram_tensor("idx_scratch", (NB, GT * RANKS), BF16, kind="Internal").ap()
    scores = nc.dram_tensor("score_scratch", (NB, 3, P * 512), F32, kind="Internal").ap()
    program(nc, A, out, idx, scores)
    r = run_bass_kernel_spmd(nc, [{"in_" + k: v for k, v in arrays.items()}], core_ids=[0])
    return r.results[0]["out_x"]
```

```python
import math
from contextlib import ExitStack

import numpy as np

import concourse.bass as bass
from concourse import mybir

F32 = mybir.dt.float32
BF16 = mybir.dt.bfloat16
U32 = mybir.dt.uint32
ALU = mybir.AluOpType
ACT = mybir.ActivationFunctionType
AX = mybir.AxisListType

P = 128
B, L, D = 8, 256, 128
NB = 2
PASSES = B // NB
NT = NB * L // P
W = NB * L
H, DH, DR, DC, DQ = 8, 64, 32, 32, 64
IH = 4
LW, RANKS = 64, 32
GT = L - LW
GP = 4
NG = GT // GP
GF = DC + 2 * DR
WIN = 64
HID = 341
SETUP = ("weights_loaded", "late_loaded", "cols_set", "setup_exp", "c_act_ready", "delta_ready", "delta_sin", "mod_mm", "absorb_mm",
         "setup_done", "dve_setup_step", "act_setup_step")
ACROSS = ("x_loaded", "y_stored")
HC = [128, 128, 85]
E1, TOPK = 16, 8
H1, D1 = 16, 8
WMAX = 192
EXCLUDED, FORWARD, TAKEN = -3.0e38, -1.0e30, -3.4e38
MASKED = -1.0e30
SCALE_A = float(DH + DR) ** -0.5
SCALE_1 = 1.0 / math.sqrt(D1)
ROUTE = 2.826
PACKED = {"ident": (P,), "mask_a": (P + WMAX,), "mask_w": (P + WMAX,), "mask_i": (LW + RANKS + WMAX,),
          "source": (2,), "cT": (2, B), "w_kv": (DC + DR,), "w_ki": (2 * DH,), "w_qi": (IH * DH,), "w_dq": (DQ,),
          "ln_gb": (2, 2), "b1": (2, 2, 3), "b2": (2,), "w1q": (P,), "w1k": (P,), "b1q": (1,), "b1k": (1,),
          "own_head": (H1,), "w1v": (D,), "b1v": (1,), "w1o": (D,), "b1o": (1,), "gate_w": (E1,)}
PACKED_LOADS = 2
LN_AND_EXP = "natural_log_exp_and_others"
LN_SHIFT = 65536.0


def shape_constants():
    f = np.float32
    c = {}
    c["ident"] = np.eye(P, dtype=f)
    theta = (1.0 / np.float32(10000.0) ** (2.0 * np.arange(DR // 2, dtype=f) / DR)).astype(f)
    pos = np.arange(L)
    turned = np.where(pos < LW, pos, 2 * pos - (LW - 1))
    ang = np.stack([turned, pos, pos]).astype(f)[:, :, None] * theta
    ang = ang.reshape(3, 2, P, DR // 2).transpose(2, 0, 1, 3).reshape(P, 6, DR // 2).astype(np.float64)
    c["rope_cos"], c["rope_sin"] = np.cos(ang).astype(f), np.sin(ang).astype(f)
    rank = np.arange(LW, LW + RANKS).astype(f)[None, :] * np.tile(theta, 2)[:, None]
    rank = rank.astype(np.float64)
    one = np.ones((DC, RANKS))
    c["rank_a"] = np.concatenate([one, np.cos(rank), np.sin(rank)]).astype(f)
    c["rank_b"] = np.concatenate([one, -np.sin(rank), np.cos(rank)]).astype(f)
    half = np.arange(0, DH, 2, dtype=f)
    inv = (1.0 / np.float32(10000.0) ** (half / DH)).astype(f)
    fr = (np.arange(L, dtype=f)[:, None] * inv[None, :]).astype(np.float64)
    fr = np.concatenate([fr, fr], 1)
    base = ((half + 0.4 * DH) / (1.4 * DH)).astype(np.float64)
    power = (np.arange(L) - L // 2) / float(WIN // 2)
    sc = base[None, :] ** power[:, None]
    sc = np.concatenate([sc, sc], 1)
    sign = np.concatenate([-np.ones(DH // 2), np.ones(DH // 2)])
    x = np.stack([np.cos(fr) * sc, np.cos(fr) / sc, np.sin(fr) * sc * sign, np.sin(fr) / sc * sign], 1)
    c["xpos"] = x.reshape(2, P, 4 * DH).transpose(1, 0, 2).astype(f)
    i = np.arange(P)[:, None]
    j0, j1 = np.arange(P)[None, :], LW + np.arange(WMAX)[None, :]
    ok0 = np.where(i < LW, j0 < LW + RANKS, (j0 <= i) & (j0 > i - LW))
    ok1 = (j1 <= i + P) & (j1 > i + P - LW)
    c["mask_a"] = np.where(np.concatenate([ok0, ok1], 1), 0, MASKED).astype(f)
    ok0 = (j0 <= i) & (j0 >= i - WIN)
    ok1 = (j1 <= i + P) & (j1 >= i + P - WIN)
    c["mask_w"] = np.where(np.concatenate([ok0, ok1], 1), 0, MASKED).astype(f)
    s0, s1 = np.arange(LW + RANKS)[None, :], np.arange(WMAX)[None, :]
    m0 = np.where(s0 < LW, np.where(s0 <= i - LW, 0, EXCLUDED), np.where(s0 > i, FORWARD, EXCLUDED))
    m0[:LW] = 0
    m1 = np.where(s1 <= i + P - LW, 0, EXCLUDED)
    c["mask_i"] = np.concatenate([m0, m1], 1).astype(f)
    head = (np.arange(P)[:, None] // D1 == np.arange(H1)[None, :]).astype(f)
    c["own_head"], c["head_rows"] = head, head.T
    c["pick"] = np.tile(np.eye(E1, dtype=f), (3, 1))
    c["source"] = (np.arange(P)[:, None] + np.array([[0, P]])).astype(f)
    return c


class Steps:

    def __init__(self, eng, sem):
        self.eng, self.sem, self.n = eng, sem, 0

    def mark(self, ins):
        ins.then_inc(self.sem, 1)
        self.n += 1
        return self.n

    def wait(self, n=None):
        self.eng.wait_ge(self.sem, self.n if n is None else n)

    def link(self, ins):
        self.mark(ins)
        self.wait()


def program(nc, A, out, idx_scratch, score_scratch):
    ctx = ExitStack()
    with ctx:
        def sb(name, shape, dt=F32):
            return ctx.enter_context(nc.sbuf_tensor(name, shape, dt))

        done = ctx.enter_context(nc.semaphore("pass_done"))
        go = {n: ctx.enter_context(nc.semaphore("go_" + n)) for n in ("sp", "act", "dve", "pe")}
        sems = {}

        def sig(name):
            if name not in sems:
                sems[name] = ctx.enter_context(nc.semaphore(name))
            return sems[name]

        SAf = sb("SAf", [P, 4096])
        loads = []
        late_loads = []

        def weight(name, shape, to=loads):
            t = sb("w_" + name, shape)
            to.append((t[tuple(slice(None) for _ in shape)], A[name]))
            return t

        width = {name: math.prod(shape) for name, shape in PACKED.items()}
        all_packed = sb("packed", [P, sum(width.values())])
        for i in range(PACKED_LOADS):
            part = slice(*(sum(width.values()) * j // PACKED_LOADS for j in (i, i + 1)))
            loads.append((all_packed[:, part], A["packed"][:, part]))

        def packed(name):
            first = sum(width[n] for n in list(PACKED)[:list(PACKED).index(name)])
            view = all_packed[:, first:first + width[name]]
            axes = "abc"[:len(PACKED[name])]
            return view.rearrange(f"p ({' '.join(axes)}) -> p {' '.join(axes)}", **dict(zip(axes, PACKED[name])))

        ident = packed("ident")
        rank_a = weight("rank_a", [GF, RANKS])
        rank_b = weight("rank_b", [GF, RANKS])
        mask_a = packed("mask_a")
        mask_w = packed("mask_w")
        mask_i = packed("mask_i")
        source = packed("source")
        cT = packed("cT")
        w_kv = packed("w_kv")
        w_ki = packed("w_ki")
        w_qi = packed("w_qi")
        w_dq = packed("w_dq")
        w_q2 = weight("w_q2", [DQ, H * DC + H * DR])
        idx_w = sb("idx_w", [P, IH])
        delta_row = sb("delta_row", [P, DR // 2])
        delta_col = weight("delta_col", [GF, 1])
        wqkv = weight("wqkv", [P, 2, 3 * H * DH], late_loads)
        wo = weight("wo", [P, 2, 4, D], late_loads)
        ln_gb = packed("ln_gb")
        w1 = weight("w1", [P, 2, 2 * HID], late_loads)
        b1 = packed("b1")
        w2 = weight("w2", [P, 2, 3, D], late_loads)
        b2 = packed("b2")
        w1q = packed("w1q")
        w1k = packed("w1k")
        b1q = packed("b1q")
        b1k = packed("b1k")
        pick = weight("pick", [3 * E1, E1])
        pick_bf = sb("pick_bf", [3 * E1, E1], BF16)
        own_head = packed("own_head")
        head_rows = weight("head_rows", [H1, P])
        w1v = packed("w1v")
        b1v = packed("b1v")
        w1o = packed("w1o")
        b1o = packed("b1o")
        gate_w = packed("gate_w")
        e_bias = sb("e_bias", [P, E1])
        region = sb("region", [P, 3 * (E1 + 1) * P])
        experts = region[:, :].rearrange("p (s e n) -> p s e n", s=3, e=E1 + 1)
        parts = np.cumsum([0, NB * NG * DC, NG * GP * H, 3 * 512, 3 * P]).tolist()
        gathT = region[:, parts[0]:parts[1]].rearrange("p (b g c) -> p b g c", b=NB, g=NG)
        pdiag = region[:, parts[1]:parts[2]].rearrange("p (g t h) -> p g t h", g=NG, t=GP)
        gsc = region[:, parts[2]:parts[3]].rearrange("p (i n) -> p i n", i=3)
        xg = region[:, parts[3]:parts[4]].rearrange("p (i n) -> p i n", i=3)
        big = sb("big", [P, 2048])
        wmod = SAf[:, 0:12 * D].rearrange("p (l n) -> p l n", l=2)
        uqT = SAf[0:DH, 1536:2048].rearrange("p (h n) -> p h n", h=H)
        ukT = SAf[0:DH, 2048:2304].rearrange("p (h n) -> p h n", h=H)
        uvT = SAf[0:DH, 2304:2560].rearrange("p (h n) -> p h n", h=H)
        w_out0 = SAf[0:DH, 2560:3584].rearrange("p (h n) -> p h n", h=H)
        xpos = SAf[:, 3584:4096].rearrange("p (t n) -> p t n", t=2)
        qk_scale = big[:, 0:512].rearrange("p (l n) -> p l n", l=2)
        rope_cos = big[:, 512:608].rearrange("p (i n) -> p i n", i=6)
        rope_sin = big[:, 608:704].rearrange("p (i n) -> p i n", i=6)
        rope_t = big[:, 704:896].rearrange("p (s i n) -> p s i n", s=2, i=6)
        for name, t in (("xpos", xpos), ("rope_cos", rope_cos), ("rope_sin", rope_sin), ("wmod", wmod), ("uqT", uqT), ("ukT", ukT), ("uvT", uvT), ("w_out0", w_out0)):
            loads.append((t, A[name]))
        rows = [(idx_w, A["idx_w"]), (delta_row, A["raw_delta"]), (qk_scale, A["qk_scale"]), (e_bias, A["e_bias"])]

        b1out = sb("b1out", [P, 1])
        mean_mat = sb("mean_mat", [P, P])
        eps_col = sb("eps_col", [P, 1])
        one_col = sb("one_col", [P, 1])
        shift_col = sb("shift_col", [P, 1])
        modT = sb("modT", [P, 12, B])
        c_act = sb("c_act", [P, 2, B])
        c_den = sb("c_den", [P, 2, B])
        mod_tmp = sb("mod_tmp", [P, 2, B])
        ang = sb("ang", [P, 8, DR // 2])
        ropeC = sb("ropeC", [P, 6, DR])
        ropeS = sb("ropeS", [P, 6, DR])
        dcol = sb("dcol", [GF, 8])
        rank_tab = sb("rank_tab", [GF, RANKS])
        rank_t = sb("rank_t", [GF, RANKS])
        xtab = sb("xtab", [P, 2, 2, 4 * DH])
        w_vo = sb("w_vo", [DC, H, D])
        w_vo4 = sb("w_vo4", [P, 2, D])

        x_tok = sb("x_tok", [P, NT, D])
        xT = sb("xT", [P, W])
        fT = sb("fT", [P, W])
        hT = sb("hT", [P, W])
        sh = sb("sh", [P, NB, L])
        mod = sb("mod", [P, 12, NB])
        cqT = sb("cqT", [DQ, W])
        kvsrc = sb("kvsrc", [P, NT, GF])
        ckv_b = sb("ckv_b", [P, NB, DC])
        ckv_c = sb("ckv_c", [LW, NB, DC])
        kr_abs = sb("kr_abs", [P, NT, DR])
        kr_raw = sb("kr_raw", [P, NT, DR])
        ka = sb("ka", [P, NT, 2, DC + DR])
        kaT = sb("kaT", [P, 2, W])
        kv_part = [sb(n, [P, NT, GF], BF16) for n in ("kv_hi", "kv_mid", "kv_lo")]
        xc, sq, rstd = big[:, 0:W], big[:, W:2 * W], big[:, 2 * W:3 * W]
        kv_rem = big[:, 0:2 * NT * GF].rearrange("p (s k n) -> p s k n", s=2, k=NT)
        qa = [sb("qa", [P, H * (DC + DR)]), big[:, 1024:1024 + H * (DC + DR)]]
        qa = [t[:, 0:H * (DC + DR)].rearrange("p (h n) -> p h n", h=H) for t in qa]
        qb = [t[:, 0:H * GF].rearrange("p (h n) -> p h n", h=H) for t in (sb("qb", [P, H * GF]), SAf)]
        queries = sb("queries", [P, 4 * W + NB * GT * H])
        qaT = queries[:, 0:4 * W].rearrange("p (i n) -> p i n", i=4)
        qbT = queries[0:GF, 4 * W:].rearrange("p (b t h) -> p b t h", b=NB, h=H)
        q_half = queries[:, 0:H * W].rearrange("p (i s n) -> p i s n", i=4, s=2)
        iscore = sb("iscore", [P, NB, LW + RANKS + WMAX])
        top8 = sb("top8", [P, NT, RANKS])
        topi = sb("topi", [P, NT, RANKS], U32)
        topb = sb("topb", [P, NT, RANKS], BF16)
        kto = sb("kto", [P, 4096])
        irel = kto[:, 1024:4096].rearrange("p (k h n) -> p k h n", k=NT, h=IH)
        hot0 = kto[:, 0:3072].bitcast(BF16)
        oTa = kto[:, 3072:4096].rearrange("p (i n) -> p i n", i=2)
        kT = kto[:, 0:2048].rearrange("p (i n) -> p i n", i=4)
        k1T, q1T = kto[:, 0:W], kto[:, W:2 * W]
        q_own = kto[:, 2 * W:6 * W].rearrange("p (s h n) -> p s h n", s=4, h=4)
        oT = kto[:, 2048:4096].rearrange("p (i n) -> p i n", i=4)
        hot1 = big[:, 0:LW * RANKS // 2].bitcast(BF16)
        wide = sb("wide", [P, GT * RANKS])
        gath = wide[0:GF, :]
        idxb = [wide[:, 3072:6144].bitcast(BF16), SAf[:, 1024:4096].bitcast(BF16)]
        og = wide[0:DC, 0:GT * H].rearrange("p (t h) -> p t h", h=H)
        qiT = wide[:, 0:1024].rearrange("p (i n) -> p i n", i=2)
        kiT = wide[:, 1024:1536]
        vt = wide[:, 0:3072].rearrange("p (b c n) -> p b c n", b=NB, c=3)
        hh = wide[:, 3072:4608].rearrange("p (c n) -> p c n", c=3)
        qk_own = [big[:, 0:1024]] + [wide[:, c:c + 1024] for c in (3072, 4096, 5120)]
        v_own = wide[:, 0:NT * H1 * 32].rearrange("p (k g j n) -> p k g j n", k=NT, g=4, j=4)
        moe_g = wide[:, 2048:3072].rearrange("p (s n) -> p s n", s=2)
        moe_h = wide[:, 3072:4096].rearrange("p (s n) -> p s n", s=2)
        PT = sb("PT", [P, 4, 512])
        qk_part = [PT[:, 2 * s:2 * s + 2, :].rearrange("p u n -> p (u n)") for s in range(2)]
        mx = sb("mx", [P, 16, H])
        nb = sb("nb", [P, 16, H])
        ls = sb("ls", [P, 16, H])
        rl = sb("rl", [P, 16, H])
        ssq = sb("ssq", [P, NT, 2 * H])
        rs = sb("rs", [P, NT, 2 * H])
        cqs = sb("cqs", [P, NT, H])
        rt = sb("rt", [P, 8, NT * E1])
        rsm = sb("rsm", [P, 4 * NT + 8 * NT])
        combT = sb("combT", [E1, W])
        ps = ctx.enter_context(nc.psum_tensor("ps", [P, 8, 512], F32))

        def pass_end(eng, name):
            eng.drain().then_inc(done, 1)
            eng.wait_ge(go[name], 1)
            eng.sem_clear(go[name])

        def cols(k):
            return slice(P * k, P * k + P)

        def bcols(b):
            return slice(L * b, L * b + L)

        def keys(T):
            return P if T == 0 else WMAX

        def key_cols(b, T):
            return slice(L * b, L * b + P) if T == 0 else slice(L * b + LW, L * b + L)

        def SA(a, T, width):
            if a < 4 and a >= 2:
                first = GT * H + (a - 2) * H * (P + RANKS)
                flat = wide[:, first:first + H * width]
            else:
                flat = SAf[:, 2048 * T:2048 * T + H * width]
            return flat.rearrange("p (h n) -> p h n", h=H)

        def bc(ap, axis, n):
            v = ap.unsqueeze(axis)
            shape = list(v.shape)
            shape[axis] = n
            return v.broadcast_to(shape)

        q_tmp = [[PT[:, 2 * s + i // 2, 256 * (i % 2):256 * (i % 2) + 256] for i in range(4)] for s in range(2)]
        comb3 = big[:, 1536:1536 + NT * 3 * E1].rearrange("p (k s e) -> p k s e", k=NT, s=3)
        comb_part = big[:, 1792:1824].bitcast(BF16)
        comb_rem = big[:, 1856:1920]
        y_tok = PT[:, 3, :].rearrange("p (k n) -> p k n", k=NT)
        combS = PT[0:3 * E1, 0, 0:W // 2].bitcast(BF16)
        ls1, rl1 = (t[:, 0:8, :].rearrange("p u h -> p (u h)") for t in (ls, rl))

        def probs1(u):
            return SAf[:, 1024 * (u % 4):1024 * (u % 4) + 1024].rearrange("p (e n) -> p e n", e=4)

        def turned_copy1(eng, u, which, done_):
            z = 2 * u + which
            eng.wait_ge(sig("l1_turned"), z + 1)
            if u >= 2:
                eng.wait_ge(sig("l1_pv"), u - 1)
            if which == 0:
                ins = eng.activation(PT[:, z % 4, :], ps[:, 4 + z % 3, :], ACT.Copy)
            else:
                ins = eng.tensor_copy(PT[:, z % 4, :], ps[:, 4 + z % 3, :])
            ins.then_inc(sig(done_), 1)

        def turn_bank(a, u):
            return (4, 5, 4, 5)[u] if a < 4 else (4, 5, 6, 5)[u]

        UNITS = {0: [(0, 0), (4, 0)], 1: [(0, 0), (0, 1), (4, 0), (4, 1)]}
        UNITS_BEFORE = [0, 2, 6, 8]

        block = ctx.enter_context(nc.Block())

        @block.sync
        def _(sp):
            for dst, src in loads:
                sp.dma_start(dst, src).then_inc(sig("weights_loaded"), 16)
            for dst, src in rows:
                n = dst.shape[-1] if len(dst.shape) == 2 else dst.shape[1] * dst.shape[2]
                flat = dst[:, :] if len(dst.shape) == 2 else dst[:, :, :].rearrange("p a n -> p (a n)")
                sp.dma_start(flat, src.to_broadcast([P, n])).then_inc(sig("weights_loaded"), 16)
            src = A["x"][0:NB, :, :].rearrange("b (t p) d -> p (b t) d", p=P)
            sp.dma_start(x_tok[:, :, :], src).then_inc(sig("x_loaded"), 16)
            for dst, src in late_loads:
                sp.dma_start(dst, src).then_inc(sig("late_loaded"), 16)
            sp.sem_inc(sig("y_stored"), 16)
            with sp.Fori(0, PASSES) as it:
                sp.wait_ge(sig("x_turned"), 1)
                src = A["x"][bass.ds(NB * it + NB, NB), :, :].rearrange("b (t p) d -> p (b t) d", p=P)
                sp.dma_start(x_tok[:, :, :], src).then_inc(sig("x_loaded"), 16)
                for b in range(NB):
                    sp.wait_ge(sig("top_ready"), 2 * b + 2)
                    first = LW * RANKS
                    sp.dma_start(idx_scratch[b, 0:first].rearrange("(p r) -> p r", r=RANKS),
                                 topb[LW:P, 2 * b, :]).then_inc(sig(f"idx_saved{b}"), 16)
                    sp.dma_start(idx_scratch[b, first:].rearrange("(p r) -> p r", r=RANKS),
                                 topb[:, 2 * b + 1, :]).then_inc(sig(f"idx_saved{b}"), 16)
                    sp.wait_ge(sig(f"idx_saved{b}"), 32)
                    sp.dma_start(idxb[b], idx_scratch[b:b + 1, :].to_broadcast([P, GT * RANKS]))\
                      .then_inc(sig(f"idx_spread{b}"), 16)

                def save_scores(b):
                    for n in range(3):
                        sp.wait_ge(sig("gsc_ready"), 3 * b + n + 1)
                        to = score_scratch[b, n, :].rearrange("(m q c) -> q m c", q=4, c=512)
                        sp.dma_start(to, gsc[:, n, :]).then_inc(sig("gsc_saved"), 16)

                def scores_back(b, T):
                    sp.wait_ge(sig("gsc_saved"), 48 * (b + 1))
                    sp.wait_ge(sig("hot_ready"), 2 * NB)
                    if b > 0:
                        sp.wait_ge(sig("gathT_mm"), 3 * NB)
                    for n in ([0] if T == 0 else [1, 2]):
                        p0 = LW if n == 0 else LW * (n - 1)
                        for t in range(GP):
                            own = score_scratch[b, n, :].rearrange("(t h g u r) -> t u g h r", t=GP, h=H, g=16, u=GP)
                            sp.dma_start(SA(2 * b + T, T, keys(T) + RANKS)[p0 + t:p0 + LW:GP, :, keys(T):], own[t, t])\
                              .then_inc(sig(f"gsc_back_{b}_{T}"), 16)

                def probs_out(b, T):
                    sp.wait_ge(sig("att_prob"), 2 * (2 * b + T + 1))
                    if b > 0:
                        sp.wait_ge(sig("xg_turned"), b)
                    for n in ([0] if T == 0 else [1, 2]):
                        p0 = LW if n == 0 else LW * (n - 1)
                        for t in range(GP):
                            sp.dma_start(xg[:, n, RANKS * t:RANKS * t + RANKS],
                                         SA(2 * b + T, T, keys(T) + RANKS)[p0 + t:p0 + LW:GP, :, keys(T):])\
                              .then_inc(sig(f"xg_loaded{T}"), 16)

                save_scores(0)
                scores_back(0, 0)
                scores_back(0, 1)
                save_scores(1)
                scores_back(1, 0)
                scores_back(1, 1)
                for b in range(NB):
                    for T in range(2):
                        probs_out(b, T)
                sp.wait_ge(sig("a_out"), 2 * NB)
                for i in range(3):
                    sp.dma_start(experts[:, i, :, :], A["experts"][:, i, :, :]).then_inc(sig("experts_loaded"), 16)
                sp.wait_ge(sig("y_ready"), 1)
                dst = out[bass.ds(NB * it, NB), :, :].rearrange("b (t p) d -> p (b t) d", p=P)
                sp.dma_start(dst, y_tok[:, :, :]).then_inc(sig("y_stored"), 16)
                pass_end(sp, "sp")
            sp.wait_ge(sig("y_stored"), 16)
            sp.wait_ge(sig("x_loaded"), 16)

        @block.vector
        def _(dve):
            st = Steps(dve, sig("dve_setup_step"))
            dve.memset(mean_mat[:, :], 1.0 / P).then_inc(sig("cols_set"), 1)
            dve.memset(eps_col[:, :], 1e-5).then_inc(sig("cols_set"), 1)
            dve.memset(one_col[:, :], 1.0).then_inc(sig("cols_set"), 1)
            dve.memset(shift_col[:, :], 0.5 * math.log(LN_SHIFT)).then_inc(sig("cols_set"), 1)
            st.mark(dve.memset(sh[:, :, :], 0.0))
            st.mark(dve.memset(kaT[:, :, :], 0.0))
            dve.wait_ge(sig("weights_loaded"), 16 * (len(loads) + len(rows)))
            dve.wait_ge(sig("setup_exp"), 3)
            st.link(dve.tensor_scalar(c_den[:, :, :], c_den[:, :, :], 1.0, None, ALU.add))
            st.link(dve.reciprocal(c_act[:, :, :], c_den[:, :, :]))
            dve.tensor_tensor(c_act[:, :, :], c_act[:, :, :], cT[:, :, :], ALU.mult).then_inc(sig("c_act_ready"), 1)
            for t in (ang[:, 0:5, :], dcol[:, 0:5].unsqueeze(2)):
                st.link(dve.tensor_scalar(t[:, 1, :], t[:, 0, :], 1.0, None, ALU.add))
                st.link(dve.reciprocal(t[:, 2, :], t[:, 1, :]))
                st.link(dve.tensor_scalar(t[:, 3, :], t[:, 2, :], -2.0 * math.pi, math.pi, ALU.mult, ALU.add))
                dve.tensor_scalar(t[:, 4, :], t[:, 3, :], 0.5, None, ALU.mult).then_inc(sig("delta_ready"), 1)
            dve.wait_ge(sig("delta_sin"), 4)
            for t in (ang, dcol[:, :].unsqueeze(2)):
                st.link(dve.tensor_scalar(t[:, 5, :], t[:, 5, :], -1.0, None, ALU.mult))
                st.link(dve.tensor_tensor(t[:, 7, :], t[:, 6, :], t[:, 6, :], ALU.mult))
                st.link(dve.tensor_scalar(t[:, 6, :], t[:, 7, :], 2.0, -1.0, ALU.mult, ALU.add))
            sd, cd = bc(ang[:, 5, :], 1, 6), bc(ang[:, 6, :], 1, 6)
            hd = DR // 2
            st.mark(dve.tensor_tensor(rope_t[:, 0, :, :], rope_cos[:, :, :], cd, ALU.mult))
            st.link(dve.tensor_tensor(rope_t[:, 1, :, :], rope_sin[:, :, :], sd, ALU.mult))
            st.link(dve.tensor_tensor(ropeC[:, :, 0:hd], rope_t[:, 0, :, :], rope_t[:, 1, :, :], ALU.subtract))
            st.mark(dve.tensor_copy(ropeC[:, :, hd:DR], ropeC[:, :, 0:hd]))
            st.mark(dve.tensor_tensor(rope_t[:, 0, :, :], rope_sin[:, :, :], cd, ALU.mult))
            st.link(dve.tensor_tensor(rope_t[:, 1, :, :], rope_cos[:, :, :], sd, ALU.mult))
            st.link(dve.tensor_tensor(ropeS[:, :, hd:DR], rope_t[:, 0, :, :], rope_t[:, 1, :, :], ALU.add))
            st.mark(dve.tensor_scalar(ropeS[:, 0:4, 0:hd], ropeS[:, 0:4, hd:DR], -1.0, None, ALU.mult))
            st.mark(dve.tensor_copy(ropeS[:, 4:6, 0:hd], ropeS[:, 4:6, hd:DR]))
            st.link(dve.tensor_scalar(rank_t[:, :], rank_a[:, :], dcol[:, 6:7], None, ALU.mult))
            st.link(dve.scalar_tensor_tensor(rank_tab[:, :], rank_b[:, :], dcol[:, 5:6], rank_t[:, :], ALU.mult, ALU.add))
            st.mark(dve.memset(rank_tab[0:DC, :], 1.0))
            for l in range(2):
                for T in range(2):
                    st.mark(dve.tensor_tensor(xtab[:, l, T, :], xpos[:, T, :], qk_scale[:, l, :], ALU.mult))
            dve.wait_ge(sig("mod_mm"), 1)
            st.link(dve.tensor_copy(modT[:, :, :], ps[:, 0, 0:12 * B].rearrange("p (j b) -> p j b", b=B)))
            for j in (1, 4, 7, 10):
                st.mark(dve.tensor_scalar(modT[:, j, :], modT[:, j, :], 1.0, None, ALU.add))
            for j in (2, 5, 8, 11):
                st.mark(dve.tensor_scalar(mod_tmp[:, 0, :], modT[:, j, :], 0.0, None, ALU.is_ge))
                st.link(dve.scalar_tensor_tensor(mod_tmp[:, 1, :], modT[:, j, :], -1.0, modT[:, j, :], ALU.mult, ALU.max))
                st.link(dve.tensor_scalar(mod_tmp[:, 1, :], mod_tmp[:, 1, :], 0.25, None, ALU.max))
                st.link(dve.tensor_scalar(mod_tmp[:, 0, :], mod_tmp[:, 0, :], 2.0, -1.0, ALU.mult, ALU.add))
                st.link(dve.tensor_tensor(modT[:, j, :], mod_tmp[:, 0, :], mod_tmp[:, 1, :], ALU.mult))
            st.mark(dve.tensor_copy(pick_bf[:, :], pick[:, :]))
            dve.wait_ge(sig("absorb_mm"), 4)
            st.mark(dve.tensor_tensor(b1out[:, :], ps[:, 5, 0:1], b1o[:, :], ALU.add))
            st.mark(dve.tensor_copy(w_q2[:, 0:H * DC], ps[0:DQ, 1, 0:H * DC]))
            for h in range(H):
                st.mark(dve.tensor_copy(w_vo[:, h, :], ps[0:DC, 2 + h // 4, D * (h % 4):D * (h % 4) + D]))
            dve.tensor_copy(w_vo4[:, :, :], ps[:, 4, 0:2 * D].rearrange("p (i n) -> p i n", i=2))\
               .then_inc(sig("setup_done"), 1)
            dve.wait_ge(sig("setup_done"), 1)

            with dve.Fori(0, PASSES) as it:
                st = Steps(dve, sig("dve_step"))
                st.link(dve.tensor_copy(mod[:, :, :], modT[:, :, bass.ds(NB * it, NB)]))

                def layernorm(n, src, modulate):
                    for b in range(NB):
                        dve.wait_ge(sig("ln_mean"), 2 * n + b + 1)
                        dve.tensor_tensor(xc[:, bcols(b)], src[:, bcols(b)], ps[:, b, 0:L], ALU.subtract)\
                           .then_inc(sig("ln_centered"), 1)
                    dve.wait_ge(sig("ln_centered"), 2 * n + 2)
                    for b in range(NB):
                        dve.wait_ge(sig("ln_rstd"), 2 * n + b + 1)
                        st.link(dve.tensor_tensor(xc[:, bcols(b)], xc[:, bcols(b)], rstd[:, bcols(b)], ALU.mult))
                        modulate(b).then_inc(sig("ln_out"), 1)

                def by_batch(c, s, dst):
                    return lambda b: dve.tensor_scalar(dst[:, bcols(b)], xc[:, bcols(b)], mod[:, c, b:b + 1],
                                                       mod[:, s, b:b + 1], ALU.mult, ALU.add)

                def tile_scores(a, T, width, mask, factor, ready=None):
                    n, off = keys(T), P * T
                    for half in range(2):
                        for bank in (2 * half, 2 * half + 1):
                            dve.wait_ge(sig("att_mm"), 4 * a + bank + 1)
                            ins = dve.tensor_tensor(SA(a, T, width)[:, 2 * bank:2 * bank + 2, 0:n],
                                                    ps[:, bank, 0:2 * n].rearrange("p (h n) -> p h n", h=2),
                                                    bc(mask[:, off:off + n], 1, 2), ALU.add)
                            ins.then_inc(sig("att_evac"), 1)
                        if ready is not None and half == 0:
                            dve.wait_ge(*ready)
                        dve.wait_ge(sig("att_evac"), 4 * a + 2 * half + 2)
                        hs = slice(4 * half, 4 * half + 4)
                        st.link(dve.tensor_reduce(mx[:, a % 4, hs], SA(a, T, width)[:, hs, :], AX.X, ALU.max))
                        if factor is None:
                            ins = dve.tensor_scalar(nb[:, a % 4, hs], mx[:, a % 4, hs], -SCALE_A, None, ALU.mult)
                        else:
                            ins = dve.scalar_tensor_tensor(nb[:, a % 4, hs], mx[:, a % 4, hs], -1.0, factor[:, hs],
                                                           ALU.mult, ALU.mult)
                        ins.then_inc(sig("att_bias"), 1)

                def tile_norm(a, T, width):
                    for half in range(2):
                        hs = slice(4 * half, 4 * half + 4)
                        dve.wait_ge(sig("att_exp"), 2 * a + half + 1)
                        st.link(dve.reciprocal(rl[:, a % 4, hs], ls[:, a % 4, hs]))
                        v = SA(a, T, width)[:, hs, :]
                        dve.tensor_tensor(v, v, bc(rl[:, a % 4, hs], 2, width), ALU.mult).then_inc(sig("att_prob"), 1)

                def tile_pt(a, T):
                    for u in range(len(UNITS[T])):
                        if u % 2:
                            dve.wait_ge(sig("pt_mm"), 12 * (a // 4) + UNITS_BEFORE[a % 4] + u + 1)
                            rows_ = P if UNITS[T][u][1] == 0 else LW
                            dve.tensor_copy(PT[0:rows_, u, :], ps[0:rows_, turn_bank(a, u), :]).then_inc(sig("pt_dve"), 1)

                dve.wait_ge(sig("xT_copied"), 1)
                layernorm(0, xT[:, :], by_batch(1, 0, hT))
                dve.wait_ge(sig("kr_abs"), 1)
                kvp = ps[:, 6, 0:NT * (DC + DR)].rearrange("p (k n) -> p k n", k=NT)
                n = NT * (DC + DR)
                st.mark(dve.tensor_copy(kr_raw[:, :, :], kvp[:, :, DC:]))
                st.mark(dve.tensor_copy(kvsrc[:, :, 0:DC], kvp[:, :, 0:DC]))
                st.mark(dve.tensor_copy(ckv_b[:, :, :], ps[:, 6, n:n + NB * DC].rearrange("p (b n) -> p b n", b=NB)))
                n += NB * DC
                st.link(dve.tensor_copy(ckv_c[:, :, :], ps[0:LW, 6, n:n + NB * DC].rearrange("p (b n) -> p b n", b=NB)))
                dve.wait_ge(sig("kr_log"), 1)
                st.link(dve.scalar_tensor_tensor(kvsrc[:, :, DC:2 * DC], kr_raw[:, :, :], 0.0, kr_abs[:, :, :],
                                                 ALU.max, ALU.add))
                st.mark(dve.tensor_scalar(kvsrc[:, :, 64:80], kvsrc[:, :, 48:64], -1.0, None, ALU.mult))
                dve.tensor_copy(kvsrc[:, :, 80:96], kvsrc[:, :, 32:48]).then_inc(sig("kvsrc_ready"), 1)
                dve.wait_ge(sig("kvsrc_ready"), 1)
                for b in range(NB):
                    kk = slice(2 * b, 2 * b + 2)
                    st.mark(dve.tensor_tensor(kr_raw[:, kk, :], kvsrc[:, kk, 32:64], ropeC[:, 4:6, :], ALU.mult))
                    st.link(dve.tensor_tensor(kr_abs[:, kk, :], kvsrc[:, kk, 64:96], ropeS[:, 4:6, :], ALU.mult))
                for j in range(2):
                    st.mark(dve.tensor_copy(ka[:, :, j, 0:DC], kvsrc[:, :, 0:DC]))
                    dve.tensor_tensor(ka[:, :, j, DC:], kr_raw[:, :, :], kr_abs[:, :, :], ALU.add)\
                       .then_inc(sig("ka_ready"), 1)

                for k in range(NT):
                    b, T = k // 2, k % 2
                    n = LW if T == 0 else WMAX
                    width = LW + RANKS if T == 0 else WMAX
                    off = 0 if T == 0 else LW + RANKS
                    iv = iscore[:, b, off:off + width]
                    dve.wait_ge(sig("irel"), 2 * k + 2)
                    for h in range(IH):
                        add = mask_i[:, off:off + n] if h == 0 else iv[:, 0:n]
                        st.link(dve.scalar_tensor_tensor(iv[:, 0:n], irel[:, k, h, 0:n], idx_w[:, h:h + 1], add,
                                                         ALU.mult, ALU.add))
                    if T == 0:
                        st.link(dve.tensor_copy(iv[:, n:width], mask_i[:, n:width]))
                    for r in range(0, RANKS, 8):
                        st.link(dve.max(top8[:, k, r:r + 8], iv))
                        st.link(dve.max_index(topi[:, k, r:r + 8], top8[:, k, r:r + 8], iv))
                        st.link(dve.match_replace(iv, top8[:, k, r:r + 8], iv, TAKEN))
                    dve.tensor_copy(topb[:, k, :], topi[:, k, :]).then_inc(sig("top_ready"), 1)

                for b in range(NB):
                    dve.wait_ge(sig(f"idx_spread{b}"), 16)
                    if b > 0:
                        dve.wait_ge(sig("gather_mm"), 12 * b)
                    else:
                        dve.wait_ge(sig("kv_split"), 5)
                    dve.tensor_scalar(hot0[:, :], idxb[b], source[:, 0:1], None, ALU.is_equal).then_inc(sig("hot_ready"), 1)
                    dve.tensor_scalar(hot1[:, :], idxb[b][:, 2 * LW * RANKS:], source[:, 1:2], None, ALU.is_equal)\
                       .then_inc(sig("hot_ready"), 1)
                    dve.wait_ge(sig("hot_ready"), 2 * b + 2)
                    if b > 0:
                        dve.wait_ge(sig("gscore_mm"), 3 * b)
                        dve.wait_ge(sig("gathT_mm"), 3 * b)
                    for g in range(12):
                        dve.wait_ge(sig("gather_mm"), 12 * b + g + 1)
                        dve.tensor_tensor(gath[:, 512 * g:512 * g + 512].rearrange("p (t r) -> p t r", r=RANKS),
                                          ps[0:GF, 5 + g % 3, :].rearrange("p (t r) -> p t r", r=RANKS),
                                          bc(rank_tab[:, :], 1, 16), ALU.mult).then_inc(sig("gath_evac"), 1)

                for a in range(2 * NB + 2):
                    b, T = a // 2, a % 2
                    if a >= 2:
                        tile_pt(a - 2, T)
                    if a < 2 * NB:
                        if T == 0:
                            st.link(dve.memset(SA(a, 0, P + RANKS)[0:LW, :, P:], MASKED))
                        tile_scores(a, T, keys(T) + RANKS, mask_a, None,
                                    (sig(f"gsc_back_{b}_{T}"), 64 * (1 + T)))
                    if 0 < a <= 2 * NB:
                        tile_norm(a - 1, 1 - T, keys(1 - T) + RANKS)
                for b in range(NB):
                    dve.wait_ge(sig("a_out"), 2 * b + 2)
                    xb = xT[:, bcols(b)]
                    st.link(dve.scalar_tensor_tensor(xb, ps[:, 6, 0:L], mod[:, 2, b:b + 1], xb, ALU.mult, ALU.add))
                    xl = xT[:, L * b + LW:L * b + L]
                    dve.scalar_tensor_tensor(xl, ps[:, 6, L:L + GT], mod[:, 2, b:b + 1], xl, ALU.mult, ALU.add)\
                       .then_inc(sig("x_updated"), 1)

                def shift(n, b):
                    f = fT[:, bcols(b)]
                    dve.tensor_copy(sh[0:64, b, :], f[0:64]).then_inc(sig("shifted"), 1)
                    dve.tensor_copy(sh[64:P, b, 1:L], f[64:P, 0:L - 1]).then_inc(sig("shifted"), 1)
                    dve.wait_ge(sig("shifted"), 4 * n + 2 * b + 2)

                dve.wait_ge(sig("x_updated"), 2)
                layernorm(1, xT[:, :], by_batch(4, 3, fT))
                for b in range(NB):
                    dve.wait_ge(sig("ln_out"), 2 + b + 1)
                    shift(0, b)

                for l in range(2):
                    def turned_queries_keys(k):
                        T, m = k % 2, NT * l + k
                        dve.wait_ge(sig("qk_squared"), m + 1)
                        v3 = lambda ap: ap.rearrange("p (s h n) -> p s h n", s=2, h=H)
                        qk = ps[:, 2 * (k % 2):2 * (k % 2) + 2, :].rearrange("p s (h n) -> p s h n", h=H)
                        own = qk_own[k]
                        r0, r1 = v3(own), v3(qk_part[k % 2])
                        if k >= 2:
                            dve.wait_ge(sig("qk_added"), m - 1)
                        tab = xtab[:, l, T, :].rearrange("p (c s n) -> p c s n", c=2, s=2)
                        hd_ = DH // 2
                        dve.tensor_tensor(r0, qk, bc(tab[:, 0, :, :], 2, H), ALU.mult).then_inc(sig("qk_parts"), 1)
                        dve.tensor_tensor(r1[:, :, :, 0:hd_], qk[:, :, :, hd_:], bc(tab[:, 1, :, 0:hd_], 2, H), ALU.mult)\
                           .then_inc(sig("qk_parts"), 1)
                        dve.tensor_tensor(r1[:, :, :, hd_:], qk[:, :, :, 0:hd_], bc(tab[:, 1, :, hd_:], 2, H), ALU.mult)\
                           .then_inc(sig("qk_parts"), 1)
                        st.link(dve.tensor_reduce(ssq[:, k, :], SAf[:, 1024 * (k % 2):1024 * (k % 2) + 1024]
                                                  .rearrange("p (h n) -> p h n", n=DH), AX.X, ALU.add))
                        dve.tensor_scalar(ssq[:, k, :], ssq[:, k, :], 1e-24, None, ALU.max).then_inc(sig("ssq_ready"), 1)

                    def normed_keys(k):
                        m = NT * l + k
                        dve.wait_ge(sig("rs_ready"), m + 1)
                        nt = nb[:, 14:16, :].rearrange("p u h -> p (u h)")
                        st.link(dve.tensor_tensor(nt, ssq[:, k, :], rs[:, k, :], ALU.mult))
                        st.link(dve.scalar_tensor_tensor(nt, nt, -0.5, rs[:, k, :], ALU.mult, ALU.mult))
                        st.link(dve.scalar_tensor_tensor(rs[:, k, :], nt, 1.5, rs[:, k, :], ALU.add, ALU.mult))
                        st.mark(dve.tensor_scalar(cqs[:, k, :], rs[:, k, 0:H], 8.0, None, ALU.mult))
                        kk = qk_own[k][:, 512:1024].rearrange("p (h n) -> p h n", h=H)
                        dve.wait_ge(sig("qk_added"), m + 1)
                        dve.tensor_tensor(kk, kk, bc(rs[:, k, H:], 2, DH), ALU.mult).then_inc(sig("qk_ready"), 1)

                    turned_queries_keys(0)
                    for k in range(NT):
                        if k + 1 < NT:
                            turned_queries_keys(k + 1)
                        normed_keys(k)
                    for k in range(NT):
                        T, a = k % 2, 4 + 4 * l + k
                        if k >= 2:
                            tile_pt(a - 2, T)
                            dve.wait_ge(sig("pt_mm"), 12 * (l + 1) + UNITS_BEFORE[k - 1])
                        tile_scores(a, T, keys(T), mask_w, cqs[:, k, :])
                        if k > 0:
                            tile_norm(a - 1, 1 - T, keys(1 - T))
                    tile_pt(a - 1, 1 - T)
                    tile_norm(a, T, keys(T))
                    for b in range(NB):
                        if b == NB - 1:
                            tile_pt(a, T)
                        dve.wait_ge(sig("f_o"), NB * l + b + 1)
                        st.link(dve.tensor_tensor(fT[:, bcols(b)], ps[:, b, 0:L], fT[:, bcols(b)], ALU.add))
                        shift(2 * l + 1, b)

                    def affine(b):
                        return dve.tensor_scalar(hT[:, bcols(b)], xc[:, bcols(b)], ln_gb[:, l, 0:1], ln_gb[:, l, 1:2],
                                                 ALU.mult, ALU.add)

                    layernorm(2 + l, sh[:, :, :].rearrange("p b t -> p (b t)"), affine)
                    for c in range(3):
                        dve.wait_ge(sig("f_a"), 3 * l + c + 1)
                        dve.wait_ge(sig("f_gelu"), 3 * l + c + 1)
                        m = HC[c]
                        dve.scalar_tensor_tensor(hh[0:m, c, :], ps[0:m, c, :], b1[0:m, l, 0, c:c + 1], PT[0:m, c, :],
                                                 ALU.add, ALU.mult).then_inc(sig("f_hidden"), 1)
                    for b in range(NB):
                        dve.wait_ge(sig("f_down"), NB * l + b + 1)
                        f = fT[:, bcols(b)]
                        dve.scalar_tensor_tensor(f, ps[:, 6 + b, 0:L], b2[:, l:l + 1], f, ALU.add, ALU.add)\
                           .then_inc(sig("f_done"), 1)
                        dve.wait_ge(sig("f_done"), NB * l + b + 1)
                        if l == 0:
                            shift(2, b)
                        else:
                            dve.scalar_tensor_tensor(xT[:, bcols(b)], f, mod[:, 5, b:b + 1], xT[:, bcols(b)],
                                                     ALU.mult, ALU.add).then_inc(sig("x_updated"), 1)

                dve.wait_ge(sig("x_updated"), 4)
                layernorm(4, xT[:, :], by_batch(7, 6, hT))
                dve.wait_ge(sig("qk1_mm"), 2)
                dve.tensor_scalar(k1T, ps[:, 1, :], b1k[:, 0:1], None, ALU.add).then_inc(sig("k1_copied"), 1)
                for u in range(4 * NT):
                    dve.wait_ge(sig("l1_mm"), u + 1)
                    b0 = 2 * (u % 2)
                    st.link(dve.tensor_reduce(mx[:, u, 0:4].rearrange("p (g j) -> p g j", j=2),
                                              ps[:, b0:b0 + 2, :].rearrange("p g (j n) -> p g j n", j=2), AX.X, ALU.max))
                    dve.tensor_scalar(nb[:, u, 0:4], mx[:, u, 0:4], -SCALE_1, None, ALU.mult).then_inc(sig("l1_bias"), 1)
                    if u > 0:
                        turned_copy1(dve, u - 1, 1, "l1_pt_dve")
                turned_copy1(dve, u, 1, "l1_pt_dve")
                dve.wait_ge(sig("l1_exp"), 4 * NT)
                dve.reciprocal(rl1, ls1).then_inc(sig("l1_recip"), 1)
                dve.wait_ge(sig("l1_recip_wide"), 1)
                dve.wait_ge(sig("l1_pv"), 4 * NT)
                dve.tensor_tensor(hT[:, :], ps[:, 7, :], xc, ALU.mult).then_inc(sig("att1_ready"), 1)
                dve.wait_ge(sig("l1_out"), 1)
                for b in range(NB):
                    st.link(dve.tensor_scalar(xc[:, bcols(b)], ps[:, 1, bcols(b)], b1out[:, 0:1], mod[:, 8, b:b + 1],
                                              ALU.add, ALU.mult))
                    dve.tensor_tensor(xT[:, bcols(b)], xT[:, bcols(b)], xc[:, bcols(b)], ALU.add).then_inc(sig("x_updated"), 1)

                dve.wait_ge(sig("x_updated"), 6)
                layernorm(5, xT[:, :], by_batch(10, 9, hT))
                v4 = lambda ap: ap.rearrange("p (k e) -> p k e", e=E1)
                den, sc, sel, rep, msk, wgt = (rt[:, i, :] for i in range(6))
                dve.wait_ge(sig("route_exp"), 1)
                st.link(dve.tensor_scalar(den, den, 1.0, None, ALU.add))
                st.link(dve.reciprocal(sc, den))
                st.link(dve.tensor_tensor(v4(sel), v4(sc), bc(e_bias[:, :], 1, NT), ALU.add))
                for k in range(NT):
                    st.mark(dve.max(rsm[:, 8 * k:8 * k + 8], v4(sel)[:, k, :]))
                st.wait()
                for k in range(NT):
                    st.mark(dve.match_replace(v4(rep)[:, k, :], rsm[:, 8 * k:8 * k + 8], v4(sel)[:, k, :], TAKEN))
                st.wait()
                st.link(dve.tensor_tensor(msk, rep, sel, ALU.not_equal))
                st.link(dve.tensor_tensor(wgt, msk, sc, ALU.mult))
                st.link(dve.tensor_reduce(rsm[:, 32:36], v4(wgt), AX.X, ALU.add))
                st.link(dve.reciprocal(rsm[:, 36:40], rsm[:, 32:36]))
                st.link(dve.scalar_tensor_tensor(v4(comb_rem), v4(wgt), ROUTE, bc(rsm[:, 36:40], 2, E1), ALU.mult, ALU.mult))
                for s in range(3):
                    st.link(dve.tensor_copy(comb_part, comb_rem))
                    ins = dve.tensor_copy(comb3[:, :, s, :], v4(comb_part))
                    if s < 2:
                        st.mark(ins)
                        st.link(dve.tensor_tensor(comb_rem, comb_rem, comb_part, ALU.subtract))
                ins.then_inc(sig("comb_ready"), 1)
                for e in range(E1 + 1):
                    s = e % 2
                    dve.wait_ge(sig("e_silu"), e + 1)
                    dve.wait_ge(sig("e_up"), e + 1)
                    if e >= 2:
                        dve.wait_ge(sig("e_down"), e - 1)
                    ins = dve.tensor_tensor(moe_h[:, s, :], moe_g[:, s, :], ps[:, 2 + s, :], ALU.mult)
                    if e > 0:
                        st.link(ins)
                        dve.wait_ge(sig("e_comb"), e)
                        ins = dve.tensor_tensor(moe_h[:, s, :], moe_h[:, s, :], ps[:, 4 + s, :], ALU.mult)
                    ins.then_inc(sig("e_hidden"), 1)
                dve.wait_ge(sig("e_down"), E1 + 1)
                for b in range(NB):
                    dve.scalar_tensor_tensor(xT[:, bcols(b)], ps[:, 6, bcols(b)], mod[:, 11, b:b + 1], xT[:, bcols(b)],
                                             ALU.mult, ALU.add).then_inc(sig("x_updated"), 1)
                pass_end(dve, "dve")

        @block.scalar
        def _(act):
            st = Steps(act, sig("act_setup_step"))
            act.wait_ge(sig("weights_loaded"), 16 * (len(loads) + len(rows)))
            act.wait_ge(sig("cols_set"), 4)
            act.activation(c_den[:, :, :], cT[:, :, :], ACT.Exp, scale=-1.0).then_inc(sig("setup_exp"), 1)
            act.activation(ang[:, 0, :], delta_row[:, :], ACT.Exp, scale=-1.0).then_inc(sig("setup_exp"), 1)
            act.activation(dcol[:, 0:1], delta_col[:, :], ACT.Exp, scale=-1.0).then_inc(sig("setup_exp"), 1)
            act.wait_ge(sig("delta_ready"), 2)
            for t in (ang, dcol[:, :].unsqueeze(2)):
                for i in range(2):
                    act.activation(t[:, 5 + i, :], t[:, 3 + i, :], ACT.Sin).then_inc(sig("delta_sin"), 1)
            act.wait_ge(sig("setup_done"), 1)

            with act.Fori(0, PASSES) as it:
                st = Steps(act, sig("act_step"))
                act.preload_act_table_set(LN_AND_EXP)
                act.wait_ge(sig("x_turned"), 1)
                act.activation(xT[:, :], ps[:, 0, :], ACT.Copy).then_inc(sig("xT_copied"), 1)

                def layernorm(n):
                    for b in range(NB):
                        act.wait_ge(sig("ln_centered"), 2 * n + b + 1)
                        act.activation(sq[:, bcols(b)], xc[:, bcols(b)], ACT.Square).then_inc(sig("ln_squared"), 1)
                    for b in range(NB):
                        r = rstd[:, bcols(b)]
                        act.wait_ge(sig("ln_var"), 2 * n + b + 1)
                        st.link(act.activation(r, ps[:, 2 + b, 0:L], ACT.Ln, bias=eps_col[:, :]))
                        act.activation(r, r, ACT.Exp, scale=-0.5).then_inc(sig("ln_rstd"), 1)

                def tile_exp(a, T, width, scale):
                    for h in range(H):
                        if h % 4 == 0:
                            act.wait_ge(sig("att_bias"), 2 * a + h // 4 + 1)
                        v = SA(a, T, width)[:, h, :]
                        ins = act.activation(v, v, ACT.Exp, bias=nb[:, a % 4, h:h + 1],
                                             scale=SCALE_A if scale is None else scale[:, h:h + 1],
                                             accum_out=ls[:, a % 4, h:h + 1])
                        if h % 4 == 3:
                            ins.then_inc(sig("att_exp"), 1)

                def tile_pt(a, T):
                    for u in range(0, len(UNITS[T]), 2):
                        act.wait_ge(sig("pt_mm"), 12 * (a // 4) + UNITS_BEFORE[a % 4] + u + 1)
                        act.activation(PT[:, u, :], ps[:, turn_bank(a, u), :], ACT.Copy)\
                           .then_inc(sig("pt_act"), 1)

                def tile_out(a, dst):
                    act.wait_ge(sig("att_pv"), a + 1)
                    n = dst.shape[1]
                    act.activation(dst[:, :, cols(a % 4)], ps[:, 7, 0:n * P].rearrange("p (i n) -> p i n", i=n), ACT.Copy)\
                       .then_inc(sig("o_copied"), 1)

                layernorm(0)
                for i, (dst, bank) in enumerate(((kiT, 3), (qiT[:, 0, :], 4), (qiT[:, 1, :], 5))):
                    act.wait_ge(sig("a_proj"), i + 1)
                    act.activation(dst, ps[:, bank, :], ACT.Copy).then_inc(sig("a_copied"), 1)
                act.wait_ge(sig("a_proj"), 4)
                act.activation(cqT[:, :], ps[0:DQ, 2, :], ACT.Copy).then_inc(sig("a_copied"), 1)
                act.wait_ge(sig("kv_proj"), 1)
                kvp = ps[:, 6, 0:NT * (DC + DR)].rearrange("p (k n) -> p k n", k=NT)
                act.activation(kr_abs[:, :, :], kvp[:, :, DC:], ACT.Abs).then_inc(sig("kr_abs"), 1)
                act.wait_ge(sig("kr_abs"), 1)
                st.link(act.activation(kr_abs[:, :, :], kr_abs[:, :, :], ACT.Exp, scale=-1.0))
                act.activation(kr_abs[:, :, :], kr_abs[:, :, :], ACT.Ln, bias=one_col[:, :]).then_inc(sig("kr_log"), 1)
                for k in range(NT):
                    n = LW if k % 2 == 0 else WMAX
                    act.wait_ge(sig("iscore_mm"), k + 1)
                    for j in range(2):
                        act.activation(irel[:, k, j:j + 3:2, 0:n],
                                       ps[:, 2 + 2 * (k % 2) + j, 0:2 * n].rearrange("p (h n) -> p h n", h=2),
                                       ACT.Relu).then_inc(sig("irel"), 1)
                act.wait_ge(sig("kaT_turned"), 1)
                def split_copy(i, src, n):
                    if n > 0:
                        act.wait_ge(sig("kv_split"), n)
                    act.activation(kv_part[i][:, :, :], src, ACT.Copy).then_inc(sig("kv_split"), 1)

                act.wait_ge(sig("kvsrc_ready"), 1)
                split_copy(0, kvsrc[:, :, :], 0)
                for s in range(2):
                    r = slice(DH * s, DH * s + DH)
                    act.activation(kaT[r, s, :], ps[r, 7, :], ACT.Copy).then_inc(sig("ka_copied"), 1)

                def query_parts(k):
                    q_abs, q_mu = q_tmp[k % 2][0:2]
                    raw = ps[:, k % 2, H * DC:]
                    act.wait_ge(sig("q2_mm"), k + 1)
                    if k >= 2:
                        act.wait_ge(sig("q_ready"), 3 * (k - 1))
                        act.wait_ge(sig("q_turned"), k - 1)
                    st.link(act.activation(q_abs, raw, ACT.Abs))
                    st.link(act.activation(q_abs, q_abs, ACT.Exp, scale=-1.0))
                    act.activation(q_mu, raw, ACT.Relu).then_inc(sig("q2_log"), 1)
                    act.activation(q_abs, q_abs, ACT.Ln, bias=one_col[:, :]).then_inc(sig("q2_log"), 1)
                    lat = ps[:, k % 2, 0:256].rearrange("p (h n) -> p h n", h=H)
                    act.activation(qa[k % 2][:, :, 0:DC], lat, ACT.Copy).then_inc(sig("q_latent"), 1)
                    act.activation(qb[k % 2][:, :, 0:DC], lat, ACT.Copy).then_inc(sig("q_latent"), 1)

                query_parts(0)
                split_copy(1, kv_rem[:, 0, :, :], 2)
                for k in range(NT):
                    if k == 0:
                        act.wait_ge(sig("y_stored"), 16)
                        act.sem_clear(sig("y_stored"))
                    if k + 1 < NT:
                        query_parts(k + 1)
                    if k == 1:
                        split_copy(2, kv_rem[:, 1, :, :], 4)
                    act.wait_ge(sig("q_turned"), k + 1)
                    act.activation(qaT[:, :, cols(k)], ps[:, 2, :].rearrange("p (i n) -> p i n", i=4), ACT.Copy)\
                       .then_inc(sig("qa_copied"), 1)
                    t0, t1, p0 = (0, LW, LW) if k % 2 == 0 else (LW, GT, 0)
                    for i in range(2):
                        src = ps[0:GF, 3 + i, :].rearrange("p (h t) -> p t h", h=4)[:, p0:P, :]
                        act.activation(qbT[:, k // 2, t0:t1, 4 * i:4 * i + 4], src, ACT.Copy).then_inc(sig("qb_copied"), 1)
                for b in range(NB):
                    if b > 0:
                        act.wait_ge(sig("gsc_saved"), 48 * b)
                    for n in range(3):
                        act.wait_ge(sig("gathT_mm"), 3 * b + n + 1)
                        act.activation(gathT[:, b, 16 * n:16 * n + 16, :],
                                       ps[:, (3 * b + n) % 2, :].rearrange("p (j c) -> p j c", c=DC), ACT.Copy)\
                           .then_inc(sig("gathT_ready"), 1)
                        act.wait_ge(sig("gscore_mm"), 3 * b + n + 1)
                        act.activation(gsc[:, n, :], ps[:, (4, 2, 3)[n], :], ACT.Copy).then_inc(sig("gsc_ready"), 1)
                def gathered(b):
                    act.wait_ge(sig("xg_turned"), b + 1)
                    act.wait_ge(sig("pdiag_zero"), 1)
                    for t in range(GP):
                        part = slice(RANKS * t, RANKS * t + RANKS)
                        act.activation(pdiag[part, :, t, :], ps[part, 2, 0:3 * P].rearrange("p (j h) -> p j h", h=H),
                                       ACT.Copy).then_inc(sig("pdiag_ready"), 1)
                    if b > 0:
                        act.wait_ge(sig("a_out"), 2 * b)
                    for n in range(3):
                        act.wait_ge(sig("og_mm"), 3 * b + n + 1)
                        act.activation(og[:, 64 * n:64 * n + 64, :],
                                       ps[0:DC, 3 - n % 2, :].rearrange("p (t h) -> p t h", h=H), ACT.Copy)\
                           .then_inc(sig("og_ready"), 1)

                for a in range(2 * NB + 2):
                    T = a % 2
                    if a < 2 * NB:
                        tile_exp(a, T, keys(T) + RANKS, None)
                    if a >= 2:
                        tile_out(a - 2, oTa)
                    if 0 < a <= 2 * NB:
                        tile_pt(a - 1, 1 - T)
                    if a >= 3 and T == 1:
                        gathered((a - 3) // 2)

                layernorm(1)
                for l in range(2):
                    def values(b, c):
                        act.wait_ge(sig("v_mm"), 6 * l + 3 * b + c + 1)
                        r = LW if c == 2 else P
                        act.activation(vt[0:r, b, c, :], ps[0:r, 4 + c % 2, :], ACT.Copy).then_inc(sig("v_copied"), 1)

                    def squares(k):
                        m = NT * l + k
                        act.wait_ge(sig("qk_mm"), m + 1)
                        if k >= 2:
                            act.wait_ge(sig("ssq_ready"), m - 1)
                        act.activation(SAf[:, 1024 * (k % 2):1024 * (k % 2) + 1024]
                                       .rearrange("p (s n) -> p s n", s=2),
                                       ps[:, 2 * (k % 2):2 * (k % 2) + 2, :], ACT.Square).then_inc(sig("qk_squared"), 1)

                    squares(0)
                    squares(1)
                    for k in range(NT):
                        m = NT * l + k
                        act.wait_ge(sig("ssq_ready"), m + 1)
                        st.link(act.activation(rs[:, k, :], ssq[:, k, :], ACT.Ln, scale=LN_SHIFT))
                        act.activation(rs[:, k, :], rs[:, k, :], ACT.Exp, scale=-0.5, bias=shift_col[:, :])\
                           .then_inc(sig("rs_ready"), 1)
                        if k + 2 < NT:
                            squares(k + 2)
                        for j in range(2 * k, 2 * k + 2):
                            if j < 6:
                                values(j // 3, j % 3)
                        act.wait_ge(sig("qk_turned"), m + 1)
                        if m == 0:
                            act.wait_ge(sig("q_zero"), 2)
                        qt = ps[:, 6, :].rearrange("p (i n) -> p i n", i=4)
                        act.activation(q_half[0:DH, :, 0, cols(k)], qt[0:DH], ACT.Copy).then_inc(sig("q_copied"), 1)
                        act.activation(q_half[DH:P, :, 1, cols(k)], qt[DH:P], ACT.Copy).then_inc(sig("q_copied"), 1)
                        act.activation(kT[:, :, cols(k)], ps[:, 7, :].rearrange("p (i n) -> p i n", i=4), ACT.Copy)\
                           .then_inc(sig("k_copied"), 1)
                    for k in range(NT):
                        a, T = 4 + 4 * l + k, k % 2
                        tile_exp(a, T, keys(T), cqs[:, k, :])
                        if k > 1:
                            tile_out(a - 2, oT)
                        if k > 0:
                            tile_pt(a - 1, 1 - T)
                    tile_out(a - 1, oT)
                    tile_pt(a, T)
                    tile_out(a, oT)
                    layernorm(2 + l)
                    for c in range(3):
                        m = HC[c]
                        act.wait_ge(sig("f_g"), 3 * l + c + 1)
                        act.activation(PT[0:m, c, :], ps[0:m, 3 + c, :], ACT.Gelu, bias=b1[0:m, l, 1, c:c + 1])\
                           .then_inc(sig("f_gelu"), 1)
                    act.preload_act_table_set(LN_AND_EXP)

                layernorm(4)
                act.wait_ge(sig("qk1_mm"), 1)
                act.activation(q1T, ps[:, 0, :], ACT.Identity, bias=b1q[:, :]).then_inc(sig("q1_copied"), 1)
                act.wait_ge(sig("v1_mm"), 1)
                act.wait_ge(sig("v_zero"), 1)
                for j in range(4):
                    src = ps[:, 2, :].rearrange("p (k g j n) -> p k g j n", k=NT, g=4, j=4)
                    for k in range(NT):
                        act.activation(v_own[:, k, :, j, D1 * j:D1 * j + D1], src[:, k, :, j, :], ACT.Copy)\
                           .then_inc(sig("v1_copied"), 1)
                for u in range(4 * NT):
                    act.wait_ge(sig("l1_bias"), u + 1)
                    if u >= 4:
                        act.wait_ge(sig("l1_turned"), 2 * u - 6)
                    for e in range(4):
                        ins = act.activation(probs1(u)[:, e, :], ps[:, 2 * (u % 2) + e // 2, L * (e % 2):L * (e % 2) + L],
                                             ACT.Exp, bias=nb[:, u, e:e + 1], scale=SCALE_1,
                                             accum_out=ls1[:, H1 * (u // 4) + 4 * e + u % 4:H1 * (u // 4) + 4 * e + u % 4 + 1])
                    ins.then_inc(sig("l1_exp"), 1)
                    if u > 0:
                        turned_copy1(act, u - 1, 0, "l1_pt_act")
                turned_copy1(act, u, 0, "l1_pt_act")
                act.wait_ge(sig("l1_recip_turned"), 1)
                act.activation(combT[:, :], ps[0:H1, 0, :], ACT.Copy).then_inc(sig("l1_recip_copied"), 1)
                act.wait_ge(sig("l1_recip_mm"), 1)
                act.activation(xc, ps[:, 1, :], ACT.Copy).then_inc(sig("l1_recip_wide"), 1)

                layernorm(5)
                act.wait_ge(sig("route_mm"), 1)
                act.activation(rt[:, 0, :], ps[:, 7, 0:NT * E1], ACT.Exp, scale=-1.0).then_inc(sig("route_exp"), 1)
                for e in range(E1 + 1):
                    if e == 2:
                        act.wait_ge(sig("comb_turned"), 1)
                        act.activation(combS, ps[0:3 * E1, 7, :], ACT.Copy).then_inc(sig("comb_copied"), 1)
                    act.wait_ge(sig("e_gate"), e + 1)
                    if e >= 2:
                        act.wait_ge(sig("e_hidden"), e - 1)
                    act.activation(moe_g[:, e % 2, :], ps[:, e % 2, :], ACT.Silu).then_inc(sig("e_silu"), 1)
                act.wait_ge(sig("y_turned"), 1)
                act.activation(y_tok[:, :, :], ps[:, 7, :].rearrange("p (k n) -> p k n", k=NT), ACT.Copy).then_inc(sig("y_ready"), 1)
                pass_end(act, "act")

        @block.tensor
        def _(pe):
            mm = pe.matmul

            pe.wait_ge(sig("weights_loaded"), 16 * (len(loads) + len(rows)))
            for h in range(H):
                last = mm(ps[0:DQ, 1, DC * h:DC * h + DC], uqT[:, h, :], ukT[:, h, :], start=True, stop=True)
            last.then_inc(sig("absorb_mm"), 1)
            for h in range(H):
                last = mm(ps[0:DC, 2 + h // 4, D * (h % 4):D * (h % 4) + D], uvT[:, h, :], w_out0[:, h, :],
                          start=True, stop=True)
            last.then_inc(sig("absorb_mm"), 1)
            for h in range(H):
                q = DC * (h % 4)
                last = mm(ps[q:q + DC, 4, D * (h // 4):D * (h // 4) + D], uvT[:, h, :], w_out0[:, h, :],
                          start=True, stop=True)
            last.then_inc(sig("absorb_mm"), 1)
            mm(ps[:, 5, 0:1], w1o[:, :], b1v[:, :], start=True, stop=True).then_inc(sig("absorb_mm"), 1)
            pe.wait_ge(sig("c_act_ready"), 1)
            for j in range(12):
                last = mm(ps[:, 0, B * j:B * j + B], wmod[:, j // 6, D * (j % 6):D * (j % 6) + D], c_act[:, j // 6, :],
                          start=True, stop=True)
            last.then_inc(sig("mod_mm"), 1)
            pe.wait_ge(sig("setup_done"), 1)

            with pe.Fori(0, PASSES) as it:
                pe.wait_ge(sig("x_loaded"), 16)
                pe.sem_clear(sig("x_loaded"))
                for k in range(NT):
                    last = pe.transpose(ps[:, 0, cols(k)], x_tok[:, k, :], ident[:, :])
                last.then_inc(sig("x_turned"), 1)

                def layernorm(n, src, source=None, before=0, each=1):
                    for b in range(NB):
                        if source is not None:
                            pe.wait_ge(sig(source), before + each * (b + 1))
                        mm(ps[:, b, 0:L], mean_mat[:, :], src[:, bcols(b)], start=True, stop=True).then_inc(sig("ln_mean"), 1)
                    for b in range(NB):
                        pe.wait_ge(sig("ln_squared"), 2 * n + b + 1)
                        mm(ps[:, 2 + b, 0:L], mean_mat[:, :], sq[:, bcols(b)], start=True, stop=True).then_inc(sig("ln_var"), 1)
                    pe.wait_ge(sig("ln_out"), 2 * n + 2)

                def tile_scores(a, T, queries_of, keys_of):
                    k, n = a % 4, keys(T)
                    for h in range(H):
                        if a > 0 and h % 2 == 0:
                            pe.wait_ge(sig("att_evac"), 4 * a - 3 + h // 2)
                        last = mm(ps[:, h // 2, n * (h % 2):n * (h % 2) + n], queries_of(h, cols(k)),
                                  keys_of(h, key_cols(k // 2, T)), start=True, stop=True)
                        if h % 2:
                            last.then_inc(sig("att_mm"), 1)

                def tile_pt(a, T, width):
                    for u, (h0, c) in enumerate(UNITS[T]):
                        first, n = (0, P) if c == 0 else (P, LW)
                        pe.wait_ge(sig("att_prob"), 2 * a + h0 // 4 + 1)
                        if u == 2 and a < 4:
                            pe.wait_ge(sig("pt_act"), pt_act(a) + 1)
                        if u == 3:
                            pe.wait_ge(sig("pt_dve"), pt_act(a) + 1)
                        for i in range(4):
                            last = pe.transpose(ps[0:n, turn_bank(a, u), P * i:P * i + P],
                                                SA(a, T, width)[:, h0 + i, first:first + n], ident[:, :])
                        last.then_inc(sig("pt_mm"), 1)

                def pt_act(a):
                    return 6 * (a // 4) + UNITS_BEFORE[a % 4] // 2

                def tile_pv(a, T, m, lhs):
                    per = P // m
                    chunks = 1 + T
                    if a > 0:
                        pe.wait_ge(sig("o_copied"), a)
                    for h0 in range(0, H, per):
                        for c in range(chunks):
                            u = (h0 // 4) * chunks + c
                            who = "pt_act" if u % 2 == 0 else "pt_dve"
                            if h0 % 4 == 0:
                                pe.wait_ge(sig(who), pt_act(a) + u // 2 + 1)
                            n = P if c == 0 else LW
                            for h in range(h0, h0 + per):
                                q = m * (h % per)
                                last = mm(ps[q:q + m, 7, P * (h // per):P * (h // per) + P], lhs(h, c),
                                          PT[0:n, u, P * (h % 4):P * (h % 4) + P], start=(c == 0), stop=(c == chunks - 1))
                    last.then_inc(sig("att_pv"), 1)

                pe.wait_ge(sig("xT_copied"), 1)
                layernorm(0, xT[:, :])
                for w, bank, r in ((w_ki[:, :], 3, P), (w_qi[:, 0:P], 4, P), (w_qi[:, P:], 5, P), (w_dq[:, :], 2, DQ)):
                    mm(ps[0:r, bank, :], w, hT[:, :], start=True, stop=True).then_inc(sig("a_proj"), 1)
                n = DC + DR
                for k in range(NT):
                    mm(ps[:, 6, n * k:n * k + n], hT[:, cols(k)], w_kv[:, :], start=True, stop=True)
                for b in range(NB):
                    mm(ps[:, 6, n * NT + DC * b:n * NT + DC * b + DC], hT[:, L * b + LW:L * b + LW + P], w_kv[:, 0:DC],
                       start=True, stop=True)
                for b in range(NB):
                    c0 = n * NT + DC * NB + DC * b
                    last = mm(ps[0:LW, 6, c0:c0 + DC], hT[:, L * b + L - LW:L * b + L], w_kv[:, 0:DC], start=True, stop=True)
                last.then_inc(sig("kv_proj"), 1)
                pe.wait_ge(sig("a_copied"), 4)
                for k in range(NT):
                    b, T = k // 2, k % 2
                    n = LW if T == 0 else WMAX
                    if k >= 2:
                        pe.wait_ge(sig("irel"), 2 * k - 2)
                    for h in (0, 2, 1, 3):
                        r = slice(DH * (h % 2), DH * (h % 2) + DH)
                        last = mm(ps[:, 2 + 2 * (k % 2) + h % 2, n * (h // 2):n * (h // 2) + n], qiT[r, h // 2, cols(k)],
                                  kiT[r, L * b:L * b + n], start=True, stop=True)
                    last.then_inc(sig("iscore_mm"), 1)
                pe.wait_ge(sig("ka_ready"), 2)
                for k in range(NT):
                    last = pe.transpose(ps[:, 7, cols(k)], ka[:, k, :, :].rearrange("p s n -> p (s n)"), ident[:, :])
                last.then_inc(sig("kaT_turned"), 1)
                pe.wait_ge(sig("irel"), 2 * NT)

                def queries_raw(k):
                    if k >= 2:
                        pe.wait_ge(sig("q2_log"), 2 * k - 2)
                        pe.wait_ge(sig("q_latent"), 2 * k - 2)
                    mm(ps[:, k % 2, :], cqT[:, cols(k)], w_q2[:, :], start=True, stop=True).then_inc(sig("q2_mm"), 1)

                def gather(b):
                    pe.wait_ge(sig("hot_ready"), 2 * b + 2)
                    for g in range(12):
                        if 12 * b + g >= 3:
                            pe.wait_ge(sig("gath_evac"), 12 * b + g - 2)
                        terms = [(kv_part[i][:, 2 * b, :], hot0[:, 512 * g:512 * g + 512]) for i in range(3)]
                        if g >= 8:
                            terms += [(kv_part[i][:, 2 * b + 1, :], hot1[:, 512 * (g - 8):512 * (g - 8) + 512])
                                      for i in range(3)]
                        for i, (l_, r_) in enumerate(terms):
                            last = mm(ps[0:GF, 5 + g % 3, :], l_, r_, start=(i == 0), stop=(i == len(terms) - 1))
                        last.then_inc(sig("gather_mm"), 1)

                queries_raw(0)
                for k in range(NT):
                    if k == NT - 1:
                        pe.wait_ge(sig("kv_split"), 5)
                        pe.wait_ge(sig("ka_copied"), 2)
                        gather(0)
                    if k + 1 < NT:
                        queries_raw(k + 1)
                    if k > 0:
                        pe.wait_ge(sig("qa_copied"), k)
                        pe.wait_ge(sig("qb_copied"), 2 * k)
                    pe.wait_ge(sig("q_ready"), 3 * k + 3)
                    pe.wait_ge(sig("q_latent"), 2 * k + 2)
                    for i in range(4):
                        pe.transpose(ps[:, 2, P * i:P * i + P],
                                     qa[k % 2][:, 2 * i:2 * i + 2, :].rearrange("p h n -> p (h n)"), ident[:, :])
                    for h in range(H):
                        last = pe.transpose(ps[0:GF, 3 + h // 4, P * (h % 4):P * (h % 4) + P], qb[k % 2][:, h, :], ident[:, :])
                    last.then_inc(sig("q_turned"), 1)
                pe.wait_ge(sig("qa_copied"), NT)
                pe.wait_ge(sig("qb_copied"), 2 * NT)
                for b in range(NB):
                    if b > 0:
                        gather(b)
                    for n in range(3):
                        pe.wait_ge(sig("gath_evac"), 12 * b + 4 * n + 4)
                        if b > 0:
                            pe.wait_ge(sig("gsc_ready"), 3 * (b - 1) + n + 1)
                        for blk in range(4):
                            for q in range(4):
                                t = 64 * n + 16 * q + 4 * blk
                                last = mm(ps[32 * q:32 * q + 32, (4, 2, 3)[n], P * blk:P * blk + P],
                                          qbT[:, b, t:t + GP, :].rearrange("p t h -> p (t h)"),
                                          gath[:, RANKS * t:RANKS * t + P], start=True, stop=True)
                        last.then_inc(sig("gscore_mm"), 1)
                        if 3 * b + n >= 2:
                            pe.wait_ge(sig("gathT_ready"), 3 * b + n - 1)
                        for j in range(16):
                            c0 = P * (16 * n + j)
                            last = pe.transpose(ps[:, (3 * b + n) % 2, DC * j:DC * j + DC], gath[0:DC, c0:c0 + P], ident[0:DC, 0:DC])
                        last.then_inc(sig("gathT_mm"), 1)
                pe.wait_ge(sig("gathT_ready"), 6)
                pe.wait_ge(sig("gsc_ready"), 6)
                pe.wait_ge(sig("ka_copied"), 2)
                def gathered(b):
                    for T in range(2):
                        pe.wait_ge(sig(f"xg_loaded{T}"), 64 * (1 + T) * (b + 1))
                    pe.wait_ge(sig("att_evac"), 4 * min(2 * b + 4, 2 * NB))
                    if b > 0:
                        pe.wait_ge(sig("og_ready"), 3 * b)
                    for n in range(3):
                        last = pe.transpose(ps[:, 2, P * n:P * n + P], xg[:, n, :], ident[:, :])
                    last.then_inc(sig("xg_turned"), 1)
                    pe.wait_ge(sig("pdiag_ready"), 4 * b + 4)
                    for n in range(3):
                        if n == 2:
                            pe.wait_ge(sig("og_ready"), 3 * b + 1)
                        for j in range(16 * n, 16 * n + 16):
                            c0 = RANKS * (j - 16 * n)
                            last = mm(ps[0:DC, 3 - n % 2, c0:c0 + GP * H], gathT[:, b, j, :],
                                      pdiag[:, j, :, :].rearrange("p t h -> p (t h)"), start=True, stop=True)
                        last.then_inc(sig("og_mm"), 1)
                    pe.wait_ge(sig("o_copied"), 2 * b + 2)
                    pe.wait_ge(sig("og_ready"), 3 * b + 3)
                    if b > 0:
                        pe.wait_ge(sig("x_updated"), b)
                    for i in range(2):
                        last = mm(ps[:, 6, 0:L], w_vo4[:, i, :], oTa[:, i, bcols(b)], start=(i == 0), stop=(i == 1))
                    last.then_inc(sig("a_out"), 1)
                    for h in range(H):
                        last = mm(ps[:, 6, L:L + GT], w_vo[:, h, :], og[:, :, h], start=(h == 0), stop=(h == H - 1))
                    last.then_inc(sig("a_out"), 1)

                def scores0(a, T):
                    tile_scores(a, T, lambda h, c: qaT[:, h // 2, c], lambda h, c: kaT[:, h % 2, c])

                scores0(0, 0)
                for a in range(2 * NB + 2):
                    T = a % 2
                    if a >= 2:
                        b = (a - 2) // 2
                        lat = {(0, 0): kvsrc[:, 2 * b, 0:DC], (1, 0): ckv_b[:, b, :], (1, 1): ckv_c[:, b, :]}
                        tile_pv(a - 2, T, DC, lambda h, c: lat[T, c])
                    if a + 1 < 2 * NB:
                        scores0(a + 1, 1 - T)
                    if 0 < a <= 2 * NB:
                        if a > 1:
                            pe.wait_ge(sig("pt_act"), pt_act(a - 1))
                            pe.wait_ge(sig("pt_dve"), pt_act(a - 1))
                        tile_pt(a - 1, 1 - T, keys(1 - T) + RANKS)
                    if a >= 3 and T == 1:
                        gathered((a - 3) // 2)

                pe.wait_ge(sig("late_loaded"), 16 * len(late_loads))
                layernorm(1, xT[:, :], "x_updated", 0)
                for l in range(2):

                    def values(b, c):
                        n = 6 * l + 3 * b + c
                        if n > 0:
                            pe.wait_ge(sig("v_copied"), n)
                        pe.wait_ge(sig("shifted"), 8 * l + 2 * b + 2)
                        first, m = ((0, P), (LW, P), (L - LW, LW))[c]
                        mm(ps[0:m, 4 + c % 2, :], sh[:, b, first:first + m], wqkv[:, l, 1024:], start=True, stop=True)\
                          .then_inc(sig("v_mm"), 1)

                    def queries_keys(k):
                        m = NT * l + k
                        if k >= 2:
                            pe.wait_ge(sig("qk_parts"), 3 * (m - 1))
                            pe.wait_ge(sig("qk_squared"), m - 1)
                        pe.wait_ge(sig("shifted"), 8 * l + 2 * (k // 2) + 2)
                        x = sh[:, k // 2, P * (k % 2):P * (k % 2) + P]
                        bank = 2 * (k % 2)
                        mm(ps[:, bank, :], x, wqkv[:, l, 0:512], start=True, stop=True)
                        mm(ps[:, bank + 1, :], x, wqkv[:, l, 512:1024], start=True, stop=True).then_inc(sig("qk_mm"), 1)

                    queries_keys(0)
                    queries_keys(1)
                    for k in range(NT):
                        m = NT * l + k
                        if k + 2 < NT:
                            queries_keys(k + 2)
                        for j in range(2 * k, 2 * k + 2):
                            if j < 6:
                                values(j // 3, j % 3)
                        if m > 0:
                            pe.wait_ge(sig("q_copied"), 2 * m)
                            pe.wait_ge(sig("k_copied"), m)
                        pe.wait_ge(sig("qk_ready"), m + 1)
                        for i in range(4):
                            pe.transpose(ps[:, 6, P * i:P * i + P], qk_own[k][:, P * i:P * i + P], ident[:, :])
                        for i in range(4):
                            last = pe.transpose(ps[:, 7, P * i:P * i + P], qk_own[k][:, 512 + P * i:512 + P * i + P],
                                                ident[:, :])
                        last.then_inc(sig("qk_turned"), 1)
                    pe.wait_ge(sig("q_copied"), 2 * NT * (l + 1))
                    pe.wait_ge(sig("k_copied"), NT * (l + 1))
                    pe.wait_ge(sig("v_copied"), 6 * (l + 1))

                    def values0(a, T):
                        b = (a % 4) // 2
                        tile_pv(a, T, DH, lambda h, c: vt[0:(P if c == 0 else LW), b, T + c, DH * h:DH * h + DH])

                    def scores2(a, T):
                        tile_scores(a, T, lambda h, c: q_half[:, h // 2, h % 2, c], lambda h, c: kT[:, h // 2, c])

                    def project2(b):
                        pe.wait_ge(sig("o_copied"), 4 + 4 * l + 2 * b + 2)
                        pe.wait_ge(sig("att_evac"), 4 * (4 + 4 * l + NT))
                        for i in range(4):
                            last = mm(ps[:, b, 0:L], wo[:, l, i, :], oT[:, i, bcols(b)], start=(i == 0), stop=(i == 3))
                        last.then_inc(sig("f_o"), 1)

                    scores2(4 + 4 * l, 0)
                    for k in range(NT + 2):
                        a, T = 4 + 4 * l + k, k % 2
                        if k >= 2:
                            values0(a - 2, T)
                        if k + 1 < NT:
                            scores2(a + 1, 1 - T)
                        if k == NT:
                            project2(0)
                        if 0 < k <= NT:
                            pe.wait_ge(sig("pt_act"), pt_act(a - 1))
                            pe.wait_ge(sig("pt_dve"), pt_act(a - 1))
                            tile_pt(a - 1, 1 - T, keys(1 - T))
                    project2(1)
                    layernorm(2 + l, sh[:, :, :].rearrange("p b t -> p (b t)"), "shifted", 8 * l + 4, 2)
                    for c in range(3):
                        m, c0 = HC[c], P * c
                        mm(ps[0:m, 3 + c, :], w1[:, l, HID + c0:HID + c0 + m], hT[:, :], start=True, stop=True)\
                          .then_inc(sig("f_g"), 1)
                        mm(ps[0:m, c, :], w1[:, l, c0:c0 + m], hT[:, :], start=True, stop=True).then_inc(sig("f_a"), 1)
                    for b in range(NB):
                        for c in range(3):
                            m = HC[c]
                            pe.wait_ge(sig("f_hidden"), 3 * l + c + 1)
                            last = mm(ps[:, 6 + b, 0:L], w2[0:m, l, c, :], hh[0:m, c, bcols(b)], start=(c == 0), stop=(c == 2))
                        last.then_inc(sig("f_down"), 1)

                layernorm(4, xT[:, :], "x_updated", 2)
                mm(ps[:, 0, :], w1q[:, :], hT[:, :], start=True, stop=True).then_inc(sig("qk1_mm"), 1)
                mm(ps[:, 1, :], w1k[:, :], hT[:, :], start=True, stop=True).then_inc(sig("qk1_mm"), 1)
                for k in range(NT):
                    last = mm(ps[:, 2, cols(k)], hT[:, cols(k)], w1v[:, :], start=True, stop=True)
                last.then_inc(sig("v1_mm"), 1)

                def scores1(u):
                    k = u // 4
                    pe.wait_ge(sig("q_own"), u + 1)
                    if u >= 2:
                        pe.wait_ge(sig("l1_exp"), u - 1)
                    for e in range(4):
                        last = mm(ps[:, 2 * (u % 2) + e // 2, L * (e % 2):L * (e % 2) + L], q_own[:, u % 4, e, :],
                                  k1T[:, bcols(k // 2)], start=True, stop=True)
                    last.then_inc(sig("l1_mm"), 1)

                def turn1(u):
                    pe.wait_ge(sig("l1_exp"), u + 1)
                    for z in (2 * u, 2 * u + 1):
                        if z >= 3:
                            pe.wait_ge(sig("l1_pt_act" if (z - 3) % 2 == 0 else "l1_pt_dve"), (z - 3) // 2 + 1)
                        for i in range(4):
                            e, c = 2 * (z % 2) + i // 2, i % 2
                            last = pe.transpose(ps[:, 4 + z % 3, P * i:P * i + P], probs1(u)[:, e, P * c:P * c + P], ident[:, :])
                        last.then_inc(sig("l1_turned"), 1)

                def values1(u):
                    k, g = u // 4, u % 4
                    pe.wait_ge(sig("l1_pt_act"), u + 1)
                    pe.wait_ge(sig("l1_pt_dve"), u + 1)
                    for c in range(2):
                        for e in range(4):
                            z, i = 2 * u + e // 2, 2 * (e % 2) + c
                            last = mm(ps[32 * e:32 * e + 32, 7, cols(k)], v_own[:, 2 * (k // 2) + c, e, g, :],
                                      PT[:, z % 4, P * i:P * i + P], start=(g == 0 and c == 0), stop=(g == 3 and c == 1))
                    last.then_inc(sig("l1_pv"), 1)

                pe.wait_ge(sig("k1_copied"), 1)
                pe.wait_ge(sig("v1_copied"), 4 * NT)
                for u in range(4 * NT + 2):
                    if u < 4 * NT:
                        scores1(u)
                    if 0 < u <= 4 * NT:
                        turn1(u - 1)
                    if u > 1:
                        values1(u - 2)
                pe.wait_ge(sig("l1_recip"), 1)
                for k in range(NT):
                    last = pe.transpose(ps[0:H1, 0, cols(k)], rl1[:, H1 * k:H1 * k + H1], ident[:, :])
                last.then_inc(sig("l1_recip_turned"), 1)
                pe.wait_ge(sig("l1_recip_copied"), 1)
                mm(ps[:, 1, :], head_rows[:, :], combT[:, :], start=True, stop=True).then_inc(sig("l1_recip_mm"), 1)
                pe.wait_ge(sig("att1_ready"), 1)
                mm(ps[:, 1, :], w1o[:, :], hT[:, :], start=True, stop=True).then_inc(sig("l1_out"), 1)

                layernorm(5, xT[:, :], "x_updated", 4)
                for k in range(NT):
                    last = mm(ps[:, 7, E1 * k:E1 * k + E1], hT[:, cols(k)], gate_w[:, :], start=True, stop=True)
                last.then_inc(sig("route_mm"), 1)

                def expert_in(e):
                    s = e % 2
                    if e >= 2:
                        pe.wait_ge(sig("e_silu"), e - 1)
                    mm(ps[:, s, :], experts[:, 0, e, :], hT[:, :], start=True, stop=True).then_inc(sig("e_gate"), 1)
                    if e >= 2:
                        pe.wait_ge(sig("e_hidden"), e - 1)
                    mm(ps[:, 2 + s, :], experts[:, 1, e, :], hT[:, :], start=True, stop=True).then_inc(sig("e_up"), 1)

                def expert_weight(e):
                    mm(ps[:, 4 + e % 2, :], bc(pick_bf[:, e - 1], 1, P), combS, start=True, stop=True)\
                      .then_inc(sig("e_comb"), 1)

                def expert_out(e):
                    pe.wait_ge(sig("e_hidden"), e + 1)
                    mm(ps[:, 6, :], experts[:, 2, e, :], moe_h[:, e % 2, :], start=(e == 0), stop=(e == E1))\
                      .then_inc(sig("e_down"), 1)

                pe.wait_ge(sig("experts_loaded"), 48)
                expert_in(0)
                expert_in(1)
                pe.wait_ge(sig("comb_ready"), 1)
                for k in range(NT):
                    last = pe.transpose(ps[0:3 * E1, 7, cols(k)], comb3[:, k, :, :].rearrange("p s e -> p (s e)"), ident[:, :])
                last.then_inc(sig("comb_turned"), 1)
                expert_out(0)
                expert_in(2)
                pe.wait_ge(sig("comb_copied"), 1)
                expert_weight(1)
                expert_weight(2)
                for e in range(1, E1 + 1):
                    expert_out(e)
                    if e + 2 <= E1:
                        expert_in(e + 2)
                        expert_weight(e + 2)
                pe.wait_ge(sig("x_updated"), 8)
                for k in range(NT):
                    last = pe.transpose(ps[:, 7, cols(k)], xT[:, cols(k)], ident[:, :])
                last.then_inc(sig("y_turned"), 1)
                pass_end(pe, "pe")

        @block.gpsimd
        def _(pool):
            pool.wait_ge(sig("setup_done"), 1)
            with pool.Fori(0, PASSES) as it:
                st = Steps(pool, sig("pool_step"))
                pool.memset(pdiag[:, :, :, :], 0.0).then_inc(sig("pdiag_zero"), 1)
                hi, mid, lo = kv_part
                pool.wait_ge(sig("kv_split"), 1)
                pool.tensor_tensor(kv_rem[:, 0, :, :], kvsrc[:, :, :], hi[:, :, :], ALU.subtract).then_inc(sig("kv_split"), 1)
                v8 = lambda ap: ap.rearrange("p (h n) -> p h n", h=H)
                for k in range(NT):
                    T = k % 2
                    q_abs, q_mu, q_c, q_s = q_tmp[k % 2]
                    pool.wait_ge(sig("q2_log"), 2 * k + 2)
                    st.link(pool.tensor_tensor(q_mu, q_mu, q_abs, ALU.add))
                    if k >= 2:
                        pool.wait_ge(sig("q_turned"), k - 1)
                    qa_, qb_ = qa[k % 2], qb[k % 2]
                    for s, dsts in ((0, (qa_[:, :, DC:],)), (1, (qb_[:, :, DC:2 * DC], qb_[:, :, 2 * DC:]))):
                        C, Sn = ropeC[:, 2 * s + T, :], ropeS[:, 2 * s + T, :]
                        st.mark(pool.tensor_tensor(v8(q_c), v8(q_mu), bc(C, 1, H), ALU.mult))
                        st.mark(pool.tensor_tensor(v8(q_s)[:, :, 0:16], v8(q_mu)[:, :, 16:32], bc(Sn[:, 0:16], 1, H), ALU.mult))
                        st.link(pool.tensor_tensor(v8(q_s)[:, :, 16:32], v8(q_mu)[:, :, 0:16], bc(Sn[:, 16:32], 1, H), ALU.mult))
                        for dst in dsts:
                            pool.tensor_tensor(dst, v8(q_c), v8(q_s), ALU.add).then_inc(sig("q_ready"), 1)
                        pool.wait_ge(sig("q_ready"), 3 * k + (1, 3)[s])
                    if k == 0:
                        pool.wait_ge(sig("kv_split"), 3)
                        pool.tensor_tensor(kv_rem[:, 1, :, :], kv_rem[:, 0, :, :], mid[:, :, :], ALU.subtract)\
                            .then_inc(sig("kv_split"), 1)
                pool.wait_ge(sig("a_out"), 2 * NB)
                pool.memset(q_half[DH:P, :, 0, :], 0.0).then_inc(sig("q_zero"), 1)
                pool.memset(q_half[0:DH, :, 1, :], 0.0).then_inc(sig("q_zero"), 1)
                pool.wait_ge(sig("q_zero"), 2)
                for m in range(2 * NT):
                    if m > 0:
                        pool.wait_ge(sig("qk_added"), m)
                    pool.wait_ge(sig("qk_parts"), 3 * (m + 1))
                    own = qk_own[m % NT]
                    pool.tensor_tensor(own, own, qk_part[m % 2], ALU.add).then_inc(sig("qk_added"), 1)
                pool.wait_ge(sig("f_done"), 2 * NB)
                pool.wait_ge(sig("qk_added"), 2 * NT)
                pool.memset(v_own[:, :, :, :, :], 0.0).then_inc(sig("v_zero"), 1)
                pool.wait_ge(sig("q1_copied"), 1)
                for u in range(4 * NT):
                    k, g = u // 4, u % 4
                    if u >= 4:
                        pool.wait_ge(sig("l1_mm"), u - 3)
                    pool.tensor_tensor(q_own[:, u % 4, :, :], bc(q1T[:, cols(k)], 1, 4),
                                       bc(own_head[:, g::4], 2, P), ALU.mult).then_inc(sig("q_own"), 1)
                pool.drain().then_inc(done, 1)
                pool.wait_ge(done, 5)
                pool.sem_clear(done)
                numbers = sorted(sems[name].num for name in sems if name not in SETUP + ACROSS)
                first = 0
                for i, number in enumerate(numbers):
                    if i + 1 == len(numbers) or numbers[i + 1] != number + 1:
                        pool.sem_clear(range(numbers[first], number + 1))
                        first = i + 1
                for name in sorted(go):
                    pool.sem_inc(go[name], 1)


def lay_out(a):
    f = np.float32
    n = {k: np.asarray(v) for k, v in a.items()}
    o = dict(shape_constants())
    o["x"] = np.concatenate([n["L0_attn_x"], np.zeros((NB, L, D), f)], 0)
    o["cT"] = np.stack([n["L0_c"].T, n["L1_c"].T], 1)
    o["wmod"] = np.stack([n["L0_wmod"], n["L1_wmod"]], 1)
    o["w_kv"] = np.concatenate([n["L0_attn_W_dkv"], n["L0_attn_W_kr"]], 1)
    o["w_ki"] = np.concatenate([n["L0_attn_idx_wk"]] * 2, 1)
    o["w_qi"] = n["L0_attn_idx_wq"]
    o["w_dq"] = n["L0_attn_W_dq"]
    o["uqT"] = n["L0_attn_W_uq"].reshape(DQ, H, DH).transpose(2, 1, 0)
    o["ukT"] = n["L0_attn_W_uk"].reshape(DC, H, DH).transpose(2, 1, 0)
    o["uvT"] = n["L0_attn_W_uv"].reshape(DC, H, DH).transpose(2, 1, 0)
    o["w_out0"] = n["L0_attn_W_out"].reshape(H, DH, D).transpose(1, 0, 2)
    o["w_q2"] = np.concatenate([n["L0_attn_W_qr"], n["L0_attn_W_qr"]], 1)
    o["idx_w"] = n["L0_attn_idx_w"].reshape(1, IH)
    o["raw_delta"] = n["L0_attn_raw_delta"].reshape(1, DR // 2)
    o["delta_col"] = np.tile(n["L0_attn_raw_delta"], GF // (DR // 2)).reshape(GF, 1)
    qs, ks = n["L0_ffn_q_scale"], n["L0_ffn_k_scale"]
    roll = lambda s: np.roll(s, DH // 2, 1)
    o["qk_scale"] = np.concatenate([qs, ks, roll(qs), roll(ks)], 1).reshape(1, 2 * 4 * DH)
    o["wqkv"] = n["L0_ffn_wqkv"].transpose(1, 0, 2)
    o["wo"] = n["L0_ffn_wo"].reshape(2, 4, P, D).transpose(2, 0, 1, 3)
    o["ln_gb"] = np.stack([n["L0_ffn_ln_g"], n["L0_ffn_ln_b"]], 1).transpose(2, 0, 1)
    o["w1"] = n["L0_ffn_w1"].transpose(1, 0, 2)
    pad = np.zeros((2, 2, 3 * P), f)
    pad[:, :, :HID] = n["L0_ffn_b1"].reshape(2, 2, HID)
    o["b1"] = pad.reshape(2, 2, 3, P).transpose(3, 0, 1, 2)
    pad = np.zeros((2, 3 * P, D), f)
    pad[:, :HID] = n["L0_ffn_w2"]
    o["w2"] = pad.reshape(2, 3, P, D).transpose(2, 0, 1, 3)
    o["b2"] = n["L0_ffn_b2"].T
    w = n["L1_attn_W_qkv"].reshape(H1, 3, D1, D)
    bias = n["L1_attn_b_qkv"].reshape(H1, 3, D1)
    for i, name in ((0, "q"), (1, "k")):
        o["w1" + name] = w[:, i].reshape(D, D).T
        o["b1" + name] = bias[:, i].reshape(D, 1)
    o["w1v"] = w[:, 2].reshape(D, D).T
    o["b1v"] = bias[:, 2].reshape(D, 1)
    o["w1o"] = n["L1_attn_W_out"].T
    o["b1o"] = n["L1_attn_b_out"].reshape(D, 1)
    o["gate_w"] = n["L1_ffn_gate_w"].T
    o["e_bias"] = n["L1_ffn_expert_bias"].reshape(1, E1)
    both = [np.concatenate([n[f"L1_ffn_shared_{name}_w"][None], n["L1_ffn_w_" + name]], 0)
            for name in ("gate", "up", "down")]
    o["experts"] = np.stack(both, 0).transpose(3, 0, 1, 2)
    o["packed"] = np.concatenate([o.pop(name).reshape(P, -1) for name in PACKED], 1)
    return {k: np.ascontiguousarray(v) for k, v in o.items()}


def kernel(**inputs):
    import concourse.bacc as bacc
    from concourse.bass_utils import run_bass_kernel_spmd

    nc = bacc.Bacc("TRN2", target_bir_lowering=False, num_devices=1)
    arrays = lay_out(inputs)
    A = {k: nc.dram_tensor("in_" + k, v.shape, mybir.dt.from_np(v.dtype), kind="ExternalInput").ap()
         for k, v in arrays.items()}
    out = nc.dram_tensor("out_x", (B, L, D), F32, kind="ExternalOutput").ap()
    idx = nc.dram_tensor("idx_scratch", (NB, GT * RANKS), BF16, kind="Internal").ap()
    scores = nc.dram_tensor("score_scratch", (NB, 3, P * 512), F32, kind="Internal").ap()
    program(nc, A, out, idx, scores)
    r = run_bass_kernel_spmd(nc, [{"in_" + k: v for k, v in arrays.items()}], core_ids=[0])
    return r.results[0]["out_x"]
```
